# Optimizing a Trainium2 kernel written in Bass

```python
import numpy as np
import jax
import jax.numpy as jnp

def _softmax(x, axis=-1):
    return jax.nn.softmax(x, axis=axis)

def _gelu(x):
    return jax.nn.gelu(x, approximate=True)

def _silu(x):
    return jax.nn.silu(x)

def _sigmoid(x):
    return jax.nn.sigmoid(x)

def _layernorm(x, axis=-1, eps=1e-05):
    m = jnp.mean(x, axis=axis, keepdims=True)
    v = jnp.var(x, axis=axis, keepdims=True)
    return (x - m) / jnp.sqrt(v + eps)

def _scatter_add(tgt, idx, src, axis=0):
    return tgt.at[idx].add(src)

def _segment_sum(src, seg, n):
    return jax.ops.segment_sum(src, seg, n)
kernel_name = 'mk_metaformer_d1_conv_nhwc256_r4_6f48cd'

def setup_inputs(seed: int=0):
    np.random.seed(seed)
    _w = jnp.asarray

    def _rec_inputs():
        import jax
        import jax.numpy as jnp
        _gk = jax.random.key(seed)
        x = -0.0003929 + 0.9999 * jax.random.normal(jax.random.fold_in(_gk, 1), (2, 128, 16, 64), jnp.float32)
        return x
    x = _rec_inputs()

    def _L0_conv_setup():
        import jax, jax.numpy as jnp
        import numpy as np
        H = 64
        NL = 6
        N = 16
        DCONV = 4
        DIN = 128
        HEADS = 8
        P = 16
        CONVD = DIN + 2 * N
        PROJ = 2 * DIN + 2 * N + HEADS

        def rmsnorm(x, w, eps=1e-06):
            return x * jax.lax.rsqrt(jnp.mean(x * x, axis=-1, keepdims=True) + eps) * w

        def mamba2(x, Win, conv_w, conv_b, dt_bias, A_log, D, gnorm, Wout):
            b, l, _ = x.shape
            zxbcdt = x @ Win
            z = zxbcdt[..., :DIN]
            xBC = zxbcdt[..., DIN:DIN + CONVD]
            dt = zxbcdt[..., DIN + CONVD:]
            xp = jnp.pad(xBC, ((0, 0), (DCONV - 1, 0), (0, 0)))
            xc = conv_b + sum((xp[:, k:k + l, :] * conv_w[k] for k in range(DCONV)))
            xBC = jax.nn.silu(xc)
            xs = xBC[..., :DIN]
            B = xBC[..., DIN:DIN + N]
            C = xBC[..., DIN + N:]
            dt = jax.nn.softplus(dt + dt_bias)
            dA = jnp.exp(dt * -jnp.exp(A_log))
            xh = xs.reshape(b, l, HEADS, P)
            xdt = xh * dt[..., None]

            def step(h, inp):
                dA_t, xdt_t, B_t, C_t = inp
                h = dA_t[:, :, None, None] * h + xdt_t[..., None] * B_t[:, None, None, :]
                return (h, jnp.einsum('bhpn,bn->bhp', h, C_t))
            h0 = jnp.zeros((b, HEADS, P, N), x.dtype)
            _, ys = jax.lax.scan(step, h0, (jnp.swapaxes(dA, 0, 1), jnp.swapaxes(xdt, 0, 1), jnp.swapaxes(B, 0, 1), jnp.swapaxes(C, 0, 1)))
            y = jnp.swapaxes(ys, 0, 1) + D[None, None, :, None] * xh
            y = y.reshape(b, l, DIN) * jax.nn.silu(z)
            return rmsnorm(y, gnorm) @ Wout

        def dual_path(x, t_norm, t_Win, t_cw, t_cb, t_dtb, t_Alog, t_D, t_gn, t_Wout, b_norm, b_Win, b_cw, b_cb, b_dtb, b_Alog, b_D, b_gn, b_Wout):
            batch, time, bands, hdim = x.shape
            for i in range(NL):
                xt = x.reshape(batch * bands, time, hdim)
                xt = xt + mamba2(rmsnorm(xt, t_norm[i]), t_Win[i], t_cw[i], t_cb[i], t_dtb[i], t_Alog[i], t_D[i], t_gn[i], t_Wout[i])
                x = jnp.swapaxes(xt.reshape(batch, bands, time, hdim), 1, 2)
                xb = x.reshape(batch * time, bands, hdim)
                xb = xb + mamba2(rmsnorm(xb, b_norm[i]), b_Win[i], b_cw[i], b_cb[i], b_dtb[i], b_Alog[i], b_D[i], b_gn[i], b_Wout[i])
                x = xb.reshape(batch, time, bands, hdim)
            return x
        key = jax.random.key(seed)
        ks = jax.random.split(key, 3)
        x = jax.random.normal(ks[0], (2, 128, 16, H), jnp.float32)

        def make_params(k):
            kk = jax.random.split(k, 5)
            g = lambda kx, sh, s: jax.random.normal(kx, sh, jnp.float32) * s
            return dict(norm=jnp.ones((NL, H), jnp.float32), Win=g(kk[0], (NL, H, PROJ), H ** (-0.5)), cw=g(kk[1], (NL, DCONV, CONVD), 0.2), cb=jnp.zeros((NL, CONVD), jnp.float32), dtb=g(kk[2], (NL, HEADS), 0.5), Alog=jnp.log(jnp.abs(g(kk[3], (NL, HEADS), 1.0)) + 0.5), D=jnp.ones((NL, HEADS), jnp.float32), gn=jnp.ones((NL, DIN), jnp.float32), Wout=g(kk[4], (NL, DIN, H), DIN ** (-0.5)))
        tp = make_params(ks[1])
        bp = make_params(ks[2])
        out = {'x': x}
        for name, d in (('t', tp), ('b', bp)):
            for kname, v in d.items():
                out[f'{name}_{kname}'] = v
        return out
    _L0_conv_all = _L0_conv_setup()
    _L0_conv_in = {k: v for k, v in _L0_conv_all.items() if k in ('t_norm', 't_Win', 't_cw', 't_cb', 't_dtb', 't_Alog', 't_D', 't_gn', 't_Wout', 'b_norm', 'b_Win', 'b_cw', 'b_cb', 'b_dtb', 'b_Alog', 'b_D', 'b_gn', 'b_Wout')}
    del _L0_conv_all

    def _L0_ffn_setup():
        import jax, jax.numpy as jnp
        import numpy as np
        D_MODEL = 64
        N_EXPERTS = 16
        HIDDEN = 128
        SCALE = 0.02
        key = jax.random.key(seed)
        ks = jax.random.split(key, 5)
        x = jax.random.normal(ks[0], (4, 2048, D_MODEL), dtype=jnp.float32)
        gate_w = jax.random.normal(ks[1], (D_MODEL, N_EXPERTS), dtype=jnp.float32) * SCALE
        gate_b = jnp.zeros((N_EXPERTS,), dtype=jnp.float32)
        w1 = jax.random.normal(ks[2], (N_EXPERTS, D_MODEL, HIDDEN), dtype=jnp.float32) * SCALE
        w2 = jax.random.normal(ks[3], (N_EXPERTS, D_MODEL, HIDDEN), dtype=jnp.float32) * SCALE
        w3 = jax.random.normal(ks[4], (N_EXPERTS, HIDDEN, D_MODEL), dtype=jnp.float32) * SCALE
        return {'x': x, 'gate_w': gate_w, 'gate_b': gate_b, 'w1': w1, 'w2': w2, 'w3': w3}
    _L0_ffn_all = _L0_ffn_setup()
    _L0_ffn_in = {k: v for k, v in _L0_ffn_all.items() if k in ('gate_w', 'gate_b', 'w1', 'w2', 'w3')}
    del _L0_ffn_all
    return {'x': x, 'L0_conv_t_norm': _L0_conv_in['t_norm'], 'L0_conv_t_Win': _L0_conv_in['t_Win'], 'L0_conv_t_cw': _L0_conv_in['t_cw'], 'L0_conv_t_cb': _L0_conv_in['t_cb'], 'L0_conv_t_dtb': _L0_conv_in['t_dtb'], 'L0_conv_t_Alog': _L0_conv_in['t_Alog'], 'L0_conv_t_D': _L0_conv_in['t_D'], 'L0_conv_t_gn': _L0_conv_in['t_gn'], 'L0_conv_t_Wout': _L0_conv_in['t_Wout'], 'L0_conv_b_norm': _L0_conv_in['b_norm'], 'L0_conv_b_Win': _L0_conv_in['b_Win'], 'L0_conv_b_cw': _L0_conv_in['b_cw'], 'L0_conv_b_cb': _L0_conv_in['b_cb'], 'L0_conv_b_dtb': _L0_conv_in['b_dtb'], 'L0_conv_b_Alog': _L0_conv_in['b_Alog'], 'L0_conv_b_D': _L0_conv_in['b_D'], 'L0_conv_b_gn': _L0_conv_in['b_gn'], 'L0_conv_b_Wout': _L0_conv_in['b_Wout'], 'L0_ffn_gate_w': _L0_ffn_in['gate_w'], 'L0_ffn_gate_b': _L0_ffn_in['gate_b'], 'L0_ffn_w1': _L0_ffn_in['w1'], 'L0_ffn_w2': _L0_ffn_in['w2'], 'L0_ffn_w3': _L0_ffn_in['w3']}

def reference(x, L0_conv_t_norm, L0_conv_t_Win, L0_conv_t_cw, L0_conv_t_cb, L0_conv_t_dtb, L0_conv_t_Alog, L0_conv_t_D, L0_conv_t_gn, L0_conv_t_Wout, L0_conv_b_norm, L0_conv_b_Win, L0_conv_b_cw, L0_conv_b_cb, L0_conv_b_dtb, L0_conv_b_Alog, L0_conv_b_D, L0_conv_b_gn, L0_conv_b_Wout, L0_ffn_gate_w, L0_ffn_gate_b, L0_ffn_w1, L0_ffn_w2, L0_ffn_w3):
    import jax
    import jax.numpy as jnp

    def _L0_conv_ref(x, t_norm, t_Win, t_cw, t_cb, t_dtb, t_Alog, t_D, t_gn, t_Wout, b_norm, b_Win, b_cw, b_cb, b_dtb, b_Alog, b_D, b_gn, b_Wout):
        import jax, jax.numpy as jnp
        import numpy as np
        H = 64
        NL = 6
        N = 16
        DCONV = 4
        DIN = 128
        HEADS = 8
        P = 16
        CONVD = DIN + 2 * N
        PROJ = 2 * DIN + 2 * N + HEADS

        def rmsnorm(x, w, eps=1e-06):
            return x * jax.lax.rsqrt(jnp.mean(x * x, axis=-1, keepdims=True) + eps) * w

        def mamba2(x, Win, conv_w, conv_b, dt_bias, A_log, D, gnorm, Wout):
            b, l, _ = x.shape
            zxbcdt = x @ Win
            z = zxbcdt[..., :DIN]
            xBC = zxbcdt[..., DIN:DIN + CONVD]
            dt = zxbcdt[..., DIN + CONVD:]
            xp = jnp.pad(xBC, ((0, 0), (DCONV - 1, 0), (0, 0)))
            xc = conv_b + sum((xp[:, k:k + l, :] * conv_w[k] for k in range(DCONV)))
            xBC = jax.nn.silu(xc)
            xs = xBC[..., :DIN]
            B = xBC[..., DIN:DIN + N]
            C = xBC[..., DIN + N:]
            dt = jax.nn.softplus(dt + dt_bias)
            dA = jnp.exp(dt * -jnp.exp(A_log))
            xh = xs.reshape(b, l, HEADS, P)
            xdt = xh * dt[..., None]

            def step(h, inp):
                dA_t, xdt_t, B_t, C_t = inp
                h = dA_t[:, :, None, None] * h + xdt_t[..., None] * B_t[:, None, None, :]
                return (h, jnp.einsum('bhpn,bn->bhp', h, C_t))
            h0 = jnp.zeros((b, HEADS, P, N), x.dtype)
            _, ys = jax.lax.scan(step, h0, (jnp.swapaxes(dA, 0, 1), jnp.swapaxes(xdt, 0, 1), jnp.swapaxes(B, 0, 1), jnp.swapaxes(C, 0, 1)))
            y = jnp.swapaxes(ys, 0, 1) + D[None, None, :, None] * xh
            y = y.reshape(b, l, DIN) * jax.nn.silu(z)
            return rmsnorm(y, gnorm) @ Wout

        def dual_path(x, t_norm, t_Win, t_cw, t_cb, t_dtb, t_Alog, t_D, t_gn, t_Wout, b_norm, b_Win, b_cw, b_cb, b_dtb, b_Alog, b_D, b_gn, b_Wout):
            batch, time, bands, hdim = x.shape
            for i in range(NL):
                xt = x.reshape(batch * bands, time, hdim)
                xt = xt + mamba2(rmsnorm(xt, t_norm[i]), t_Win[i], t_cw[i], t_cb[i], t_dtb[i], t_Alog[i], t_D[i], t_gn[i], t_Wout[i])
                x = jnp.swapaxes(xt.reshape(batch, bands, time, hdim), 1, 2)
                xb = x.reshape(batch * time, bands, hdim)
                xb = xb + mamba2(rmsnorm(xb, b_norm[i]), b_Win[i], b_cw[i], b_cb[i], b_dtb[i], b_Alog[i], b_D[i], b_gn[i], b_Wout[i])
                x = xb.reshape(batch, time, bands, hdim)
            return x
        return dual_path(x, t_norm, t_Win, t_cw, t_cb, t_dtb, t_Alog, t_D, t_gn, t_Wout, b_norm, b_Win, b_cw, b_cb, b_dtb, b_Alog, b_D, b_gn, b_Wout)

    def _L0_ffn_ref(x, gate_w, gate_b, w1, w2, w3):
        import jax, jax.numpy as jnp
        import numpy as np
        D_MODEL = 64
        N_EXPERTS = 16
        HIDDEN = 128
        SCALE = 0.02
        n_experts = w1.shape[0]
        logits = jnp.einsum('bsd,de->bse', x, gate_w) + gate_b
        probs = jax.nn.softmax(logits, axis=-1)
        top_probs, top_idx = jax.lax.top_k(probs, 2)
        top_probs = top_probs / jnp.sum(top_probs, axis=-1, keepdims=True)
        dispatch = jnp.sum(jax.nn.one_hot(top_idx, n_experts, dtype=x.dtype) * top_probs[..., None], axis=-2)
        h1 = jnp.einsum('bsd,edh->bseh', x, w1)
        h2 = jnp.einsum('bsd,edh->bseh', x, w2)
        hidden = jax.nn.silu(h1) * h2
        expert_out = jnp.einsum('bseh,eho->bseo', hidden, w3)
        return jnp.einsum('bseo,bse->bso', expert_out, dispatch)

    def _gn(v, G=32, eps=1e-05):
        B_, H_, W_, C_ = v.shape
        g = v.reshape(B_, H_, W_, G, C_ // G)
        m = jnp.mean(g, axis=(1, 2, 4), keepdims=True)
        s = jnp.var(g, axis=(1, 2, 4), keepdims=True)
        return ((g - m) / jnp.sqrt(s + eps)).reshape(v.shape)

    def _ln_c(v, eps=1e-06):
        m = jnp.mean(v, axis=-1, keepdims=True)
        s = jnp.var(v, axis=-1, keepdims=True)
        return (v - m) / jnp.sqrt(s + eps)

    def _ln_t(v, eps=1e-05):
        m = jnp.mean(v, axis=-1, keepdims=True)
        s = jnp.var(v, axis=-1, keepdims=True)
        return (v - m) / jnp.sqrt(s + eps)

    def _to_tokens(v):
        B_, H_, W_, C_ = v.shape
        return v.reshape(B_, H_ * W_, C_)

    def _from_tokens(t, like):
        return t.reshape(like.shape)
    x = x + _L0_conv_ref(_ln_c(x), L0_conv_t_norm, L0_conv_t_Win, L0_conv_t_cw, L0_conv_t_cb, L0_conv_t_dtb, L0_conv_t_Alog, L0_conv_t_D, L0_conv_t_gn, L0_conv_t_Wout, L0_conv_b_norm, L0_conv_b_Win, L0_conv_b_cw, L0_conv_b_cb, L0_conv_b_dtb, L0_conv_b_Alog, L0_conv_b_D, L0_conv_b_gn, L0_conv_b_Wout)
    t = _to_tokens(x)
    t = t + _L0_ffn_ref(_ln_t(t), L0_ffn_gate_w, L0_ffn_gate_b, L0_ffn_w1, L0_ffn_w2, L0_ffn_w3)
    x = _from_tokens(t, x)
    return x

_drawn_inputs = setup_inputs


def setup_inputs(seed=0):
    import zlib

    import numpy as np

    out = dict(_drawn_inputs(seed))
    spreads = {'L0_conv_t_norm': (1.0, 0.2),
     'L0_conv_t_cb': (0.0, 0.1),
     'L0_conv_t_D': (1.0, 0.2),
     'L0_conv_t_gn': (1.0, 0.2),
     'L0_conv_b_norm': (1.0, 0.2),
     'L0_conv_b_cb': (0.0, 0.1),
     'L0_conv_b_D': (1.0, 0.2),
     'L0_conv_b_gn': (1.0, 0.2),
     'L0_ffn_gate_b': (0.0, 0.8)}
    factors = {'L0_ffn_gate_w': 8.0, 'L0_ffn_w1': 8.0, 'L0_ffn_w2': 8.0, 'L0_ffn_w3': 8.0}
    for name, (base, spread) in spreads.items():
        noise = np.random.default_rng([zlib.crc32(name.encode()), seed]).standard_normal(out[name].shape)
        drawn = base * np.exp(spread * noise) if base else spread * noise
        out[name] = jnp.asarray(drawn.astype(out[name].dtype))
    for name, factor in factors.items():
        out[name] = (out[name] * factor).astype(out[name].dtype)
    return out
```

```python
from contextlib import ExitStack

import concourse.bass as bass
from concourse import mybir

ALU = mybir.AluOpType
ACT = mybir.ActivationFunctionType
AX = mybir.AxisListType
F32 = mybir.dt.float32
BF16 = mybir.dt.bfloat16

P = 128
NBATCH = 2
C = 64
TOK = 2048
NPAIR = TOK // P
NL = 6
DIN = 128
NST = 16
HEADS = 8
HD = DIN // HEADS
DCONV = 4
CONVD = DIN + 2 * NST
PROJ = 2 * DIN + 2 * NST + HEADS
SEQ = (128, 16)
QS = (P // SEQ[0], P // SEQ[1])
BANDS = 16
E = 16
HID = 128
BH = NBATCH * HEADS
PART = 32
NPART = 3
FAR = -30000.0
CK = 512
NCK = TOK // CK

W_C0 = 0
W_C1 = W_C0 + CONVD
W_DT = W_C1 + CONVD + DIN
W_OUT = W_DT + BH
W_D = W_OUT + C
W_DTB = W_D + DIN
W_NA = W_DTB + HEADS
W_ALL = W_NA + HEADS


def build(nc, a, out, n_layers=NL):
    with ExitStack() as ctx:
        def sb(name, shape, dt=F32):
            return ctx.enter_context(nc.sbuf_tensor(name, shape, dt))

        def sem(name):
            return ctx.enter_context(nc.semaphore(name))

        bank = [ctx.enter_context(nc.psum_tensor(f"bank{i}", [P, CK], F32)) for i in range(8)]

        ident = sb("ident", [P, P])
        identb = sb("identb", [P, P], BF16)
        tri = [sb("tri_time", [P, P]), sb("tri_bands", [P, P])]
        mean64 = sb("mean64", [P, P])
        ones3 = sb("ones3", [P, P], BF16)
        head_row = sb("head_row", [P, BH, P], BF16)
        head_neg = sb("head_neg", [P, BH, P], BF16)
        eps6 = sb("eps6", [P, 1])
        eps5 = sb("eps5", [P, 1])
        eps2 = sb("eps2", [P, NBATCH])
        mhalf = sb("mhalf", [P, NBATCH])

        wall = sb("wall", [P, NL, 2, W_ALL])
        ball = sb("ball", [P, 2, NL, CONVD], BF16)
        wcur = [sb(f"wcur{s}", [P, W_ALL]) for s in range(2)]
        bcur = [sb(f"bcur{s}", [P, CONVD], BF16) for s in range(2)]

        x_io = [sb("x_time_in", [P, TOK]), sb("x_bands_in", [P, TOK])]
        wide = [(SEQ[s] + DCONV - 1) * QS[s] for s in range(2)]
        h_pad = [sb(f"h_pad{s}", [P, NPAIR, wide[s]]) for s in range(2)]
        slot = [[[sb(f"slot{s}{u}{b}", [P, wide[s]]) for b in range(2)] for u in range(2)] for s in range(2)]
        sq = sb("sq", [P, TOK])
        rstd = sb("rstd", [P, TOK])
        dtv = sb("dtv", [P, NPAIR * BH])
        dta = sb("dta", [P, NPAIR * BH])
        dtl = sb("dtl", [P, NPAIR * BH])
        dt_half = sb("dt_half", [P, NPAIR * BH])
        dta_log = sb("dta_log", [P, NPAIR * BH])
        rest = sb("rest", [P, NPAIR * BH])
        parts = sb("parts", [P, NPAIR, NPART, PART], BF16)
        cum_t = sb("cum_t", [P, NPAIR, P], BF16)

        th = sb("th", [P, NBATCH, CONVD + DIN])
        xbc = [sb(f"xbc{u}", [P, NBATCH, CONVD]) for u in range(2)]
        z_all = sb("z_all", [P, NPAIR, NBATCH, DIN])
        bct = [sb(f"bct{u}", [NST, NBATCH, 2, P]) for u in range(2)]
        gm = [sb(f"gm{u}", [P, NBATCH, P]) for u in range(2)]
        em = [sb(f"em{u}", [P, NBATCH, HEADS, P]) for u in range(2)]
        xdt = [sb(f"xdt{u}", [P, NBATCH, DIN]) for u in range(2)]
        xd = [sb(f"xd{u}", [P, NBATCH, DIN]) for u in range(2)]
        yd = sb("yd", [P, NBATCH, DIN])
        yg = [sb(f"yg{u}", [P, NBATCH, DIN]) for u in range(2)]
        ysq = sb("ysq", [P, DIN])
        ss = [sb(f"ss{u}", [P, NBATCH]) for u in range(2)]
        var = sb("var", [P, NBATCH])
        rr = sb("rr", [P, NBATCH])
        yr = [sb(f"yr{u}", [P, NBATCH, DIN]) for u in range(2)]
        yt = sb("yt", [P, NBATCH, P])

        x_in = sb("x_in", [P, NPAIR, NBATCH, C])
        stat = sb("stat", [P, NPAIR * NBATCH])
        stat2 = sb("stat2", [P, NPAIR * NBATCH])

        s_ld = sem("x_loaded")
        s_wld = sem("weights_loaded")
        s_const = sem("constants_made")
        s_wd = sem("weights_made")
        s_bld = sem("bias_rows_placed")
        s_ln = sem("norm_step")
        s_tp = sem("norm_transposed")
        s_x0 = sem("x0_ready")

        win_raw = z_all[:].rearrange("p a b c -> p (a b c)")[:, 0:2 * NL * PROJ].rearrange(
            "p (s l n) -> p s l n", s=2, l=NL)
        cw_raw = em[0][:].rearrange("p a b c -> p (a b c)")[:, 0:2 * NL * CONVD].rearrange(
            "p (s l n) -> p s l n", s=2, l=NL)
        cw_raw2 = em[1][:].rearrange("p a b c -> p (a b c)")[:, 0:2 * NL * CONVD].rearrange(
            "p (s l n) -> p s l n", s=2, l=NL)
        wout_raw = rstd[:, 0:2 * NL * C].rearrange("p (s l n) -> p s l n", s=2, l=NL)
        small = sb("small", [P, 2, NL, 2])
        hd_raw = sb("hd_raw", [P, 2, NL, 2, HEADS])
        cb_raw = sb("cb_raw", [2 * NL * CONVD // 16, 16])
        cb_rest = sb("cb_rest", [2 * NL * CONVD // 16, 16])
        cb_part = sb("cb_part", [2 * NL * CONVD // 16, NPART, 16], BF16)
        CBROWS = NL * CONVD // 16

        names = ("t", "b")
        N_WDMA = 28
        WD_CB = 4
        WD_ALL = 34
        N_CONST = 49
        LN_STEPS = 8
        MIX_STEPS = 24
        s_ea = sem("exp_a_log")

        s_sq, s_ms, s_lnv, s_rstd, s_h = (sem(n) for n in (
            "squares", "mean_squares", "log_var", "rstd_ready", "h_ready"))
        s_dtp, s_v, s_abs, s_e, s_l, s_dt, s_dta, s_cum = (sem(n) for n in (
            "dt_projected", "dt_biased", "dt_abs", "dt_exp", "dt_log1p", "dt_ready", "dta_ready", "cum_ready"))
        s_hi, s_rest, s_mid, s_lo, s_pt, s_ct = (sem(n) for n in (
            "cum_hi", "cum_rest", "cum_mid", "cum_lo", "parts_transposed", "cum_t_ready"))
        s_wcur = sem("current_weights")
        s_st = [sem("slot0_staged"), sem("slot1_staged")]
        s_proj, s_th, s_xbc, s_z, s_bt, s_btc, s_g, s_gm = (sem(n) for n in (
            "projected", "tanh_done", "xbc_ready", "z_ready", "bc_transposed", "bc_copied", "g_ready", "gm_ready"))
        s_seg, s_exp, s_m, s_xdt, s_xd, s_y, s_yd, s_yg = (sem(n) for n in (
            "seg_ready", "exp_done", "m_ready", "xdt_ready", "xd_ready", "y_ready", "y_plus_d", "y_gated"))
        s_ss, s_var, s_rr, s_yr, s_yt, s_ytc, s_o, s_x = (sem(n) for n in (
            "ss_ready", "var_ready", "r_ready", "y_normed", "y_transposed", "yt_copied", "o_ready", "x_updated"))

        w1s = em[0][:].rearrange("p a b c -> p (a b c)").rearrange("p (e h) -> p e h", e=E)
        w2s = em[1][:].rearrange("p a b c -> p (a b c)").rearrange("p (e h) -> p e h", e=E)
        w3s = h_pad[0][:].rearrange("p j v -> p (j v)")[:, 0:E * C].rearrange("p (e c) -> p e c", e=E)
        xq = rstd[:, 0:CK]
        zflat = z_all[:].rearrange("p a b c -> p (a b c)")
        sil = [zflat[:, CK * i:CK * (i + 1)] for i in range(2)]
        hid = [zflat[:, CK * (2 + i):CK * (3 + i)] for i in range(3)]
        gate_w = sb("gate_w", [P, NBATCH, E])
        gate_b = sb("gate_b", [P, E])
        rank = sb("rank", [P, E])
        NT2 = NPAIR * NBATCH
        hb = h_pad[1][:].rearrange("p j v -> p (j v)")
        prob, hot1, hot2, work = (hb[:, NT2 * E * i:NT2 * E * (i + 1)].rearrange("p (t e) -> p t e", e=E)
                                  for i in range(4))
        mix = sb("mix", [P, NPAIR, NBATCH, E])
        top = [sb(f"top{i}", [P, NT2]) for i in range(4)]
        s_out = sem("out_stored")
        s_ew = sem("expert_weights_loaded")
        s_bt2, s_x1, s_gate, s_mix, s_prob = (sem(n) for n in (
            "conv_transposed", "x1_ready", "gate_ready", "mix_step", "prob_exp"))
        s_xq, s_h12, s_sil, s_hid, s_eo, s_acc = (sem(n) for n in (
            "xq_ready", "h12_ready", "silu_done", "hidden_ready", "expert_out", "accumulated"))
        NSTEP = NBATCH * E
        N_ACC = NCK * NSTEP

        def hcols(s, j):
            return h_pad[s][:].rearrange("p j v -> p (j v)")[:, bass.ds(j * wide[s], wide[s])]

        def lhs(s, ap, first):
            return ap[:, QS[s] * first:QS[s] * first + P]

        def x_tokens(s, j, n):
            if s == 0:
                return x_io[0][:].rearrange("p (t v) -> p t v", v=P)[:, bass.ds(j, n), :]
            v = x_io[1][:].rearrange("p (v t q) -> p t v q", v=BANDS, q=QS[1])
            return v[:, bass.ds(j, n), :, :]

        def in_tiles(s, ap):
            if s == 0:
                return ap.rearrange("p (t v) -> p t v", v=P)
            return ap.rearrange("p (t v q) -> p t v q", v=BANDS, q=QS[1])

        block = ctx.enter_context(nc.Block())

        @block.sync
        def _(sp):
            for b in range(NBATCH):
                sp.dma_start(x_in[:, :, b, :], a["x"][b].rearrange("t k c -> (t k) c").rearrange(
                    "(j p) c -> p j c", p=P)).then_inc(s_ld, 16)
            for s, nm in enumerate(names):
                for d in range(2):
                    rows = slice(C * d, C * d + C)
                    sp.dma_start(win_raw[rows, s], a[f"{nm}_Win"].rearrange("l c n -> c l n")).then_inc(s_wld, 16)
                    sp.dma_start(small[rows, s, :, 0:1], a[f"{nm}_norm"].rearrange("l (c o) -> c l o", o=1),
                                 allow_slow_non_contiguous=True).then_inc(s_wld, 16)
                    sp.dma_start(cw_raw[rows, s], a[f"{nm}_cw"][:, d, :].partition_broadcast(C)).then_inc(s_wld, 16)
                    sp.dma_start(cw_raw2[rows, s], a[f"{nm}_cw"][:, 2 + d, :].partition_broadcast(C)).then_inc(s_wld, 16)
                sp.dma_start(small[:, s, :, 1:2], a[f"{nm}_gn"].rearrange("l (c o) -> c l o", o=1),
                                 allow_slow_non_contiguous=True).then_inc(s_wld, 16)
                sp.dma_start(wout_raw[:, s], a[f"{nm}_Wout"].rearrange("l c n -> c l n")).then_inc(s_wld, 16)
                sp.dma_start(hd_raw[:, s, :, 0, :], a[f"{nm}_D"].partition_broadcast(P)).then_inc(s_wld, 16)
                sp.dma_start(hd_raw[:, s, :, 1, :], a[f"{nm}_Alog"].partition_broadcast(P)).then_inc(s_wld, 16)
                sp.dma_start(wall[:, :, s, W_DTB:W_DTB + HEADS], a[f"{nm}_dtb"].partition_broadcast(P)).then_inc(s_wld, 16)
                sp.dma_start(cb_raw[CBROWS * s:CBROWS * (s + 1), :],
                             a[f"{nm}_cb"].rearrange("l n -> (l n)").rearrange("(p f) -> p f", f=16)).then_inc(s_wld, 16)
            sp.wait_ge(s_wd, WD_CB)
            sp.wait_ge(s_const, N_CONST)
            brow = ball[:].rearrange("p s l n -> p (s l n)")
            for r in range(NPART):
                sp.dma_start(brow[r:r + 1, :].rearrange("o (p f) -> o p f", f=16),
                             cb_part[:, r, :]).then_inc(s_bld, 16)

            with sp.Fori(0, n_layers) as layer:
                for s in range(2):
                    g = 2 * layer + s

                    def stage_in(m, u, first):
                        j = 2 * m + u
                        if not first:
                            sp.wait_ge(s_h, NCK * (g + 1))
                            sp.wait_ge(s_proj, NPAIR * g + j - 1)
                        for b in range(2):
                            src = hcols(s, j)[C * b:C * b + C, :]
                            sp.dma_start(slot[s][u][b][0:C, :], src).then_inc(s_st[u], 16)
                            sp.dma_start(slot[s][u][b][C:P, 0:wide[s] - QS[s]], src[:, QS[s]:wide[s]]).then_inc(s_st[u], 16)

                    sp.wait_ge(s_h, NCK * g + 1)
                    stage_in(0, 0, True)
                    stage_in(0, 1, True)
                    with sp.Fori(1, NPAIR // 2) as m:
                        stage_in(m, 0, False)
                        stage_in(m, 1, False)

            sp.wait_ge(s_x, NPAIR * 2 * n_layers)
            sp.wait_ge(s_y, NPAIR * 2 * n_layers)
            for b in range(2):
                rows = slice(C * b, C * b + C)
                sp.dma_start(w1s[rows], a["w1"].rearrange("e c h -> c e h")).then_inc(s_ew, 16)
                sp.dma_start(w2s[rows], a["w2"].rearrange("e c h -> c e h")).then_inc(s_ew, 16)
                sp.dma_start(gate_w[rows, b, :], a["gate_w"]).then_inc(s_ew, 16)
            sp.dma_start(w3s, a["w3"].rearrange("e h c -> h e c")).then_inc(s_ew, 16)
            sp.dma_start(gate_b[:], a["gate_b"].partition_broadcast(P)).then_inc(s_ew, 16)

            sp.wait_ge(s_acc, N_ACC)
            for b in range(NBATCH):
                sp.dma_start(out[b].rearrange("t k c -> (t k) c").rearrange("(j p) c -> p j c", p=P),
                             x_in[:, :, b, :]).then_inc(s_out, 16)
            sp.wait_ge(s_out, 16 * NBATCH)

        @block.gpsimd
        def _(pool):
            made = [0]

            def const(ins):
                made[0] += 1
                ins.then_inc(s_const, 1)
                pool.wait_ge(s_const, made[0])

            const(pool.memset(ident[:], 0.0))
            const(pool.affine_select(out=ident[:], in_=ident[:], compare_op=ALU.not_equal, fill=1.0, base=0,
                                     pattern=[[-1, P]], channel_multiplier=1))
            const(pool.tensor_copy(identb[:], ident[:]))
            const(pool.memset(tri[0][:], 1.0))
            const(pool.memset(tri[1][:], 0.0))
            v = tri[1][:].rearrange("p (v q) -> p v q", q=QS[1])
            for k in range(SEQ[1]):
                const(pool.affine_select(out=v, in_=v, compare_op=ALU.not_equal, fill=1.0, base=-QS[1] * k,
                                         pattern=[[0, SEQ[1]], [-1, QS[1]]], channel_multiplier=1))
            for s in range(2):
                const(pool.affine_select(out=tri[s][:], in_=tri[s][:], compare_op=ALU.is_ge, fill=0.0, base=0,
                                         pattern=[[1, P]], channel_multiplier=-1))
            const(pool.memset(mean64[:], 0.0))
            for b in range(2):
                const(pool.memset(mean64[C * b:C * b + C, C * b:C * b + C], 1.0 / C))
            const(pool.memset(ones3[:], 0.0))
            const(pool.memset(ones3[0:NPART, :], 1.0))
            for tile, value in ((head_row, 1.0), (head_neg, -1.0)):
                const(pool.memset(tile[:], 0.0))
                for r in range(NPART):
                    v = tile[PART * r:PART * (r + 1)]
                    const(pool.affine_select(out=v, in_=v, compare_op=ALU.not_equal, fill=value, base=0,
                                             pattern=[[-1, BH], [0, P]], channel_multiplier=1))
            blocks = slice(NPART * PART, P)
            v = head_neg[blocks].rearrange("p h (k t) -> p h k t", k=PART)
            const(pool.affine_select(out=v, in_=v, compare_op=ALU.is_ge, fill=FAR, base=0,
                                     pattern=[[0, BH], [1, PART], [0, P // PART]], channel_multiplier=-1))
            const(pool.memset(cum_t[:], 0.0))
            v = cum_t[blocks].rearrange("p h (k t) -> p h k t", k=PART)
            const(pool.affine_select(out=v, in_=v, compare_op=ALU.not_equal, fill=1.0, base=0,
                                     pattern=[[0, NPAIR], [-1, PART], [0, P // PART]], channel_multiplier=1))
            const(pool.memset(eps6[:], 1e-6))
            const(pool.memset(eps5[:], 1e-5))
            const(pool.memset(mhalf[:], -0.5))
            const(pool.memset(eps2[:], 1e-6))
            const(pool.memset(ball[:], 0.0))
            const(pool.memset(parts[:], 0.0))
            for s in range(2):
                const(pool.memset(h_pad[s][:], 0.0))
            const(pool.memset(gate_w[:], 0.0))
            const(pool.iota(rank[:], pattern=[[-1, E]], base=E, channel_multiplier=0,
                            allow_small_or_imprecise_dtypes=True))
            assert made[0] == N_CONST

            pool.wait_ge(s_wd, WD_ALL)
            pool.wait_ge(s_bld, 16 * NPART)
            with pool.Fori(0, n_layers) as layer:
                for s in range(2):
                    g = 2 * layer + s

                    pool.wait_ge(s_x, NPAIR * g)
                    pool.tensor_copy(wcur[s][:], wall[:, bass.ds(layer, 1), s, :].rearrange("p l n -> p (l n)")
                                     ).then_inc(s_wcur, 1)
                    pool.tensor_copy(bcur[s][:], ball[:, s, bass.ds(layer, 1), :].rearrange("p l n -> p (l n)")
                                     ).then_inc(s_wcur, 1)
                    pool.wait_ge(s_wcur, 2 * g + 2)
                    pool.wait_ge(s_dt, 2 * g + 2)

                    def x_dt(m, u, first):
                        j, n = 2 * m + u, NPAIR * g + 2 * m + u
                        pool.wait_ge(s_xbc, 2 * n + 2)
                        if not first:
                            pool.wait_ge(s_y, n - 1)
                        xs = xbc[u][:, :, 0:DIN]
                        pool.tensor_tensor(
                            out=xdt[u][:].rearrange("p b (h d) -> p b h d", h=HEADS),
                            in0=xs.rearrange("p b (h d) -> p b h d", h=HEADS),
                            in1=dt_half[:, bass.ds(BH * j, BH)].rearrange("p (b h o) -> p b h o", b=NBATCH, o=1)
                                .to_broadcast([P, NBATCH, HEADS, HD]),
                            op=ALU.mult).then_inc(s_xdt, 1)
                        if not first:
                            pool.wait_ge(s_yd, n - 1)
                        pool.tensor_tensor(
                            out=xd[u][:], in0=xs,
                            in1=wcur[s][:, W_D:W_D + DIN].rearrange("p (o d) -> p o d", o=1)
                                .to_broadcast([P, NBATCH, DIN]),
                            op=ALU.mult).then_inc(s_xd, 1)

                    def norm(m, u, first):
                        n = NPAIR * g + 2 * m + u
                        pool.wait_ge(s_ss, 2 * n + 2)
                        pool.tensor_tensor(out=var[:], in0=ss[u][:], in1=eps2[:], op=ALU.add).then_inc(s_var, 1)
                        pool.wait_ge(s_var, n + 1)
                        pool.tensor_tensor(out=rr[:], in0=var[:], in1=mhalf[:], op=ALU.pow).then_inc(s_rr, 1)
                        pool.wait_ge(s_rr, n + 1)
                        if not first:
                            pool.wait_ge(s_yt, n - 1)
                        pool.tensor_tensor(
                            out=yr[u][:], in0=yg[u][:],
                            in1=rr[:].rearrange("p (b o) -> p b o", o=1).to_broadcast([P, NBATCH, DIN]),
                            op=ALU.mult).then_inc(s_yr, 1)

                    def step(m, u, j=None):
                        if j is None or j + 1 < NPAIR:
                            x_dt(m + (u + 1) // 2, (u + 1) % 2, j is not None and j + 1 < 2)
                        if j is None or j >= 1:
                            norm(m + (u - 1) // 2, (u - 1) % 2, j is not None and j - 1 < 2)

                    for j in range(-1, 2):
                        step(j // 2, j % 2, j)
                    with pool.Fori(1, NPAIR // 2 - 1) as m:
                        step(m, 0)
                        step(m, 1)
                    for j in range(NPAIR - 2, NPAIR + 1):
                        step(j // 2, j % 2, j)

        @block.tensor
        def _(pe):
            pe.wait_ge(s_const, N_CONST)

            def to_features(done, tiles, count):
                for j in range(NPAIR):
                    t = pe.transpose(bank[j // 4][:, P * (j % 4):P * (j % 4) + P], tiles(j), ident[:])
                    if j % 4 == 3:
                        t.then_inc(done, 1)

            pe.wait_ge(s_ln, LN_STEPS)
            to_features(s_tp, lambda j: sq[:, P * j:P * j + P], 0)

            with pe.Fori(0, n_layers) as layer:
                for s in range(2):
                    g = 2 * layer + s
                    w = wcur[s]

                    for c in range(NCK):
                        pe.wait_ge(s_sq, NCK * g + c + 1)
                        pe.matmul(bank[c][:], mean64[:], sq[:, CK * c:CK * (c + 1)],
                                  start=True, stop=True).then_inc(s_ms, 1)
                    pe.wait_ge(s_wcur, 2 * g + 2)
                    for j in range(NPAIR):
                        if j % 4 == 0:
                            pe.wait_ge(s_h, NCK * g + j // 4 + 1)
                        mm = pe.matmul(bank[4][:, BH * j:BH * (j + 1)], lhs(s, hcols(s, j), DCONV - 1),
                                       w[:, W_DT:W_DT + BH], start=True, stop=True)
                    mm.then_inc(s_dtp, 1)
                    pe.wait_ge(s_dta, g + 1)
                    pe.matmul(bank[5][:, 0:NPAIR * BH], tri[s][:], dta_log[:],
                              start=True, stop=True).then_inc(s_cum, 1)
                    pe.wait_ge(s_lo, g + 1)
                    for i in range(2):
                        ptb = bank[6 + i][:].bitcast(BF16)
                        for k in range(NPAIR // 2):
                            t = pe.transpose(ptb[0:NPART * PART, P * k:P * (k + 1)],
                                             parts[:, NPAIR // 2 * i + k].rearrange("p r h -> p (r h)"), identb[:])
                        t.then_inc(s_pt, 1)

                    def project(m, u, first):
                        n = NPAIR * g + 2 * m + u
                        pe.wait_ge(s_st[u], 64 * ((NPAIR // 2) * g + m + 1))
                        if not first:
                            pe.wait_ge(s_z, n)
                        for b in range(2):
                            src = slot[s][u][b][:]
                            o = bank[b]
                            pe.matmul(o[:, 0:CONVD], ones3[:], bcur[s][:], start=True, stop=False,
                                      skip_group_check=True)
                            pe.matmul(o[:, 0:CONVD], lhs(s, src, 0), w[:, W_C0:W_C0 + CONVD], start=False,
                                      stop=False, skip_group_check=True)
                            mm = pe.matmul(o[:, 0:CONVD + DIN], lhs(s, src, 2), w[:, W_C1:W_C1 + CONVD + DIN],
                                           start=False, stop=True, skip_group_check=True)
                        mm.then_inc(s_proj, 1)

                    def turn_bc(m, u, first):
                        n = NPAIR * g + 2 * m + u
                        pe.wait_ge(s_xbc, 2 * n + 2)
                        if not first:
                            pe.wait_ge(s_gm, n)
                        for b in range(2):
                            for k in range(2):
                                t = pe.transpose(bank[4][0:NST, (2 * b + k) * P:(2 * b + k + 1) * P],
                                                 xbc[u][:, b, DIN + NST * k:DIN + NST * (k + 1)], ident[:])
                        t.then_inc(s_bt, 1)

                    def b_dot_c(m, u):
                        pe.wait_ge(s_btc, NPAIR * g + 2 * m + u + 1)
                        for b in range(2):
                            mm = pe.matmul(bank[4][:, P * b:P * (b + 1)], bct[u][:, b, 0, :], bct[u][:, b, 1, :],
                                           start=True, stop=True)
                        mm.then_inc(s_g, 1)

                    def decays(m, u, q, first):
                        n = NPAIR * g + 2 * m + u
                        b, hh = q // 2, q % 2
                        if not first:
                            pe.wait_ge(s_exp, 4 * n + q - 1)
                        o = bank[2 + hh]
                        tile = cum_t[:, bass.ds(2 * m + u, 1), :].rearrange("p o t -> p (o t)")
                        h0 = HEADS * b + 4 * hh
                        pe.matmul(o[:], tile, head_neg[:, h0:h0 + 4, :].rearrange("p h t -> p (h t)"),
                                  start=True, stop=False, skip_group_check=True)
                        for h in range(4):
                            mm = pe.matmul(o[:, P * h:P * (h + 1)], head_row[:, h0 + h, :], tile,
                                           start=False, stop=(h == 3), skip_group_check=True)
                        mm.then_inc(s_seg, 1)

                    def mix_states(m, u, first):
                        n = NPAIR * g + 2 * m + u
                        pe.wait_ge(s_m, 4 * n + 4)
                        pe.wait_ge(s_xdt, n + 1)
                        if not first:
                            pe.wait_ge(s_yd, n)
                        for b in range(2):
                            for h in range(HEADS):
                                mm = pe.matmul(bank[5][:, DIN * b + HD * h:DIN * b + HD * (h + 1)], em[u][:, b, h, :],
                                               xdt[u][:, b, HD * h:HD * (h + 1)], start=True, stop=True)
                        mm.then_inc(s_y, 1)

                    def turn_y(m, u, first):
                        n = NPAIR * g + 2 * m + u
                        pe.wait_ge(s_yr, n + 1)
                        if not first:
                            pe.wait_ge(s_ytc, n)
                        for b in range(2):
                            t = pe.transpose(bank[6][:, P * b:P * (b + 1)], yr[u][:, b, :], ident[:])
                        t.then_inc(s_yt, 1)

                    def project_out(m, u, first):
                        n = NPAIR * g + 2 * m + u
                        pe.wait_ge(s_ytc, n + 1)
                        if not first:
                            pe.wait_ge(s_x, n)
                        for b in range(2):
                            mm = pe.matmul(bank[7][C * b:C * (b + 1), 0:P], w[:, W_OUT:W_OUT + C], yt[:, b, :],
                                           start=True, stop=True)
                        mm.then_inc(s_o, 1)

                    def step(m, u, j=None):
                        nxt = (m + (u + 1) // 2, (u + 1) % 2)
                        prv = (m + (u - 1) // 2, (u - 1) % 2)
                        pr2 = (m - 1, u)
                        has_next = j is None or j + 1 < NPAIR
                        here = j is None or 0 <= j < NPAIR
                        if has_next:
                            project(*nxt, j is not None and j + 1 < 1)
                        if j is None or 1 <= j <= NPAIR:
                            mix_states(*prv, j is not None and j - 1 < 1)
                        if j is None or j >= 2:
                            turn_y(*pr2, j is not None and j - 2 < 1)
                        if here:
                            decays(m, u, 0, j == 0)
                            decays(m, u, 1, j == 0)
                        if has_next:
                            turn_bc(*nxt, j is not None and j + 1 < 1)
                        if here:
                            decays(m, u, 2, False)
                            decays(m, u, 3, False)
                        if has_next:
                            b_dot_c(*nxt)
                        if j is None or j >= 2:
                            project_out(*pr2, j is not None and j - 2 < 1)

                    step(-1, 1, -1)
                    pe.wait_ge(s_ct, 2 * (g + 1))
                    for j in range(2):
                        step(j // 2, j % 2, j)
                    with pe.Fori(1, NPAIR // 2 - 1) as m:
                        step(m, 0)
                        step(m, 1)
                    for j in range(NPAIR - 2, NPAIR + 2):
                        step(j // 2, j % 2, j)

            pe.wait_ge(s_x, NPAIR * 2 * n_layers)
            to_features(s_bt2, lambda j: x_io[0][:, P * j:P * j + P], 0)
            pe.wait_ge(s_x1, NCK)
            pe.wait_ge(s_ln, 2 * LN_STEPS)
            to_features(s_tp, lambda j: sq[:, P * j:P * j + P], 1)
            pe.wait_ge(s_ew, 16 * 8)
            for j in range(NPAIR):
                if j % 4 == 0:
                    pe.wait_ge(s_x0, NCK + j // 4 + 1)
                mm = pe.matmul(bank[4][:, NBATCH * E * j:NBATCH * E * (j + 1)], x_io[1][:, P * j:P * j + P],
                               gate_w[:].rearrange("p b e -> p (b e)"), start=True, stop=True)
            mm.then_inc(s_gate, 1)

            pe.wait_ge(s_mix, MIX_STEPS)
            with pe.Fori(0, NCK) as q:
                base = NSTEP * q

                def expert_in(i):
                    e, b = i // 2, i % 2
                    if i == 0:
                        pe.wait_ge(s_xq, q + 1)
                    if i >= 3:
                        pe.wait_ge(s_hid, base + i - 2)
                    rows = slice(C * b, C * b + C)
                    pe.matmul(bank[2 * (i % 3)][:], w1s[rows, e, :], xq[rows, :], start=True, stop=True)
                    pe.matmul(bank[2 * (i % 3) + 1][:], w2s[rows, e, :], xq[rows, :],
                              start=True, stop=True).then_inc(s_h12, 1)

                def expert_out(i):
                    e = i // 2
                    pe.wait_ge(s_hid, base + i + 1)
                    if i >= 2:
                        pe.wait_ge(s_acc, base + i - 1)
                    for t in range(4):
                        mm = pe.matmul(bank[6 + i % 2][:, C * t:C * (t + 1)], hid[i % 3][:, P * t:P * (t + 1)],
                                       w3s[:, e, :], start=True, stop=True)
                    mm.then_inc(s_eo, 1)

                pe.wait_ge(s_acc, base)
                for i in range(NSTEP + 2):
                    if i < NSTEP:
                        expert_in(i)
                    if i >= 2:
                        expert_out(i - 2)

        @block.scalar
        def _(act):
            def norm_scalar(k, eps):
                act.wait_ge(s_ln, LN_STEPS * k + 3)
                act.activation(x_io[1][:], sq[:], ACT.Square).then_inc(s_ln, 1)
                act.wait_ge(s_ln, LN_STEPS * k + 5)
                act.activation(stat2[:], stat2[:], ACT.Ln, bias=eps[:], scale=1.0 / C).then_inc(s_ln, 1)
                act.wait_ge(s_ln, LN_STEPS * k + 6)
                act.activation(stat2[:], stat2[:], ACT.Exp, scale=-0.5).then_inc(s_ln, 1)

            act.wait_ge(s_const, N_CONST)
            act.wait_ge(s_wld, 16 * N_WDMA)
            act.activation(hd_raw[:, :, :, 1, :], hd_raw[:, :, :, 1, :], ACT.Exp).then_inc(s_ea, 1)
            norm_scalar(0, eps6)

            with act.Fori(0, n_layers) as layer:
                for s in range(2):
                    g = 2 * layer + s
                    act.wait_ge(s_x0, NCK)
                    act.wait_ge(s_x, NPAIR * g)
                    for c in range(NCK):
                        act.activation(in_tiles(s, sq[:, CK * c:CK * (c + 1)]), x_tokens(s, 4 * c, 4),
                                       ACT.Square).then_inc(s_sq, 1)
                    for c in range(NCK):
                        act.wait_ge(s_ms, NCK * g + c + 1)
                        act.activation(rstd[:, CK * c:CK * (c + 1)], bank[c][:], ACT.Ln,
                                       bias=eps6[:]).then_inc(s_lnv, 1)
                    for c in range(NCK):
                        act.wait_ge(s_lnv, NCK * g + c + 1)
                        r = rstd[:, CK * c:CK * (c + 1)]
                        act.activation(r, r, ACT.Exp, scale=-0.5).then_inc(s_rstd, 1)
                    act.wait_ge(s_v, g + 1)
                    act.activation(dta[:], dtv[:], ACT.Abs).then_inc(s_abs, 1)
                    act.wait_ge(s_abs, g + 1)
                    act.activation(dta[:], dta[:], ACT.Exp, scale=-1.0).then_inc(s_e, 1)
                    act.wait_ge(s_e, g + 1)
                    act.activation(dtl[:], dta[:], ACT.Ln, bias=1.0).then_inc(s_l, 1)
                    act.wait_ge(s_cum, g + 1)
                    act.activation(parts[:, :, 0, 0:BH],
                                   bank[5][:, 0:NPAIR * BH].rearrange("p (j k) -> p j k", k=BH),
                                   ACT.Copy).then_inc(s_hi, 1)
                    act.wait_ge(s_pt, 2 * g + 1)
                    act.activation(cum_t[0:NPART * PART, 0:NPAIR // 2, :].rearrange("p j t -> p (j t)"),
                                   bank[6][:].bitcast(BF16)[0:NPART * PART, :], ACT.Copy).then_inc(s_ct, 1)

                    def tanh(m, u, first):
                        n = NPAIR * g + 2 * m + u
                        act.wait_ge(s_proj, n + 1)
                        if not first:
                            act.wait_ge(s_z, n)
                        for b in range(2):
                            act.activation(th[:, b, :], bank[b][:, 0:CONVD + DIN], ACT.Tanh,
                                           scale=0.5).then_inc(s_th, 1)

                    def copy_bc(m, u):
                        act.wait_ge(s_bt, NPAIR * g + 2 * m + u + 1)
                        act.activation(bct[u][:].rearrange("p b k t -> p (b k t)"), bank[4][0:NST, :],
                                       ACT.Copy).then_inc(s_btc, 1)

                    def exps(m, u, q, first):
                        n = NPAIR * g + 2 * m + u
                        act.wait_ge(s_seg, 4 * n + q + 1)
                        if not first:
                            act.wait_ge(s_y, n - 1)
                        act.activation(em[u][:, q // 2, 4 * (q % 2):4 * (q % 2) + 4, :].rearrange("p h t -> p (h t)"),
                                       bank[2 + q % 2][:], ACT.Exp).then_inc(s_exp, 1)

                    def squares(m, u):
                        n = NPAIR * g + 2 * m + u
                        act.wait_ge(s_yg, n + 1)
                        for b in range(2):
                            act.wait_ge(s_ss, 2 * n + b)
                            act.activation(ysq[:], yg[u][:, b, :], ACT.Square, scale=0.5 * DIN ** -0.5,
                                           accum_out=ss[u][:, b:b + 1]).then_inc(s_ss, 1)

                    def copy_yt(m, u, first):
                        n = NPAIR * g + 2 * m + u
                        act.wait_ge(s_yt, n + 1)
                        if not first:
                            act.wait_ge(s_o, n)
                        act.activation(yt[:].rearrange("p b t -> p (b t)"), bank[6][:, 0:2 * P],
                                       ACT.Copy).then_inc(s_ytc, 1)

                    def step(m, u, j=None):
                        nxt = (m + (u + 1) // 2, (u + 1) % 2)
                        prv = (m + (u - 1) // 2, (u - 1) % 2)
                        pr2 = (m - 1, u)
                        has_next = j is None or j + 1 < NPAIR
                        here = j is None or 0 <= j < NPAIR
                        if has_next:
                            tanh(*nxt, j is not None and j + 1 < 1)
                        if j is None or j >= 2:
                            copy_yt(*pr2, j is not None and j - 2 < 1)
                        if here:
                            exps(m, u, 0, j is not None and j < 2)
                            exps(m, u, 1, j is not None and j < 2)
                        if has_next:
                            copy_bc(*nxt)
                        if here:
                            exps(m, u, 2, j is not None and j < 2)
                            exps(m, u, 3, j is not None and j < 2)
                        if j is None or 1 <= j <= NPAIR:
                            squares(*prv)

                    for j in range(-1, 2):
                        step(j // 2, j % 2, j)
                    with act.Fori(1, NPAIR // 2 - 1) as m:
                        step(m, 0)
                        step(m, 1)
                    for j in range(NPAIR - 2, NPAIR + 2):
                        step(j // 2, j % 2, j)

            norm_scalar(1, eps5)
            act.wait_ge(s_mix, 3)
            act.activation(prob, prob, ACT.Exp).then_inc(s_prob, 1)
            act.wait_ge(s_x0, 2 * NCK)
            act.wait_ge(s_mix, MIX_STEPS)
            with act.Fori(0, NCK) as q:
                base = NSTEP * q
                act.wait_ge(s_acc, base)
                act.activation(xq, x_io[1][:, bass.ds(CK * q, CK)], ACT.Copy).then_inc(s_xq, 1)
                for i in range(NSTEP):
                    act.wait_ge(s_h12, base + i + 1)
                    if i >= 2:
                        act.wait_ge(s_hid, base + i - 1)
                    act.activation(sil[i % 2], bank[2 * (i % 3)][:], ACT.Silu).then_inc(s_sil, 1)

        @block.vector
        def _(dve):
            tm = sq[:].rearrange("p (t c) -> p t c", c=C)
            xi = x_in[:].rearrange("p j b c -> p (j b) c")
            sq2 = x_io[1][:].rearrange("p (t c) -> p t c", c=C)

            def spread(ap, n):
                return ap.rearrange("p (t o) -> p t o", o=1).to_broadcast([P, NPAIR * NBATCH, n])

            def norm_vector(k):
                dve.tensor_reduce(stat[:], xi, AX.X, ALU.add).then_inc(s_ln, 1)
                dve.wait_ge(s_ln, LN_STEPS * k + 1)
                dve.tensor_scalar(stat[:], stat[:], 1.0 / C, None, ALU.mult).then_inc(s_ln, 1)
                dve.wait_ge(s_ln, LN_STEPS * k + 2)
                dve.tensor_tensor(tm, xi, spread(stat[:], C), ALU.subtract).then_inc(s_ln, 1)
                dve.wait_ge(s_ln, LN_STEPS * k + 4)
                dve.tensor_reduce(stat2[:], sq2, AX.X, ALU.add).then_inc(s_ln, 1)
                dve.wait_ge(s_ln, LN_STEPS * k + 7)
                dve.tensor_tensor(tm, tm, spread(stat2[:], C), ALU.mult).then_inc(s_ln, 1)

            def from_banks(k, dst):
                for c in range(NCK):
                    dve.wait_ge(s_tp, NCK * k + c + 1)
                    dve.tensor_copy(dst[:, CK * c:CK * (c + 1)], bank[c][:]).then_inc(s_x0, 1)

            dve.wait_ge(s_const, N_CONST)
            dve.wait_ge(s_wld, 16 * N_WDMA)

            made = [0]

            def link(ins):
                made[0] += 1
                ins.then_inc(s_wd, 1)
                dve.wait_ge(s_wd, made[0])

            link(dve.tensor_copy(cb_part[:, 0, :], cb_raw[:]))
            link(dve.tensor_tensor(cb_rest[:], cb_raw[:], cb_part[:, 0, :], ALU.subtract))
            link(dve.tensor_copy(cb_part[:, 1, :], cb_rest[:]))
            link(dve.tensor_tensor(cb_part[:, 2, :], cb_rest[:], cb_part[:, 1, :], ALU.subtract))
            for s in range(2):
                wn = win_raw[:, s]
                link(dve.tensor_tensor(wn, wn, small[:, s, :, 0:1].to_broadcast([P, NL, PROJ]), ALU.mult))
                link(dve.tensor_tensor(wall[:, :, s, W_C0:W_C0 + CONVD], wn[:, :, DIN:DIN + CONVD], cw_raw[:, s],
                                       ALU.mult))
                link(dve.tensor_tensor(wall[:, :, s, W_C1:W_C1 + CONVD], wn[:, :, DIN:DIN + CONVD], cw_raw2[:, s],
                                       ALU.mult))
                link(dve.memset(wall[:, :, s, W_C1 + CONVD:W_DT + BH], 0.0))
                link(dve.tensor_copy(wall[C:P, :, s, W_C1 + CONVD:W_DT], wn[C:P, :, 0:DIN]))
                for b in range(2):
                    link(dve.tensor_copy(wall[C * b:C * (b + 1), :, s, W_DT + HEADS * b:W_DT + HEADS * (b + 1)],
                                         wn[C * b:C * (b + 1), :, DIN + CONVD:PROJ]))
                link(dve.scalar_tensor_tensor(out=wall[:, :, s, W_OUT:W_OUT + C], in0=wout_raw[:, s], scalar=0.5,
                                              in1=small[:, s, :, 1:2].to_broadcast([P, NL, C]),
                                              op0=ALU.mult, op1=ALU.mult))
                for i in range(NL):
                    link(dve.tensor_scalar(
                        wall[:, i, s, W_D:W_D + DIN].rearrange("p (h d) -> p h d", h=HEADS),
                        hd_raw[:, s, i, 0, :].rearrange("p (h o) -> p h o", o=1).to_broadcast([P, HEADS, HD]),
                        0.5, None, ALU.mult))
                dve.wait_ge(s_ea, 1)
                link(dve.tensor_scalar(wall[:, :, s, W_NA:W_NA + HEADS], hd_raw[:, s, :, 1, :], -1.0, None,
                                       ALU.mult))
            assert made[0] == WD_ALL

            dve.wait_ge(s_ld, 16 * NBATCH)
            norm_vector(0)
            from_banks(0, x_io[0])

            with dve.Fori(0, n_layers) as layer:
                for s in range(2):
                    g = 2 * layer + s
                    w = wcur[s]
                    for c in range(NCK):
                        dve.wait_ge(s_rstd, NCK * g + c + 1)
                        h = h_pad[s][:, 4 * c:4 * (c + 1), wide[s] - P:]
                        if s == 1:
                            h = h.rearrange("p t (v q) -> p t v q", q=QS[1])
                        dve.tensor_tensor(h, x_tokens(s, 4 * c, 4), in_tiles(s, rstd[:, CK * c:CK * (c + 1)]),
                                          ALU.mult).then_inc(s_h, 1)
                    dve.wait_ge(s_dtp, g + 1)

                    def per_head(col):
                        return w[:, col:col + HEADS].rearrange("p (o h) -> p o h", o=1).to_broadcast(
                            [P, NPAIR * NBATCH, HEADS])

                    def heads(t):
                        return t[:, 0:NPAIR * BH].rearrange("p (t h) -> p t h", h=HEADS)

                    dve.wait_ge(s_wcur, 2 * g + 2)
                    dve.tensor_tensor(heads(dtv), heads(bank[4]), per_head(W_DTB), ALU.add).then_inc(s_v, 1)
                    dve.wait_ge(s_l, g + 1)
                    dve.scalar_tensor_tensor(out=dtl[:], in0=dtv[:], scalar=0.0, in1=dtl[:], op0=ALU.max,
                                             op1=ALU.add).then_inc(s_dt, 1)
                    dve.wait_ge(s_dt, 2 * g + 1)
                    dve.tensor_tensor(heads(dta_log), heads(dtl), per_head(W_NA), ALU.mult).then_inc(s_dta, 1)
                    dve.tensor_scalar(dt_half[:], dtl[:], 0.5, None, ALU.mult).then_inc(s_dt, 1)
                    dve.wait_ge(s_hi, g + 1)
                    cum = bank[5][:, 0:NPAIR * BH].rearrange("p (j k) -> p j k", k=BH)
                    r3 = rest[:].rearrange("p (j k) -> p j k", k=BH)
                    dve.tensor_tensor(r3, cum, parts[:, :, 0, 0:BH], ALU.subtract).then_inc(s_rest, 1)
                    dve.wait_ge(s_rest, g + 1)
                    dve.tensor_copy(parts[:, :, 1, 0:BH], r3).then_inc(s_mid, 1)
                    dve.wait_ge(s_mid, g + 1)
                    dve.tensor_tensor(parts[:, :, 2, 0:BH], r3, parts[:, :, 1, 0:BH], ALU.subtract).then_inc(s_lo, 1)
                    dve.wait_ge(s_pt, 2 * g + 2)
                    dve.tensor_copy(cum_t[0:NPART * PART, NPAIR // 2:, :].rearrange("p j t -> p (j t)"),
                                    bank[7][:].bitcast(BF16)[0:NPART * PART, :]).then_inc(s_ct, 1)

                    def gates(m, u, first):
                        n, j = NPAIR * g + 2 * m + u, 2 * m + u
                        if not first:
                            dve.wait_ge(s_xd, n - 1)
                        for b in range(2):
                            dve.wait_ge(s_th, 2 * n + b + 1)
                            dve.scalar_tensor_tensor(out=xbc[u][:, b, :], in0=th[:, b, 0:CONVD], scalar=1.0,
                                                     in1=bank[b][:, 0:CONVD], op0=ALU.add, op1=ALU.mult
                                                     ).then_inc(s_xbc, 1)
                        for b in range(2):
                            ins = dve.scalar_tensor_tensor(
                                out=z_all[:, bass.ds(j, 1), b, :].rearrange("p o d -> p (o d)"),
                                in0=th[:, b, CONVD:], scalar=1.0, in1=bank[b][:, CONVD:CONVD + DIN],
                                op0=ALU.add, op1=ALU.mult)
                            if b == 1:
                                ins.then_inc(s_z, 1)

                    def mask(m, u):
                        dve.wait_ge(s_g, NPAIR * g + 2 * m + u + 1)
                        dve.scalar_tensor_tensor(out=gm[u][:], in0=bank[4][:, 0:2 * P].rearrange("p (b t) -> p b t", b=2),
                                                 scalar=0.25,
                                                 in1=tri[s][:].rearrange("p (o t) -> p o t", o=1).to_broadcast([P, 2, P]),
                                                 op0=ALU.mult, op1=ALU.mult).then_inc(s_gm, 1)

                    def weigh(m, u, q):
                        n, b, hh = NPAIR * g + 2 * m + u, q // 2, q % 2
                        dve.wait_ge(s_exp, 4 * n + q + 1)
                        if q == 0:
                            dve.wait_ge(s_gm, n + 1)
                        e = em[u][:, b, 4 * hh:4 * hh + 4, :]
                        dve.scalar_tensor_tensor(out=e, in0=e, scalar=1.0,
                                                 in1=gm[u][:, b:b + 1, :].to_broadcast([P, 4, P]),
                                                 op0=ALU.min, op1=ALU.mult).then_inc(s_m, 1)

                    def gate_y(m, u, first):
                        n, j = NPAIR * g + 2 * m + u, 2 * m + u
                        dve.wait_ge(s_y, n + 1)
                        dve.wait_ge(s_xd, n + 1)
                        dve.tensor_tensor(yd[:], bank[5][:, 0:2 * DIN].rearrange("p (b d) -> p b d", b=2), xd[u][:],
                                          ALU.add).then_inc(s_yd, 1)
                        dve.wait_ge(s_yd, n + 1)
                        dve.wait_ge(s_z, n + 1)
                        if not first:
                            dve.wait_ge(s_yr, n - 1)
                        dve.tensor_tensor(yg[u][:], yd[:], z_all[:, bass.ds(j, 1), :, :].rearrange("p o b d -> p (o b) d"),
                                          ALU.mult).then_inc(s_yg, 1)

                    def add_x(m, u):
                        n, j = NPAIR * g + 2 * m + u, 2 * m + u
                        dve.wait_ge(s_o, n + 1)
                        o = x_io[1 - s][:].rearrange("p (t v) -> p t v", v=P)[:, bass.ds(j, 1), :]
                        if s == 1:
                            o = o.rearrange("p t (q v) -> p t v q", v=SEQ[1])
                        d = in_tiles(s, bank[7][:, 0:P])
                        dve.tensor_tensor(o, d, x_tokens(s, j, 1), ALU.add).then_inc(s_x, 1)

                    def step(m, u, j=None):
                        nxt = (m + (u + 1) // 2, (u + 1) % 2)
                        prv = (m + (u - 1) // 2, (u - 1) % 2)
                        has_next = j is None or j + 1 < NPAIR
                        here = j is None or 0 <= j < NPAIR
                        if has_next:
                            gates(*nxt, j is not None and j + 1 < 2)
                        if j is None or 1 <= j <= NPAIR:
                            gate_y(*prv, j is not None and j - 1 < 2)
                        if here:
                            for q in range(4):
                                weigh(m, u, q)
                        if has_next:
                            mask(*nxt)
                        if j is None or j >= 2:
                            add_x(m - 1, u)

                    for j in range(-1, 2):
                        step(j // 2, j % 2, j)
                    with dve.Fori(1, NPAIR // 2 - 1) as m:
                        step(m, 0)
                        step(m, 1)
                    for j in range(NPAIR - 2, NPAIR + 2):
                        step(j // 2, j % 2, j)

            for c in range(NCK):
                dve.wait_ge(s_bt2, c + 1)
                v = x_in[:].rearrange("p j b c -> p (j b c)")[:, CK * c:CK * (c + 1)]
                dve.tensor_tensor(v, bank[c][:], v, ALU.add).then_inc(s_x1, 1)
            dve.wait_ge(s_x1, NCK)
            norm_vector(1)
            from_banks(1, x_io[1])

            made2 = [0]

            def mixed(ins):
                made2[0] += 1
                ins.then_inc(s_mix, 1)
                dve.wait_ge(s_mix, made2[0])

            def over_e(t):
                return t[:].rearrange("p (t o) -> p t o", o=1).to_broadcast([P, NT2, E])

            dve.wait_ge(s_gate, 1)
            mixed(dve.tensor_tensor(prob, bank[4][:].rearrange("p (t e) -> p t e", e=E),
                                    gate_b[:].rearrange("p (o e) -> p o e", o=1).to_broadcast([P, NT2, E]), ALU.add))
            mixed(dve.tensor_reduce(top[0][:], prob, AX.X, ALU.max))
            mixed(dve.tensor_tensor(prob, prob, over_e(top[0]), ALU.subtract))
            dve.wait_ge(s_prob, 1)
            mixed(dve.tensor_reduce(top[0][:], prob, AX.X, ALU.add))
            mixed(dve.reciprocal(top[1][:], top[0][:]))
            mixed(dve.tensor_tensor(prob, prob, over_e(top[1]), ALU.mult))
            rk = rank[:].rearrange("p (o e) -> p o e", o=1).to_broadcast([P, NT2, E])
            for i, (hot, src) in enumerate(((hot1, prob), (hot2, work))):
                if i == 1:
                    mixed(dve.scalar_tensor_tensor(out=work, in0=hot1, scalar=-2.0, in1=prob, op0=ALU.mult,
                                                   op1=ALU.add))
                mixed(dve.tensor_reduce(top[i][:], src, AX.X, ALU.max))
                mixed(dve.tensor_tensor(hot, src, over_e(top[i]), ALU.is_equal))
                mixed(dve.tensor_tensor(hot, hot, rk, ALU.mult))
                mixed(dve.tensor_reduce(top[2][:], hot, AX.X, ALU.max))
                mixed(dve.tensor_tensor(hot, hot, over_e(top[2]), ALU.is_equal))
            mixed(dve.tensor_tensor(top[2][:], top[0][:], top[1][:], ALU.add))
            mixed(dve.reciprocal(top[3][:], top[2][:]))
            for i, hot in enumerate((hot1, hot2)):
                mixed(dve.tensor_tensor(top[i][:], top[i][:], top[3][:], ALU.mult))
                mixed(dve.tensor_tensor(hot, hot, over_e(top[i]), ALU.mult))
            mixed(dve.tensor_tensor(mix[:].rearrange("p j b e -> p (j b) e"), hot1, hot2, ALU.add))
            assert made2[0] == MIX_STEPS

            with dve.Fori(0, NCK) as q:
                base = NSTEP * q

                def hidden(i):
                    dve.wait_ge(s_sil, base + i + 1)
                    if i >= 3:
                        dve.wait_ge(s_eo, base + i - 2)
                    dve.tensor_tensor(hid[i % 3], sil[i % 2], bank[2 * (i % 3) + 1][:], ALU.mult).then_inc(s_hid, 1)

                def accumulate(i):
                    e, b = i // 2, i % 2
                    dve.wait_ge(s_eo, base + i + 1)
                    if i >= 2:
                        dve.wait_ge(s_acc, base + i - 1)
                    for t in range(4):
                        v = x_in[:, bass.ds(4 * q + t, 1), b, :].rearrange("p o c -> p (o c)")
                        ins = dve.scalar_tensor_tensor(
                            out=v, in0=bank[6 + i % 2][:, C * t:C * (t + 1)],
                            scalar=mix[:, bass.ds(4 * q + t, 1), b, e:e + 1].rearrange("p o e -> p (o e)"),
                            in1=v, op0=ALU.mult, op1=ALU.add)
                    ins.then_inc(s_acc, 1)

                for i in range(NSTEP + 2):
                    if i < NSTEP:
                        hidden(i)
                    if i >= 2:
                        accumulate(i - 2)


_INS = ["x"] + [f"L0_conv_{k}_{n}" for k in ("t", "b")
                for n in ("norm", "Win", "cw", "cb", "dtb", "Alog", "D", "gn", "Wout")] + [
    f"L0_ffn_{n}" for n in ("gate_w", "gate_b", "w1", "w2", "w3")]


def kernel(**inputs):
    import numpy as _np
    import concourse.bacc as _bacc
    from concourse import mybir as _mybir
    from concourse.bass_utils import run_bass_kernel_spmd as _run

    nc = _bacc.Bacc("TRN2", target_bir_lowering=False, num_devices=1)
    arrays, args = {}, {}
    for name in _INS:
        v = _np.ascontiguousarray(inputs[name])
        arrays[f"in_{name}"] = v
        args[name.replace("L0_conv_", "").replace("L0_ffn_", "")] = nc.dram_tensor(
            f"in_{name}", v.shape, _mybir.dt.from_np(v.dtype), kind="ExternalInput").ap()
    out = nc.dram_tensor("out", inputs["x"].shape, _mybir.dt.from_np(_np.dtype("float32")),
                         kind="ExternalOutput").ap()
    build(nc, args, out)
    return _run(nc, [arrays], core_ids=[0]).results[0]["out"]
```

```python
from contextlib import ExitStack

import concourse.bass as bass
from concourse import mybir

ALU = mybir.AluOpType
ACT = mybir.ActivationFunctionType
AX = mybir.AxisListType
F32 = mybir.dt.float32
BF16 = mybir.dt.bfloat16

P = 128
QUAD = 32
NBATCH = 2
C = 64
TOK = 2048
NPAIR = TOK // P
NL = 6
DIN = 128
NST = 16
HEADS = 8
HD = DIN // HEADS
DCONV = 4
CONVD = DIN + 2 * NST
PROJ = 2 * DIN + 2 * NST + HEADS
SEQ = (128, 16)
QS = (P // SEQ[0], P // SEQ[1])
BANDS = 16
E = 16
HID = 128
BH = NBATCH * HEADS
NPART = 3
NBLK = 32
R_ONE = NPART * BH
R_TOP = P - NBLK
R_BLK = R_TOP
FAR = -30000.0
CK = 512
NCK = TOK // CK

W_C0 = 0
W_C1 = W_C0 + CONVD
W_Z = W_C1 + CONVD
W_DT = W_Z + DIN
W_OUT = W_DT + QUAD
W_D = W_OUT + C
W_DTB = W_D + DIN
W_NA = W_DTB + HEADS
W_ALL = W_NA + HEADS
G_COL = CK - P


def build(nc, a, out, n_layers=NL):
    with ExitStack() as ctx:
        def sb(name, shape, dt=F32):
            return ctx.enter_context(nc.sbuf_tensor(name, shape, dt))

        def sem(name):
            return ctx.enter_context(nc.semaphore(name))

        bank = [ctx.enter_context(nc.psum_tensor(f"bank{i}", [P, CK], F32)) for i in range(8)]

        ident = sb("ident", [P, P])
        identb = sb("identb", [P, P], BF16)
        tri = [sb("tri_time", [P, P]), sb("tri_bands", [P, P])]
        mean64 = sb("mean64", [P, P])
        ones3 = sb("ones3", [P, P], BF16)
        target = [sb(f"target{u}", [P, BH, P], BF16) for u in range(2)]
        eps6 = sb("eps6", [P, 1])
        eps5 = sb("eps5", [P, 1])
        mhalf = sb("mhalf", [P, NBATCH])
        ones1 = sb("ones1", [P, 1])

        wall = sb("wall", [P, NL + 1, 2, W_ALL])
        ball = sb("ball", [P, 2, NL + 1, CONVD], BF16)
        wcur = [sb(f"wcur{s}", [P, W_ALL]) for s in range(2)]
        bcur = [sb(f"bcur{s}", [P, CONVD], BF16) for s in range(2)]

        x_io = [sb("x_time_in", [P, TOK]), sb("x_bands_in", [P, TOK])]
        wide = [(SEQ[s] + DCONV - 1) * QS[s] for s in range(2)]
        h_pad = [sb(f"h_pad{s}", [P, NPAIR, wide[s]]) for s in range(2)]
        slot = [[[sb(f"slot{s}{u}{b}", [P, wide[s]]) for b in range(2)] for u in range(2)] for s in range(2)]
        sq = sb("sq", [P, TOK])
        rstd = sb("rstd", [P, TOK])
        dtv = sb("dtv", [P, NPAIR * BH])
        dta = sb("dta", [P, NPAIR * BH])
        dtl = sb("dtl", [P, NPAIR * BH])
        dtf = sb("dtf", [P, CK])
        dt_half = sb("dt_half", [P, NPAIR * BH])
        dta_log = sb("dta_log", [P, NPAIR * BH])
        rest = sb("rest", [P, NPAIR * BH])
        parts = sb("parts", [P, NPAIR, R_TOP], BF16)
        cum_t = sb("cum_t", [P, NPAIR, P], BF16)

        th = sb("th", [P, NBATCH, CONVD])
        thz = sb("thz", [P, NBATCH, P])
        xbc = [sb(f"xbc{u}", [P, NBATCH, CONVD]) for u in range(2)]
        z_all = sb("z_all", [P, NPAIR, NBATCH, P])
        bt = [sb(f"bt{u}", [2 * QUAD, P]) for u in range(2)]
        ct = [sb(f"ct{u}", [2 * QUAD, P]) for u in range(2)]
        gm = [sb(f"gm{u}", [P, NBATCH, P]) for u in range(2)]
        em = [sb(f"em{u}", [P, NBATCH, HEADS, P]) for u in range(2)]
        xdt = [sb(f"xdt{u}", [P, NBATCH, HEADS // 2, 2, 2 * HD]) for u in range(2)]
        xd = [sb(f"xd{u}", [P, NBATCH, DIN]) for u in range(2)]
        yg = [sb(f"yg{u}", [P, NBATCH, P]) for u in range(2)]
        ysq = [sb(f"ysq{u}", [P, NBATCH, P]) for u in range(2)]
        var = [sb(f"var{u}", [P, NBATCH]) for u in range(2)]
        rr = [sb(f"rr{u}", [P, NBATCH]) for u in range(2)]
        oc = [sb(f"oc{u}", [P, P]) for u in range(2)]
        on = [sb(f"on{u}", [P, P]) for u in range(2)]
        xsq = [sb(f"xsq{u}", [P, P]) for u in range(2)]

        x_in = sb("x_in", [P, NPAIR, NBATCH, C])
        stat = sb("stat", [P, NPAIR * NBATCH])
        stat2 = sb("stat2", [P, NPAIR * NBATCH])

        s_ld = sem("x_loaded")
        s_wld = sem("weights_loaded")
        s_const = sem("constants_made")
        s_wd = sem("weights_made")
        s_bld = sem("bias_rows_placed")
        s_ln = sem("norm_step")
        s_tp = sem("norm_transposed")
        s_x0 = sem("x0_ready")

        win_raw = z_all[:].rearrange("p a b c -> p (a b c)")[:, 0:2 * NL * PROJ].rearrange(
            "p (s l n) -> p s l n", s=2, l=NL)
        cw_raw = em[0][:].rearrange("p a b c -> p (a b c)")[:, 0:2 * NL * CONVD].rearrange(
            "p (s l n) -> p s l n", s=2, l=NL)
        cw_raw2 = em[1][:].rearrange("p a b c -> p (a b c)")[:, 0:2 * NL * CONVD].rearrange(
            "p (s l n) -> p s l n", s=2, l=NL)
        wout_raw = rstd[:, 0:2 * NL * C].rearrange("p (s l n) -> p s l n", s=2, l=NL)
        small = sb("small", [P, 2, NL, 2])
        hd_raw = sb("hd_raw", [P, 2, NL, 2, HEADS])
        cb_raw = sb("cb_raw", [2 * NL * CONVD // 16, 16])
        cb_rest = sb("cb_rest", [2 * NL * CONVD // 16, 16])
        cb_part = sb("cb_part", [2 * NL * CONVD // 16, NPART, 16], BF16)
        CBROWS = NL * CONVD // 16

        names = ("t", "b")
        N_WDMA = 28
        WD_CB = 4
        WD_ALL = 34
        N_CONST = 54
        LN_STEPS = 8
        MIX_STEPS = 28
        s_ea = sem("exp_a_log")

        s_sq, s_ms, s_lnv, s_rstd, s_h = (sem(n) for n in (
            "squares", "mean_squares", "log_var", "rstd_ready", "h_ready"))
        s_dtf, s_dtt = sem("dt_copied"), sem("dt_transposed")
        s_xs, s_mx, s_mc = (sem(n) for n in ("x_squared", "x_mean_square", "mean_square_copied"))
        s_dtp, s_v, s_abs, s_e, s_l, s_dt, s_dta, s_cum = (sem(n) for n in (
            "dt_projected", "dt_biased", "dt_abs", "dt_exp", "dt_log1p", "dt_ready", "dta_ready", "cum_ready"))
        s_hi, s_rest, s_mid, s_lo, s_pt, s_ct = (sem(n) for n in (
            "cum_hi", "cum_rest", "cum_mid", "cum_lo", "parts_transposed", "cum_t_ready"))
        s_wcur = sem("current_weights")
        s_st = [sem("slot0_staged"), sem("slot1_staged")]
        s_tg = [sem("target0_staged"), sem("target1_staged")]
        s_proj, s_zp, s_th, s_thz, s_xbc, s_z, s_bt, s_btc, s_g, s_gm = (sem(n) for n in (
            "projected", "z_projected", "tanh_done", "tanh_z_done", "xbc_ready", "z_ready", "bc_transposed",
            "bc_copied", "g_ready", "gm_ready"))
        s_seg, s_exp, s_m, s_xdt, s_xd, s_y, s_yg = (sem(n) for n in (
            "seg_ready", "exp_done", "m_ready", "xdt_ready", "xd_ready", "y_ready", "y_gated"))
        s_ysq, s_o, s_oc, s_ss, s_var, s_rr, s_rb, s_on, s_x = (sem(n) for n in (
            "y_squared", "o_ready", "o_copied", "ss_ready", "var_ready", "r_ready", "r_spread", "o_normed", "x_updated"))

        w1s = em[0][:].rearrange("p a b c -> p (a b c)").rearrange("p (e h) -> p e h", e=E)
        w2s = em[1][:].rearrange("p a b c -> p (a b c)").rearrange("p (e h) -> p e h", e=E)
        w3s = h_pad[0][:].rearrange("p j v -> p (j v)")[:, 0:E * C].rearrange("p (e c) -> p e c", e=E)
        xq = rstd[:, 0:CK]
        zflat = z_all[:].rearrange("p a b c -> p (a b c)")
        sil, act_h = ([zflat[:, CK * (2 * k + b):CK * (2 * k + b + 1)] for b in range(NBATCH)] for k in range(2))
        hidden = [[zflat[:, CK * (4 + 2 * k + b):CK * (5 + 2 * k + b)] for b in range(NBATCH)] for k in range(2)]
        moe = sq[:, 0:CK]
        gate_w = sb("gate_w", [P, NBATCH, E])
        gate_b = sb("gate_b", [P, E])
        rank = sb("rank", [P, E])
        NT2 = NPAIR * NBATCH
        hb = h_pad[1][:].rearrange("p j v -> p (j v)")
        prob, hot1, hot2, work = (hb[:, NT2 * E * i:NT2 * E * (i + 1)].rearrange("p (t e) -> p t e", e=E)
                                  for i in range(4))
        mix = sb("mix", [P, NPAIR, NBATCH, E])
        top = [sb(f"top{i}", [P, NT2]) for i in range(4)]
        s_out = sem("out_stored")
        s_ew = sem("expert_weights_loaded")
        s_bt2, s_x1, s_gate, s_mix, s_prob = (sem(n) for n in (
            "conv_transposed", "x1_ready", "gate_ready", "mix_step", "prob_exp"))
        s_sel, s_gt, s_gc = (sem(n) for n in ("selectors_made", "mix_transposed", "mix_rows_copied"))
        s_xq, s_h12, s_gb, s_sil, s_u, s_hid, s_eo, s_oc2, s_ot, s_acc = (sem(n) for n in (
            "xq_ready", "h12_ready", "mix_spread", "silu_done", "silu_times_h2", "hidden_ready", "expert_out",
            "sum_copied", "sum_transposed", "accumulated"))
        NSTEP = NBATCH * E

        def hcols(s, j):
            return h_pad[s][:].rearrange("p j v -> p (j v)")[:, bass.ds(j * wide[s], wide[s])]

        def part(r):
            return parts[:, :, BH * r:BH * (r + 1)]

        def lhs(s, ap, first):
            return ap[:, QS[s] * first:QS[s] * first + P]

        def x_tokens(s, j, n):
            if s == 0:
                return x_io[0][:].rearrange("p (t v) -> p t v", v=P)[:, bass.ds(j, n), :]
            v = x_io[1][:].rearrange("p (v t q) -> p t v q", v=BANDS, q=QS[1])
            return v[:, bass.ds(j, n), :, :]

        def of_tile(ap):
            return ap.rearrange("p (a q) -> p a q", q=QS[1])

        def x_out(s, j):
            v = x_io[1 - s][:, bass.ds(P * j, P)]
            return of_tile(v) if s == 0 else v.rearrange("p (q v) -> p v q", v=SEQ[1])

        def ms_out(s, j):
            if s == 0:
                return rstd[:].rearrange("p (t w) -> p t w", w=P)[:, :, bass.ds(QS[1] * j, QS[1])]
            return rstd[:, bass.ds(P * j, P)].rearrange("p (q v) -> p v q", v=SEQ[1])

        def ms_done(g):
            return NCK + NPAIR * g

        def in_tiles(s, ap):
            if s == 0:
                return ap.rearrange("p (t v) -> p t v", v=P)
            return ap.rearrange("p (t v q) -> p t v q", v=BANDS, q=QS[1])

        block = ctx.enter_context(nc.Block())

        @block.sync
        def _(sp):
            for b in range(NBATCH):
                sp.dma_start(x_in[:, :, b, :], a["x"][b].rearrange("t k c -> (t k) c").rearrange(
                    "(j p) c -> p j c", p=P)).then_inc(s_ld, 16)
            for s, nm in enumerate(names):
                for d in range(2):
                    rows = slice(C * d, C * d + C)
                    sp.dma_start(win_raw[rows, s], a[f"{nm}_Win"].rearrange("l c n -> c l n")).then_inc(s_wld, 16)
                    sp.dma_start(small[rows, s, :, 0:1], a[f"{nm}_norm"].rearrange("l (c o) -> c l o", o=1),
                                 allow_slow_non_contiguous=True).then_inc(s_wld, 16)
                    sp.dma_start(cw_raw[rows, s], a[f"{nm}_cw"][:, d, :].partition_broadcast(C)).then_inc(s_wld, 16)
                    sp.dma_start(cw_raw2[rows, s], a[f"{nm}_cw"][:, 2 + d, :].partition_broadcast(C)).then_inc(s_wld, 16)
                sp.dma_start(small[:, s, :, 1:2], a[f"{nm}_gn"].rearrange("l (c o) -> c l o", o=1),
                                 allow_slow_non_contiguous=True).then_inc(s_wld, 16)
                sp.dma_start(wout_raw[:, s], a[f"{nm}_Wout"].rearrange("l c n -> c l n")).then_inc(s_wld, 16)
                sp.dma_start(hd_raw[:, s, :, 0, :], a[f"{nm}_D"].partition_broadcast(P)).then_inc(s_wld, 16)
                sp.dma_start(hd_raw[:, s, :, 1, :], a[f"{nm}_Alog"].partition_broadcast(P)).then_inc(s_wld, 16)
                sp.dma_start(wall[:, 0:NL, s, W_DTB:W_DTB + HEADS], a[f"{nm}_dtb"].partition_broadcast(P)).then_inc(s_wld, 16)
                sp.dma_start(cb_raw[CBROWS * s:CBROWS * (s + 1), :],
                             a[f"{nm}_cb"].rearrange("l n -> (l n)").rearrange("(p f) -> p f", f=16)).then_inc(s_wld, 16)
            sp.wait_ge(s_wd, WD_CB)
            sp.wait_ge(s_const, N_CONST)
            for r in range(NPART):
                for s in range(2):
                    sp.dma_start(ball[r:r + 1, s, 0:NL, :].rearrange("o l n -> o (l n)").rearrange(
                        "o (p f) -> o p f", f=16), cb_part[CBROWS * s:CBROWS * (s + 1), r, :]).then_inc(s_bld, 16)

            def weights_in(s, layer):
                sp.dma_start(wcur[s][:], wall[:, bass.ds(layer, 1), s, :].rearrange("p l n -> p (l n)")
                             ).then_inc(s_wcur, 16)
                sp.dma_start(bcur[s][:], ball[:, s, bass.ds(layer, 1), :].rearrange("p l n -> p (l n)")
                             ).then_inc(s_wcur, 16)

            sp.wait_ge(s_wd, WD_ALL)
            sp.wait_ge(s_bld, 16 * 2 * NPART)
            weights_in(0, 0)

            with sp.Fori(0, n_layers) as layer:
                for s in range(2):
                    g = 2 * layer + s

                    def stage_in(m, u, first):
                        j = 2 * m + u
                        if not first:
                            sp.wait_ge(s_h, NCK * (g + 1))
                            sp.wait_ge(s_zp, NPAIR * g + j - 1)
                        for b in range(2):
                            src = hcols(s, j)[C * b:C * b + C, :]
                            sp.dma_start(slot[s][u][b][0:C, :], src).then_inc(s_st[u], 16)
                            sp.dma_start(slot[s][u][b][C:P, 0:wide[s] - QS[s]], src[:, QS[s]:wide[s]]).then_inc(s_st[u], 16)

                    def target_in(m, u, first):
                        j = 2 * m + u
                        if first and u == 0:
                            sp.wait_ge(s_ct, 2 * g + 2)
                        if not first:
                            sp.wait_ge(s_seg, 4 * (NPAIR * g + j - 1))
                        for r in range(NPART):
                            sp.dma_start(target[u][R_ONE + r:R_ONE + r + 1, :, :],
                                         cum_t[BH * r:BH * (r + 1), bass.ds(j, 1), :].rearrange("h o t -> h (o t)")
                                         ).then_inc(s_tg[u], 16)

                    sp.wait_ge(s_h, NCK * g + 1)
                    stage_in(0, 0, True)
                    stage_in(0, 1, True)
                    target_in(0, 0, True)
                    target_in(0, 1, True)
                    sp.wait_ge(s_xd, NPAIR * g + 1)
                    weights_in(1 - s, layer + s)
                    with sp.Fori(1, NPAIR // 2) as m:
                        for u in range(2):
                            stage_in(m, u, False)
                            target_in(m, u, False)

            sp.wait_ge(s_x, NPAIR * 2 * n_layers)
            sp.wait_ge(s_y, NPAIR * 2 * n_layers)
            for b in range(2):
                rows = slice(C * b, C * b + C)
                sp.dma_start(w1s[rows], a["w1"].rearrange("e c h -> c e h")).then_inc(s_ew, 16)
                sp.dma_start(w2s[rows], a["w2"].rearrange("e c h -> c e h")).then_inc(s_ew, 16)
                sp.dma_start(gate_w[rows, b, :], a["gate_w"]).then_inc(s_ew, 16)
            sp.dma_start(w3s, a["w3"].rearrange("e h c -> h e c")).then_inc(s_ew, 16)
            sp.dma_start(gate_b[:], a["gate_b"].partition_broadcast(P)).then_inc(s_ew, 16)

            with sp.Fori(0, NCK) as q:
                for b in range(NBATCH):
                    sp.wait_ge(s_acc, q + 1)
                    sp.dma_start(out[b].rearrange("t k c -> (t k) c").rearrange("(j p) c -> p j c", p=P)[
                        :, bass.ds(4 * q, 4), :], x_in[:, bass.ds(4 * q, 4), b, :]).then_inc(s_out, 16)
            sp.wait_ge(s_out, 16 * NBATCH * NCK)

        @block.gpsimd
        def _(pool):
            made = [0]

            def const(ins):
                made[0] += 1
                ins.then_inc(s_const, 1)
                pool.wait_ge(s_const, made[0])

            const(pool.memset(ident[:], 0.0))
            const(pool.affine_select(out=ident[:], in_=ident[:], compare_op=ALU.not_equal, fill=1.0, base=0,
                                     pattern=[[-1, P]], channel_multiplier=1))
            const(pool.tensor_copy(identb[:], ident[:]))
            const(pool.memset(tri[0][:], 1.0))
            const(pool.memset(tri[1][:], 0.0))
            v = tri[1][:].rearrange("p (v q) -> p v q", q=QS[1])
            for k in range(SEQ[1]):
                const(pool.affine_select(out=v, in_=v, compare_op=ALU.not_equal, fill=1.0, base=-QS[1] * k,
                                         pattern=[[0, SEQ[1]], [-1, QS[1]]], channel_multiplier=1))
            for s in range(2):
                const(pool.affine_select(out=tri[s][:], in_=tri[s][:], compare_op=ALU.is_ge, fill=0.0, base=0,
                                         pattern=[[1, P]], channel_multiplier=-1))
            const(pool.memset(mean64[:], 0.0))
            for b in range(2):
                const(pool.memset(mean64[C * b:C * b + C, C * b:C * b + C], 1.0 / C))
            const(pool.memset(ones3[:], 0.0))
            const(pool.memset(ones3[0:NPART, :], 1.0))
            for u in range(2):
                const(pool.memset(target[u][:], 0.0))
                v = target[u][0:R_TOP]
                for r in range(NPART):
                    const(pool.affine_select(out=v, in_=v, compare_op=ALU.not_equal, fill=-1.0, base=-BH * r,
                                             pattern=[[-1, BH], [0, P]], channel_multiplier=1))
                v = target[u][R_BLK:P].rearrange("p h (k t) -> p h k t", k=NBLK)
                const(pool.affine_select(out=v, in_=v, compare_op=ALU.is_ge, fill=FAR, base=0,
                                         pattern=[[0, BH], [1, NBLK], [0, P // NBLK]], channel_multiplier=-1))
            const(pool.memset(cum_t[:], 0.0))
            v = cum_t[R_BLK:P].rearrange("p h (k t) -> p h k t", k=NBLK)
            const(pool.affine_select(out=v, in_=v, compare_op=ALU.not_equal, fill=1.0, base=0,
                                     pattern=[[0, NPAIR], [-1, NBLK], [0, P // NBLK]], channel_multiplier=1))
            const(pool.memset(eps6[:], 1e-6))
            const(pool.memset(eps5[:], 1e-5))
            const(pool.memset(mhalf[:], -0.5))
            const(pool.memset(ones1[:], 1.0))
            for u in range(2):
                const(pool.memset(xdt[u][:], 0.0))
            const(pool.memset(ball[:], 0.0))
            const(pool.memset(wall[:, NL, 0, :], 0.0))
            const(pool.memset(parts[:], 0.0))
            const(pool.memset(parts[:, :, R_ONE:R_ONE + NPART], 1.0))
            for s in range(2):
                const(pool.memset(h_pad[s][:], 0.0))
            const(pool.memset(gate_w[:], 0.0))
            const(pool.iota(rank[:], pattern=[[-1, E]], base=E, channel_multiplier=0,
                            allow_small_or_imprecise_dtypes=True))
            assert made[0] == N_CONST

            with pool.Fori(0, n_layers) as layer:
                for s in range(2):
                    g = 2 * layer + s

                    pool.wait_ge(s_wcur, 32 * (g + 1))
                    pool.wait_ge(s_dt, 2 * g + 2)

                    def x_dt(m, u, first):
                        j, n = 2 * m + u, NPAIR * g + 2 * m + u
                        pool.wait_ge(s_xbc, n + 1)
                        if not first:
                            pool.wait_ge(s_y, n - 1)
                        for b in range(NBATCH):
                            for r in range(2):
                                ins = pool.tensor_tensor(
                                    out=xdt[u][:, b, :, r, HD * r:HD * (r + 1)],
                                    in0=xbc[u][:, b, 0:DIN].rearrange("p (k r d) -> p k r d", r=2, d=HD)[:, :, r, :],
                                    in1=dt_half[:, bass.ds(BH * j, BH)].rearrange(
                                        "p (b k r) -> p b k r", b=NBATCH, r=2)[:, b, :, r:r + 1]
                                        .to_broadcast([P, HEADS // 2, HD]),
                                    op=ALU.mult)
                        ins.then_inc(s_xdt, 1)
                        pool.tensor_tensor(
                            out=xd[u][:], in0=xbc[u][:, :, 0:DIN],
                            in1=wcur[s][:, W_D:W_D + DIN].rearrange("p (o d) -> p o d", o=1)
                                .to_broadcast([P, NBATCH, DIN]),
                            op=ALU.mult).then_inc(s_xd, 1)

                    def norm(m, u, first):
                        n, j = NPAIR * g + 2 * m + u, 2 * m + u
                        pool.wait_ge(s_var, n + 1)
                        if not first:
                            pool.wait_ge(s_rb, n - 1)
                        pool.tensor_tensor(out=rr[u][:], in0=var[u][:], in1=mhalf[:], op=ALU.pow).then_inc(s_rr, 1)

                    def add_x(m, u):
                        n, j = NPAIR * g + 2 * m + u, 2 * m + u
                        pool.wait_ge(s_on, n + 1)
                        o = x_io[1 - s][:].rearrange("p (t v) -> p t v", v=P)[:, bass.ds(j, 1), :]
                        if s == 1:
                            o = o.rearrange("p t (q v) -> p t v q", v=SEQ[1])
                        pool.tensor_tensor(out=o, in0=in_tiles(s, on[u][:]), in1=x_tokens(s, j, 1),
                                           op=ALU.add).then_inc(s_x, 1)

                    def step(m, u, j=None):
                        if j is None or j >= 2:
                            norm(m - 1, u, j is not None and j - 2 < 2)
                        if j is None or j + 1 < NPAIR:
                            x_dt(m + (u + 1) // 2, (u + 1) % 2, j is not None and j + 1 < 2)
                        if j is None or j >= 2:
                            add_x(m - 1, u)

                    for j in range(-1, 4):
                        step(j // 2, j % 2, j)
                    with pool.Fori(2, NPAIR // 2 - 1) as m:
                        step(m, 0)
                        step(m, 1)
                    for j in range(NPAIR - 2, NPAIR + 2):
                        step(j // 2, j % 2, j)

            pool.wait_ge(s_seg, 4 * NPAIR * 2 * n_layers)
            made_sel = [0]

            def select(ins):
                made_sel[0] += 1
                ins.then_inc(s_sel, 1)
                pool.wait_ge(s_sel, made_sel[0])

            for b in range(NBATCH):
                select(pool.memset(target[b][:], 0.0))
                for r in range(NPART):
                    v = target[b][QUAD * r:QUAD * (r + 1)]
                    select(pool.affine_select(out=v, in_=v, compare_op=ALU.not_equal, fill=1.0, base=-E * b,
                                              pattern=[[-1, E], [0, P]], channel_multiplier=1))

        @block.tensor
        def _(pe):
            pe.wait_ge(s_const, N_CONST)

            def to_features(done, tiles, count):
                for j in range(NPAIR):
                    t = pe.transpose(bank[j // 4][:, P * (j % 4):P * (j % 4) + P], tiles(j), ident[:])
                    if j % 4 == 3:
                        t.then_inc(done, 1)

            pe.wait_ge(s_ln, LN_STEPS)
            to_features(s_tp, lambda j: sq[:, P * j:P * j + P], 0)

            for c in range(NCK):
                pe.wait_ge(s_sq, c + 1)
                pe.matmul(bank[c][:], mean64[:], sq[:, CK * c:CK * (c + 1)],
                          start=True, stop=True).then_inc(s_ms, 1)

            with pe.Fori(0, n_layers) as layer:
                for s in range(2):
                    g = 2 * layer + s
                    w = wcur[s]

                    pe.wait_ge(s_wcur, 32 * (g + 1))
                    pe.wait_ge(s_h, NCK * (g + 1))
                    for c in range(NCK):
                        mm = pe.matmul(bank[4][QUAD * c:QUAD * (c + 1), :], w[:, W_DT:W_DT + QUAD],
                                       h_pad[s][:, 4 * c:4 * (c + 1), wide[s] - P:], start=True, stop=True)
                    mm.then_inc(s_dtp, 1)
                    pe.wait_ge(s_dtf, g + 1)
                    for t in range(4):
                        tr = pe.transpose(bank[4][:, P * t:P * (t + 1)], dtf[:, P * t:P * (t + 1)], ident[:])
                    tr.then_inc(s_dtt, 1)

                    def project(m, u, first):
                        n = NPAIR * g + 2 * m + u
                        pe.wait_ge(s_st[u], 64 * ((NPAIR // 2) * g + m + 1))
                        if not first:
                            pe.wait_ge(s_gm, n)
                        for b in range(2):
                            src = slot[s][u][b][:]
                            o = bank[0][:, CONVD * b:CONVD * (b + 1)]
                            pe.matmul(o, ones3[:], bcur[s][:], start=True, stop=False, skip_group_check=True)
                            pe.matmul(o, lhs(s, src, 0), w[:, W_C0:W_C0 + CONVD], start=False,
                                      stop=False, skip_group_check=True)
                            mm = pe.matmul(o, lhs(s, src, 2), w[:, W_C1:W_C1 + CONVD],
                                           start=False, stop=True, skip_group_check=True)
                        mm.then_inc(s_proj, 1)

                    def project_z(m, u, first):
                        n = NPAIR * g + 2 * m + u
                        if not first:
                            pe.wait_ge(s_z, n)
                        for b in range(2):
                            mm = pe.matmul(bank[1][:, P * b:P * (b + 1)], w[C:P, W_Z:W_Z + DIN],
                                           lhs(s, slot[s][u][b][C:P], 2), start=True, stop=True)
                        mm.then_inc(s_zp, 1)

                    def turn_bc(m, u, first):
                        n = NPAIR * g + 2 * m + u
                        pe.wait_ge(s_xbc, n + 1)
                        if not first:
                            pe.wait_ge(s_gm, n)
                        for k in range(2):
                            for b in range(2):
                                row = QUAD * (2 * k + b)
                                t = pe.matmul(bank[4][row:row + NST, 0:P],
                                              xbc[u][:, b, DIN + NST * k:DIN + NST * (k + 1)], ident[:],
                                              start=True, stop=True)
                        t.then_inc(s_bt, 1)

                    def b_dot_c(m, u):
                        pe.wait_ge(s_btc, 2 * (NPAIR * g + 2 * m + u) + 2)
                        for b in range(2):
                            rows = slice(QUAD * b, QUAD * b + NST)
                            mm = pe.matmul(bank[(4, 0)[b]][:, G_COL:G_COL + P], bt[u][rows, :], ct[u][rows, :],
                                           start=True, stop=True)
                        mm.then_inc(s_g, 1)

                    def decays(m, u, q, first):
                        n = NPAIR * g + 2 * m + u
                        b, hh = q // 2, q % 2
                        if q == 0:
                            pe.wait_ge(s_tg[u], 16 * NPART * ((NPAIR // 2) * g + m + 1))
                        if not first:
                            pe.wait_ge(s_exp, 4 * n + q - 1)
                        tile = cum_t[:, bass.ds(2 * m + u, 1), :].rearrange("p o t -> p (o t)")
                        h0 = HEADS * b + 4 * hh
                        pe.matmul(bank[2 + hh][:], tile, target[u][:, h0:h0 + 4, :].rearrange("p h t -> p (h t)"),
                                  start=True, stop=True).then_inc(s_seg, 1)

                    def mix_states(m, u, first, second):
                        n = NPAIR * g + 2 * m + u
                        pe.wait_ge(s_xd, n + 1)
                        if not first:
                            pe.wait_ge(s_yg, n)
                        if second:
                            pe.wait_ge(s_mc, NCK + n - 2)
                        for b in range(2):
                            pe.matmul(bank[5][:, P * b:P * (b + 1)], xd[u][:, b, :], ident[:], start=True,
                                      stop=False, skip_group_check=True)
                            pe.wait_ge(s_m, 4 * n + 2 * b + 2)
                            for r in range(2):
                                for k in range(HEADS // 2):
                                    mm = pe.matmul(bank[5][QUAD * k:QUAD * (k + 1), P * b:P * (b + 1)],
                                                   xdt[u][:, b, k, r, :], em[u][:, b, 2 * k + r, :],
                                                   start=False, stop=(r == 1), skip_group_check=True)
                        mm.then_inc(s_y, 1)

                    def project_out(m, u, first):
                        n = NPAIR * g + 2 * m + u
                        pe.wait_ge(s_yg, n + 1)
                        if not first:
                            pe.wait_ge(s_oc, n)
                        for b in range(2):
                            mm = pe.matmul(bank[6][C * b:C * (b + 1), 0:P], w[:, W_OUT:W_OUT + C], yg[u][:, b, :],
                                           start=True, stop=True)
                        mm.then_inc(s_o, 1)
                        pe.wait_ge(s_ysq, n + 1)
                        if not first:
                            pe.wait_ge(s_on, n)
                        for b in range(2):
                            mm = pe.matmul(bank[7][:, b:b + 1], ysq[u][:, b, :], ones1[:], start=True, stop=True)
                        mm.then_inc(s_ss, 1)

                    def spread_r(m, u):
                        pe.wait_ge(s_rr, NPAIR * g + 2 * m + u + 1)
                        for b in range(2):
                            mm = pe.matmul(bank[7][C * b:C * (b + 1), P:2 * P], rr[u][:, b:b + 1].to_broadcast([P, C]),
                                           ident[:], start=True, stop=True)
                        mm.then_inc(s_rb, 1)

                    def mean_x(m, u, y_read):
                        n = NPAIR * g + 2 * m + u
                        pe.wait_ge(s_xs, n + 1)
                        if y_read:
                            pe.wait_ge(s_yg, n + 3)
                        pe.matmul(bank[5][:, 2 * P:3 * P], mean64[:], xsq[u][:], start=True,
                                  stop=True).then_inc(s_mx, 1)

                    def step(m, u, j=None):
                        nxt = (m + (u + 1) // 2, (u + 1) % 2)
                        prv = (m + (u - 1) // 2, (u - 1) % 2)
                        pr2 = (m - 1, u)
                        has_next = j is None or j + 1 < NPAIR
                        here = j is None or 0 <= j < NPAIR
                        pr3 = (m + (u - 3) // 2, (u - 1) % 2)
                        if has_next and j == 0:
                            project(*nxt, False)
                        if here:
                            decays(m, u, 0, j == 0)
                            decays(m, u, 1, j == 0)
                        if j is None or 2 <= j <= NPAIR + 1:
                            project_out(*pr2, j is not None and j - 2 < 1)
                        if has_next and j != 0:
                            project(*nxt, False)
                        if here:
                            decays(m, u, 2, False)
                            decays(m, u, 3, False)
                        if j is None or 1 <= j <= NPAIR:
                            mix_states(*prv, j is not None and j - 1 < 1, j is None or j >= 4)
                        if has_next:
                            turn_bc(*nxt, False)
                            project_z(*nxt, False)
                        if j is None or 2 <= j <= NPAIR + 1:
                            spread_r(*pr2)
                        if has_next:
                            b_dot_c(*nxt)
                        if j is None or j >= 3:
                            mean_x(*pr3, j is None or j <= NPAIR)

                    project(0, 0, True)
                    project_z(0, 0, True)
                    pe.wait_ge(s_dta, g + 1)
                    pe.matmul(bank[5][:, 0:NPAIR * BH], tri[s][:], dta_log[:],
                              start=True, stop=True).then_inc(s_cum, 1)
                    pe.wait_ge(s_lo, g + 1)
                    for i in range(2):
                        ptb = bank[6 + i][:].bitcast(BF16)
                        for k in range(NPAIR // 2):
                            t = pe.transpose(ptb[0:R_TOP, P * k:P * (k + 1)], parts[:, NPAIR // 2 * i + k, :],
                                             identb[:])
                        t.then_inc(s_pt, 1)
                    turn_bc(0, 0, True)
                    b_dot_c(0, 0)
                    for j in range(6):
                        step(j // 2, j % 2, j)
                    with pe.Fori(3, NPAIR // 2 - 1) as m:
                        step(m, 0)
                        step(m, 1)
                    for j in range(NPAIR - 2, NPAIR + 3):
                        step(j // 2, j % 2, j)

            pe.wait_ge(s_x, NPAIR * 2 * n_layers)
            to_features(s_bt2, lambda j: x_io[0][:, P * j:P * j + P], 0)
            pe.wait_ge(s_x1, NCK)
            pe.wait_ge(s_ln, 2 * LN_STEPS)
            to_features(s_tp, lambda j: sq[:, P * j:P * j + P], 1)
            pe.wait_ge(s_ew, 16 * 8)
            for j in range(NPAIR):
                if j % 4 == 0:
                    pe.wait_ge(s_x0, NCK + j // 4 + 1)
                mm = pe.matmul(bank[4][:, NBATCH * E * j:NBATCH * E * (j + 1)], x_io[1][:, P * j:P * j + P],
                               gate_w[:].rearrange("p b e -> p (b e)"), start=True, stop=True)
            mm.then_inc(s_gate, 1)

            pe.wait_ge(s_mix, MIX_STEPS)
            for i in range(2):
                ptb = bank[6 + i][:].bitcast(BF16)
                for k in range(NPAIR // 2):
                    t = pe.transpose(ptb[0:NPART * QUAD, P * k:P * (k + 1)], parts[:, NPAIR // 2 * i + k, :], identb[:])
                t.then_inc(s_gt, 1)
            pe.wait_ge(s_gc, 2)
            pe.wait_ge(s_sel, NBATCH * (1 + NPART))
            with pe.Fori(0, NCK) as q:
                def expert_in(e, b):
                    if e >= 1:
                        pe.wait_ge(s_hid, NSTEP * q + 2 * e + b - 1)
                    rows = slice(C * b, C * b + C)
                    pe.matmul(bank[2 * b][:], w1s[rows, e, :], xq[rows, :], start=True, stop=True)
                    pe.matmul(bank[2 * b + 1][:], w2s[rows, e, :], xq[rows, :],
                              start=True, stop=True).then_inc(s_h12, 1)
                    pe.matmul(bank[4 + b][:], target[b][0:NPART * QUAD, e, :],
                              cum_t[0:NPART * QUAD, bass.ds(4 * q, 4), :].rearrange("k j t -> k (j t)"),
                              start=True, stop=True).then_inc(s_gb, 1)

                def expert_out(e):
                    pe.wait_ge(s_hid, NSTEP * q + 2 * e + 2)
                    if e == 0:
                        pe.wait_ge(s_oc2, q)
                    for b in range(NBATCH):
                        mm = pe.matmul(bank[6][C * b:C * (b + 1), :], w3s[:, e, :], hidden[e % 2][b],
                                       start=(e == 0), stop=(e == E - 1), skip_group_check=True)
                    mm.then_inc(s_eo, 1)

                pe.wait_ge(s_xq, q + 1)
                for e in range(E + 1):
                    if e < E:
                        for b in range(NBATCH):
                            expert_in(e, b)
                    if e >= 1:
                        expert_out(e - 1)
                pe.wait_ge(s_oc2, q + 1)
                pe.wait_ge(s_acc, q)
                for t in range(4):
                    tr = pe.transpose(bank[7][:, P * t:P * (t + 1)], moe[:, P * t:P * (t + 1)], ident[:])
                tr.then_inc(s_ot, 1)

        @block.scalar
        def _(act):
            def norm_scalar(k, eps):
                act.wait_ge(s_ln, LN_STEPS * k + 3)
                act.activation(x_io[1][:], sq[:], ACT.Square).then_inc(s_ln, 1)
                act.wait_ge(s_ln, LN_STEPS * k + 5)
                act.activation(stat2[:], stat2[:], ACT.Ln, bias=eps[:], scale=1.0 / C).then_inc(s_ln, 1)
                act.wait_ge(s_ln, LN_STEPS * k + 6)
                act.activation(stat2[:], stat2[:], ACT.Exp, scale=-0.5).then_inc(s_ln, 1)

            act.preload_act_table_set("natural_log_exp_and_others")
            act.wait_ge(s_const, N_CONST)
            act.wait_ge(s_wld, 16 * N_WDMA)
            act.activation(hd_raw[:, :, :, 1, :], hd_raw[:, :, :, 1, :], ACT.Exp).then_inc(s_ea, 1)
            norm_scalar(0, eps6)

            act.wait_ge(s_x0, NCK)
            for c in range(NCK):
                act.activation(sq[:, CK * c:CK * (c + 1)], x_io[0][:, CK * c:CK * (c + 1)],
                               ACT.Square).then_inc(s_sq, 1)
            for c in range(NCK):
                act.wait_ge(s_ms, c + 1)
                act.activation(rstd[:, CK * c:CK * (c + 1)], bank[c][:], ACT.Copy).then_inc(s_mc, 1)

            with act.Fori(0, n_layers) as layer:
                for s in range(2):
                    g = 2 * layer + s
                    act.preload_act_table_set("natural_log_exp_and_others")
                    act.wait_ge(s_mc, ms_done(g))
                    for c in range(NCK):
                        r = rstd[:, CK * c:CK * (c + 1)]
                        act.activation(r, r, ACT.Ln, bias=eps6[:]).then_inc(s_lnv, 1)
                        act.wait_ge(s_lnv, NCK * g + c + 1)
                        act.activation(r, r, ACT.Exp, scale=-0.5).then_inc(s_rstd, 1)
                    act.wait_ge(s_dtp, g + 1)
                    act.activation(dtf[:], bank[4][:], ACT.Copy).then_inc(s_dtf, 1)
                    act.wait_ge(s_v, g + 1)
                    act.activation(dta[:], dtv[:], ACT.Abs).then_inc(s_abs, 1)
                    act.wait_ge(s_abs, g + 1)
                    act.activation(dta[:], dta[:], ACT.Exp, scale=-1.0).then_inc(s_e, 1)
                    act.wait_ge(s_e, g + 1)
                    act.activation(dta[:], dta[:], ACT.Ln, bias=1.0).then_inc(s_l, 1)
                    act.preload_act_table_set("exp_and_others")
                    def tanh(m, u, first):
                        n = NPAIR * g + 2 * m + u
                        act.wait_ge(s_proj, n + 1)
                        if not first:
                            act.wait_ge(s_xbc, n)
                        act.activation(th[:].rearrange("p b c -> p (b c)"), bank[0][:, 0:NBATCH * CONVD], ACT.Tanh,
                                       scale=0.5).then_inc(s_th, 1)

                    def tanh_z(m, u, first):
                        n = NPAIR * g + 2 * m + u
                        act.wait_ge(s_zp, n + 1)
                        if not first:
                            act.wait_ge(s_z, n)
                        act.activation(thz[:].rearrange("p b c -> p (b c)"), bank[1][:, 0:NBATCH * P], ACT.Tanh,
                                       scale=0.5).then_inc(s_thz, 1)

                    def copy_bc(m, u):
                        act.wait_ge(s_bt, NPAIR * g + 2 * m + u + 1)
                        act.activation(bt[u][:], bank[4][0:2 * QUAD, 0:P], ACT.Copy).then_inc(s_btc, 1)
                        act.activation(ct[u][:], bank[4][2 * QUAD:P, 0:P], ACT.Copy).then_inc(s_btc, 1)

                    def exps(m, u, q, first):
                        n = NPAIR * g + 2 * m + u
                        act.wait_ge(s_seg, 4 * n + q + 1)
                        if not first:
                            act.wait_ge(s_y, n - 1)
                        act.activation(em[u][:, q // 2, 4 * (q % 2):4 * (q % 2) + 4, :].rearrange("p h t -> p (h t)"),
                                       bank[2 + q % 2][:], ACT.Exp).then_inc(s_exp, 1)

                    def squares(m, u, first):
                        n = NPAIR * g + 2 * m + u
                        act.wait_ge(s_yg, n + 1)
                        if not first:
                            act.wait_ge(s_ss, n - 1)
                        act.activation(ysq[u][:], yg[u][:], ACT.Square, scale=0.5 * DIN ** -0.5).then_inc(s_ysq, 1)

                    def add_eps(m, u, first):
                        n = NPAIR * g + 2 * m + u
                        act.wait_ge(s_o, n + 1)
                        if not first:
                            act.wait_ge(s_on, n - 1)
                        act.activation(oc[u][:], bank[6][:, 0:P], ACT.Copy).then_inc(s_oc, 1)
                        act.wait_ge(s_ss, n + 1)
                        if not first:
                            act.wait_ge(s_rr, n - 1)
                        act.activation(var[u][:], bank[7][:, 0:NBATCH], ACT.Identity, bias=eps6[:]).then_inc(s_var, 1)

                    def square_x(m, u, first):
                        n, j = NPAIR * g + 2 * m + u, 2 * m + u
                        act.wait_ge(s_x, n + 1)
                        if not first:
                            act.wait_ge(s_mx, n - 1)
                        act.activation(of_tile(xsq[u][:]), x_out(s, j), ACT.Square).then_inc(s_xs, 1)

                    def copy_mean(m, u):
                        n, j = NPAIR * g + 2 * m + u, 2 * m + u
                        act.wait_ge(s_mx, n + 1)
                        act.activation(ms_out(s, j), of_tile(bank[5][:, 2 * P:3 * P]), ACT.Copy).then_inc(s_mc, 1)

                    def step(m, u, j=None):
                        nxt = (m + (u + 1) // 2, (u + 1) % 2)
                        prv = (m + (u - 1) // 2, (u - 1) % 2)
                        pr2 = (m - 1, u)
                        has_next = j is None or j + 1 < NPAIR
                        here = j is None or 0 <= j < NPAIR
                        pr3 = (m + (u - 3) // 2, (u - 1) % 2)
                        if j == 0:
                            tanh(*nxt, False)
                        if here:
                            exps(m, u, 0, j is not None and j < 2)
                            exps(m, u, 1, j is not None and j < 2)
                        if j is None or j >= 4:
                            copy_mean(m + (u - 4) // 2, u)
                        if j is None or 2 <= j <= NPAIR + 1:
                            add_eps(*pr2, j is not None and j - 2 < 2)
                        if has_next and j != 0:
                            tanh(*nxt, False)
                        if j is None or 3 <= j <= NPAIR + 2:
                            square_x(*pr3, j is not None and j - 3 < 2)
                        if here:
                            exps(m, u, 2, j is not None and j < 2)
                            exps(m, u, 3, j is not None and j < 2)
                        if has_next:
                            copy_bc(*nxt)
                        if j is None or 1 <= j <= NPAIR:
                            squares(*prv, j is not None and j - 1 < 2)
                        if has_next:
                            tanh_z(*nxt, False)

                    tanh(0, 0, True)
                    act.wait_ge(s_cum, g + 1)
                    act.activation(part(0),
                                   bank[5][:, 0:NPAIR * BH].rearrange("p (j k) -> p j k", k=BH),
                                   ACT.Copy).then_inc(s_hi, 1)
                    tanh_z(0, 0, True)
                    act.wait_ge(s_pt, 2 * g + 1)
                    act.activation(cum_t[0:R_TOP, 0:NPAIR // 2, :].rearrange("p j t -> p (j t)"),
                                   bank[6][:].bitcast(BF16)[0:R_TOP, :], ACT.Copy).then_inc(s_ct, 1)
                    copy_bc(0, 0)
                    for j in range(6):
                        step(j // 2, j % 2, j)
                    with act.Fori(3, NPAIR // 2 - 1) as m:
                        step(m, 0)
                        step(m, 1)
                    for j in range(NPAIR - 2, NPAIR + 4):
                        step(j // 2, j % 2, j)

            norm_scalar(1, eps5)
            act.wait_ge(s_mix, 3)
            act.activation(prob, prob, ACT.Exp).then_inc(s_prob, 1)
            act.wait_ge(s_x0, 2 * NCK)
            act.wait_ge(s_gt, 1)
            act.activation(cum_t[0:NPART * QUAD, 0:NPAIR // 2, :].rearrange("p j t -> p (j t)"),
                           bank[6][:].bitcast(BF16)[0:NPART * QUAD, :], ACT.Copy).then_inc(s_gc, 1)
            act.wait_ge(s_gc, 2)
            with act.Fori(0, NCK) as q:
                act.wait_ge(s_hid, NSTEP * q)
                act.activation(xq, x_io[1][:, bass.ds(CK * q, CK)], ACT.Copy).then_inc(s_xq, 1)
                for e in range(E):
                    for b in range(NBATCH):
                        k = NSTEP * q + 2 * e + b
                        act.wait_ge(s_h12, k + 1)
                        if e >= 1:
                            act.wait_ge(s_u, k - 1)
                        act.activation(sil[b], bank[2 * b][:], ACT.Silu).then_inc(s_sil, 1)
                act.wait_ge(s_eo, E * (q + 1))
                act.wait_ge(s_ot, q)
                act.activation(moe, bank[6][:], ACT.Copy).then_inc(s_oc2, 1)

        @block.vector
        def _(dve):
            tm = sq[:].rearrange("p (t c) -> p t c", c=C)
            xi = x_in[:].rearrange("p j b c -> p (j b) c")
            sq2 = x_io[1][:].rearrange("p (t c) -> p t c", c=C)

            def spread(ap, n):
                return ap.rearrange("p (t o) -> p t o", o=1).to_broadcast([P, NPAIR * NBATCH, n])

            def norm_vector(k):
                dve.tensor_reduce(stat[:], xi, AX.X, ALU.add).then_inc(s_ln, 1)
                dve.wait_ge(s_ln, LN_STEPS * k + 1)
                dve.tensor_scalar(stat[:], stat[:], 1.0 / C, None, ALU.mult).then_inc(s_ln, 1)
                dve.wait_ge(s_ln, LN_STEPS * k + 2)
                dve.tensor_tensor(tm, xi, spread(stat[:], C), ALU.subtract).then_inc(s_ln, 1)
                dve.wait_ge(s_ln, LN_STEPS * k + 4)
                dve.tensor_reduce(stat2[:], sq2, AX.X, ALU.add).then_inc(s_ln, 1)
                dve.wait_ge(s_ln, LN_STEPS * k + 7)
                dve.tensor_tensor(tm, tm, spread(stat2[:], C), ALU.mult).then_inc(s_ln, 1)

            def from_banks(k, dst):
                for c in range(NCK):
                    dve.wait_ge(s_tp, NCK * k + c + 1)
                    dve.tensor_copy(dst[:, CK * c:CK * (c + 1)], bank[c][:]).then_inc(s_x0, 1)

            dve.wait_ge(s_const, N_CONST)
            dve.wait_ge(s_wld, 16 * N_WDMA)

            made = [0]

            def link(ins):
                made[0] += 1
                ins.then_inc(s_wd, 1)
                dve.wait_ge(s_wd, made[0])

            link(dve.tensor_copy(cb_part[:, 0, :], cb_raw[:]))
            link(dve.tensor_tensor(cb_rest[:], cb_raw[:], cb_part[:, 0, :], ALU.subtract))
            link(dve.tensor_copy(cb_part[:, 1, :], cb_rest[:]))
            link(dve.tensor_tensor(cb_part[:, 2, :], cb_rest[:], cb_part[:, 1, :], ALU.subtract))
            for s in range(2):
                wn = win_raw[:, s]
                link(dve.tensor_tensor(wn, wn, small[:, s, :, 0:1].to_broadcast([P, NL, PROJ]), ALU.mult))
                link(dve.tensor_tensor(wall[:, 0:NL, s, W_C0:W_C0 + CONVD], wn[:, :, DIN:DIN + CONVD], cw_raw[:, s],
                                       ALU.mult))
                link(dve.tensor_tensor(wall[:, 0:NL, s, W_C1:W_C1 + CONVD], wn[:, :, DIN:DIN + CONVD], cw_raw2[:, s],
                                       ALU.mult))
                link(dve.memset(wall[:, 0:NL, s, W_Z:W_OUT], 0.0))
                link(dve.tensor_copy(wall[C:P, 0:NL, s, W_C1 + CONVD:W_DT], wn[C:P, :, 0:DIN]))
                for b in range(2):
                    link(dve.tensor_copy(wall[C * b:C * (b + 1), 0:NL, s, W_DT + HEADS * b:W_DT + HEADS * (b + 1)],
                                         wn[C * b:C * (b + 1), :, DIN + CONVD:PROJ]))
                link(dve.scalar_tensor_tensor(out=wall[:, 0:NL, s, W_OUT:W_OUT + C], in0=wout_raw[:, s], scalar=0.5,
                                              in1=small[:, s, :, 1:2].to_broadcast([P, NL, C]),
                                              op0=ALU.mult, op1=ALU.mult))
                for i in range(NL):
                    link(dve.tensor_scalar(
                        wall[:, i, s, W_D:W_D + DIN].rearrange("p (h d) -> p h d", h=HEADS),
                        hd_raw[:, s, i, 0, :].rearrange("p (h o) -> p h o", o=1).to_broadcast([P, HEADS, HD]),
                        0.5, None, ALU.mult))
                dve.wait_ge(s_ea, 1)
                link(dve.tensor_scalar(wall[:, 0:NL, s, W_NA:W_NA + HEADS], hd_raw[:, s, :, 1, :], -1.0, None,
                                       ALU.mult))
            assert made[0] == WD_ALL

            dve.wait_ge(s_ld, 16 * NBATCH)
            norm_vector(0)
            from_banks(0, x_io[0])

            with dve.Fori(0, n_layers) as layer:
                for s in range(2):
                    g = 2 * layer + s
                    w = wcur[s]
                    for c in range(NCK):
                        dve.wait_ge(s_rstd, NCK * g + c + 1)
                        h = h_pad[s][:, 4 * c:4 * (c + 1), wide[s] - P:]
                        if s == 1:
                            h = h.rearrange("p t (v q) -> p t v q", q=QS[1])
                        dve.tensor_tensor(h, x_tokens(s, 4 * c, 4), in_tiles(s, rstd[:, CK * c:CK * (c + 1)]),
                                          ALU.mult).then_inc(s_h, 1)
                    dve.wait_ge(s_dtt, g + 1)

                    def per_head(col):
                        return w[:, col:col + HEADS].rearrange("p (o q h) -> p o q h", o=1, q=1).to_broadcast(
                            [P, NPAIR, NBATCH, HEADS])

                    def heads(t):
                        return t[:].rearrange("p (t b h) -> p t b h", b=NBATCH, h=HEADS)

                    def block_of(ap, t):
                        return ap[:, NCK * BH * t:NCK * BH * (t + 1)].rearrange("p (c k) -> p c k", k=BH)

                    dve.wait_ge(s_wcur, 32 * (g + 1))
                    cols = bank[4][:].rearrange("p (t k) -> p t k", k=QUAD)[:, :, 0:BH].rearrange(
                        "p t (b h) -> p t b h", h=HEADS)
                    dve.tensor_tensor(heads(dtv), cols, per_head(W_DTB), ALU.add).then_inc(s_v, 1)
                    dve.wait_ge(s_l, g + 1)
                    for t in range(NPAIR // NCK):
                        ins = dve.scalar_tensor_tensor(
                            out=dtl[:].rearrange("p (c t k) -> p c t k", c=NCK, k=BH)[:, :, t, :],
                            in0=block_of(dtv, t), scalar=0.0, in1=block_of(dta, t), op0=ALU.max, op1=ALU.add)
                    ins.then_inc(s_dt, 1)
                    dve.wait_ge(s_dt, 2 * g + 1)
                    dve.tensor_tensor(heads(dta_log), heads(dtl), per_head(W_NA), ALU.mult).then_inc(s_dta, 1)
                    dve.tensor_scalar(dt_half[:], dtl[:], 0.5, None, ALU.mult).then_inc(s_dt, 1)
                    def gates(m, u, first):
                        n, j = NPAIR * g + 2 * m + u, 2 * m + u
                        if not first:
                            dve.wait_ge(s_xd, n - 1)
                        dve.wait_ge(s_th, n + 1)
                        dve.scalar_tensor_tensor(
                            out=xbc[u][:].rearrange("p b c -> p (b c)"), in0=th[:].rearrange("p b c -> p (b c)"),
                            scalar=1.0, in1=bank[0][:, 0:NBATCH * CONVD], op0=ALU.add, op1=ALU.mult
                            ).then_inc(s_xbc, 1)

                    def gate_z(m, u):
                        n, j = NPAIR * g + 2 * m + u, 2 * m + u
                        dve.wait_ge(s_thz, n + 1)
                        dve.scalar_tensor_tensor(
                            out=z_all[:, bass.ds(j, 1), :, :].rearrange("p o b t -> p (o b t)"),
                            in0=thz[:].rearrange("p b t -> p (b t)"), scalar=1.0, in1=bank[1][:, 0:NBATCH * P],
                            op0=ALU.add, op1=ALU.mult).then_inc(s_z, 1)

                    def mask(m, u):
                        dve.wait_ge(s_g, NPAIR * g + 2 * m + u + 1)
                        for b in range(2):
                            ins = dve.scalar_tensor_tensor(out=gm[u][:, b, :], in0=bank[(4, 0)[b]][:, G_COL:G_COL + P],
                                                           scalar=0.25, in1=tri[s][:], op0=ALU.mult, op1=ALU.mult)
                        ins.then_inc(s_gm, 1)

                    def weigh(m, u, q):
                        n, b, hh = NPAIR * g + 2 * m + u, q // 2, q % 2
                        dve.wait_ge(s_exp, 4 * n + q + 1)
                        if q == 0:
                            dve.wait_ge(s_gm, n + 1)
                        e = em[u][:, b, 4 * hh:4 * hh + 4, :]
                        dve.scalar_tensor_tensor(out=e, in0=e, scalar=1.0,
                                                 in1=gm[u][:, b:b + 1, :].to_broadcast([P, 4, P]),
                                                 op0=ALU.min, op1=ALU.mult).then_inc(s_m, 1)

                    def gate_y(m, u, first):
                        n, j = NPAIR * g + 2 * m + u, 2 * m + u
                        dve.wait_ge(s_y, n + 1)
                        dve.wait_ge(s_z, n + 1)
                        if not first:
                            dve.wait_ge(s_ss, n - 1)
                        dve.tensor_tensor(yg[u][:], bank[5][:, 0:2 * P].rearrange("p (b t) -> p b t", b=2),
                                          z_all[:, bass.ds(j, 1), :, :].rearrange("p o b t -> p (o b) t"),
                                          ALU.mult).then_inc(s_yg, 1)

                    def norm_out(m, u, first):
                        n = NPAIR * g + 2 * m + u
                        dve.wait_ge(s_oc, n + 1)
                        dve.wait_ge(s_rb, n + 1)
                        if not first:
                            dve.wait_ge(s_x, n - 1)
                        dve.tensor_tensor(on[u][:], bank[7][:, P:2 * P], oc[u][:], ALU.mult).then_inc(s_on, 1)

                    def step(m, u, j=None):
                        nxt = (m + (u + 1) // 2, (u + 1) % 2)
                        prv = (m + (u - 1) // 2, (u - 1) % 2)
                        has_next = j is None or j + 1 < NPAIR
                        here = j is None or 0 <= j < NPAIR
                        if j == 0:
                            gates(*nxt, True)
                        if here:
                            weigh(m, u, 0)
                            weigh(m, u, 1)
                        if has_next and j != 0:
                            gates(*nxt, j is not None and j + 1 < 2)
                        if here:
                            weigh(m, u, 2)
                            weigh(m, u, 3)
                        if j is None or 1 <= j <= NPAIR:
                            gate_y(*prv, j is not None and j - 1 < 2)
                        if j is None or j >= 2:
                            norm_out(m - 1, u, j is not None and j - 2 < 2)
                        if has_next:
                            mask(*nxt)
                            gate_z(*nxt)

                    gates(0, 0, True)
                    dve.wait_ge(s_hi, g + 1)
                    cum = bank[5][:, 0:NPAIR * BH].rearrange("p (j k) -> p j k", k=BH)
                    r3 = rest[:].rearrange("p (j k) -> p j k", k=BH)
                    dve.tensor_tensor(r3, cum, part(0), ALU.subtract).then_inc(s_rest, 1)
                    dve.wait_ge(s_rest, g + 1)
                    dve.tensor_copy(part(1), r3).then_inc(s_mid, 1)
                    dve.wait_ge(s_mid, g + 1)
                    dve.tensor_tensor(part(2), r3, part(1), ALU.subtract).then_inc(s_lo, 1)
                    gate_z(0, 0)
                    dve.wait_ge(s_pt, 2 * g + 2)
                    dve.tensor_copy(cum_t[0:R_TOP, NPAIR // 2:, :].rearrange("p j t -> p (j t)"),
                                    bank[7][:].bitcast(BF16)[0:R_TOP, :]).then_inc(s_ct, 1)
                    mask(0, 0)
                    for j in range(4):
                        step(j // 2, j % 2, j)
                    with dve.Fori(2, NPAIR // 2 - 1) as m:
                        step(m, 0)
                        step(m, 1)
                    for j in range(NPAIR - 2, NPAIR + 2):
                        step(j // 2, j % 2, j)

            for c in range(NCK):
                dve.wait_ge(s_bt2, c + 1)
                v = x_in[:].rearrange("p j b c -> p (j b c)")[:, CK * c:CK * (c + 1)]
                dve.tensor_tensor(v, bank[c][:], v, ALU.add).then_inc(s_x1, 1)
            dve.wait_ge(s_x1, NCK)
            norm_vector(1)
            from_banks(1, x_io[1])

            made2 = [0]

            def mixed(ins):
                made2[0] += 1
                ins.then_inc(s_mix, 1)
                dve.wait_ge(s_mix, made2[0])

            def over_e(t):
                return t[:].rearrange("p (t o) -> p t o", o=1).to_broadcast([P, NT2, E])

            dve.wait_ge(s_gate, 1)
            mixed(dve.tensor_tensor(prob, bank[4][:].rearrange("p (t e) -> p t e", e=E),
                                    gate_b[:].rearrange("p (o e) -> p o e", o=1).to_broadcast([P, NT2, E]), ALU.add))
            mixed(dve.tensor_reduce(top[0][:], prob, AX.X, ALU.max))
            mixed(dve.tensor_tensor(prob, prob, over_e(top[0]), ALU.subtract))
            dve.wait_ge(s_prob, 1)
            mixed(dve.tensor_reduce(top[0][:], prob, AX.X, ALU.add))
            mixed(dve.reciprocal(top[1][:], top[0][:]))
            mixed(dve.tensor_tensor(prob, prob, over_e(top[1]), ALU.mult))
            rk = rank[:].rearrange("p (o e) -> p o e", o=1).to_broadcast([P, NT2, E])
            for i, (hot, src) in enumerate(((hot1, prob), (hot2, work))):
                if i == 1:
                    mixed(dve.scalar_tensor_tensor(out=work, in0=hot1, scalar=-2.0, in1=prob, op0=ALU.mult,
                                                   op1=ALU.add))
                mixed(dve.tensor_reduce(top[i][:], src, AX.X, ALU.max))
                mixed(dve.tensor_tensor(hot, src, over_e(top[i]), ALU.is_equal))
                mixed(dve.tensor_tensor(hot, hot, rk, ALU.mult))
                mixed(dve.tensor_reduce(top[2][:], hot, AX.X, ALU.max))
                mixed(dve.tensor_tensor(hot, hot, over_e(top[2]), ALU.is_equal))
            mixed(dve.tensor_tensor(top[2][:], top[0][:], top[1][:], ALU.add))
            mixed(dve.reciprocal(top[3][:], top[2][:]))
            for i, hot in enumerate((hot1, hot2)):
                mixed(dve.tensor_tensor(top[i][:], top[i][:], top[3][:], ALU.mult))
                mixed(dve.tensor_tensor(hot, hot, over_e(top[i]), ALU.mult))
            mixed(dve.tensor_tensor(mix[:].rearrange("p j b e -> p (j b) e"), hot1, hot2, ALU.add))
            mixv = mix[:].rearrange("p j b e -> p j (b e)")
            left = work.rearrange("p (j b) e -> p j (b e)", b=NBATCH)

            def mix_part(i):
                return parts[:, :, QUAD * i:QUAD * (i + 1)]

            mixed(dve.tensor_copy(mix_part(0), mixv))
            mixed(dve.tensor_tensor(left, mixv, mix_part(0), ALU.subtract))
            mixed(dve.tensor_copy(mix_part(1), left))
            mixed(dve.tensor_tensor(mix_part(2), left, mix_part(1), ALU.subtract))
            assert made2[0] == MIX_STEPS
            dve.wait_ge(s_gt, 2)
            dve.tensor_copy(cum_t[0:NPART * QUAD, NPAIR // 2:, :].rearrange("p j t -> p (j t)"),
                            bank[7][:].bitcast(BF16)[0:NPART * QUAD, :]).then_inc(s_gc, 1)

            with dve.Fori(0, NCK) as q:
                dve.wait_ge(s_eo, E * q)
                for e in range(E):
                    for b in range(NBATCH):
                        k = NSTEP * q + 2 * e + b
                        dve.wait_ge(s_sil, k + 1)
                        dve.tensor_tensor(act_h[b], sil[b], bank[2 * b + 1][:], ALU.mult).then_inc(s_u, 1)
                        dve.wait_ge(s_gb, k + 1)
                        dve.wait_ge(s_u, k + 1)
                        if e >= 2:
                            dve.wait_ge(s_eo, E * q + e - 1)
                        dve.tensor_tensor(hidden[e % 2][b], act_h[b], bank[4 + b][:], ALU.mult).then_inc(s_hid, 1)
                dve.wait_ge(s_ot, q + 1)
                v = x_in[:, bass.ds(4 * q, 4), :, :].rearrange("p j b c -> p (j b c)")
                dve.tensor_tensor(v, bank[7][:], v, ALU.add).then_inc(s_acc, 1)


_INS = ["x"] + [f"L0_conv_{k}_{n}" for k in ("t", "b")
                for n in ("norm", "Win", "cw", "cb", "dtb", "Alog", "D", "gn", "Wout")] + [
    f"L0_ffn_{n}" for n in ("gate_w", "gate_b", "w1", "w2", "w3")]


def kernel(**inputs):
    import numpy as _np
    import concourse.bacc as _bacc
    from concourse import mybir as _mybir
    from concourse.bass_utils import run_bass_kernel_spmd as _run

    nc = _bacc.Bacc("TRN2", target_bir_lowering=False, num_devices=1)
    arrays, args = {}, {}
    for name in _INS:
        v = _np.ascontiguousarray(inputs[name])
        arrays[f"in_{name}"] = v
        args[name.replace("L0_conv_", "").replace("L0_ffn_", "")] = nc.dram_tensor(
            f"in_{name}", v.shape, _mybir.dt.from_np(v.dtype), kind="ExternalInput").ap()
    out = nc.dram_tensor("out", inputs["x"].shape, _mybir.dt.from_np(_np.dtype("float32")),
                         kind="ExternalOutput").ap()
    build(nc, args, out)
    return _run(nc, [arrays], core_ids=[0]).results[0]["out"]
```

```python
from contextlib import ExitStack

import concourse.bass as bass
from concourse import mybir

ALU = mybir.AluOpType
ACT = mybir.ActivationFunctionType
AX = mybir.AxisListType
F32 = mybir.dt.float32
BF16 = mybir.dt.bfloat16

P = 128
QUAD = 32
NBATCH = 2
C = 64
TOK = 2048
NPAIR = TOK // P
NL = 6
DIN = 128
NST = 16
HEADS = 8
HD = DIN // HEADS
DCONV = 4
CONVD = DIN + 2 * NST
PROJ = 2 * DIN + 2 * NST + HEADS
SEQ = (128, 16)
QS = (P // SEQ[0], P // SEQ[1])
BANDS = 16
E = 16
HID = 128
BH = NBATCH * HEADS
NPART = 3
NBLK = 32
R_ONE = NPART * BH
R_TOP = P - NBLK
R_BLK = R_TOP
FAR = -30000.0
CK = 512
NCK = TOK // CK

W_C0 = 0
W_C1 = W_C0 + CONVD
W_Z = W_C1 + CONVD
W_DT = W_Z + DIN
W_OUT = W_DT + QUAD
W_D = W_OUT + C
W_DTB = W_D + DIN
W_NA = W_DTB + HEADS
W_ALL = W_NA + HEADS
G_COL = CK - P
GROUPS = ((0, 4), (4, 8), (8, 12), (12, 15), (15, 16))
NG = len(GROUPS)


def build(nc, a, out, n_layers=NL):
    with ExitStack() as ctx:
        def sb(name, shape, dt=F32):
            return ctx.enter_context(nc.sbuf_tensor(name, shape, dt))

        def sem(name):
            return ctx.enter_context(nc.semaphore(name))

        bank = [ctx.enter_context(nc.psum_tensor(f"bank{i}", [P, CK], F32)) for i in range(8)]

        ident = sb("ident", [P, P])
        identb = sb("identb", [P, P], BF16)
        tri = [sb("tri_time", [P, P]), sb("tri_bands", [P, P])]
        mean64 = sb("mean64", [P, P])
        ones3 = sb("ones3", [P, P], BF16)
        target = [sb(f"target{u}", [P, BH, P], BF16) for u in range(2)]
        far_rows = sb("far_rows", [P, P], BF16)
        one_rows = sb("one_rows", [P, P], BF16)
        eps6 = sb("eps6", [P, 1])
        eps5 = sb("eps5", [P, 1])
        mhalf = sb("mhalf", [P, NBATCH])
        ones1 = sb("ones1", [P, 1])

        wall = sb("wall", [P, NL + 1, 2, W_ALL])
        ball = sb("ball", [P, 2, NL + 1, CONVD], BF16)
        wcur = [sb(f"wcur{s}", [P, W_ALL]) for s in range(2)]
        bcur = [sb(f"bcur{s}", [P, CONVD], BF16) for s in range(2)]

        x_io = [sb("x_time_in", [P, TOK]), sb("x_bands_in", [P, TOK])]
        wide = [(SEQ[s] + DCONV - 1) * QS[s] for s in range(2)]
        h_pad = [sb(f"h_pad{s}", [P, NPAIR, wide[s]]) for s in range(2)]
        slot = [[[sb(f"slot{s}{u}{b}", [P, wide[s]]) for b in range(2)] for u in range(2)] for s in range(2)]
        sq = sb("sq", [P, TOK])
        head_neg, head_row = (sq[:].bitcast(BF16)[:, BH * P * k:BH * P * (k + 1)].rearrange(
            "p (h t) -> p h t", h=BH) for k in range(2))
        rstd = sb("rstd", [P, TOK])
        dtv = sb("dtv", [P, NPAIR * BH])
        dta = sb("dta", [P, NPAIR * BH])
        dtl = sb("dtl", [P, NPAIR * BH])
        dtf = sb("dtf", [P, CK])
        dt_half = sb("dt_half", [P, NPAIR * BH])
        dta_log = sb("dta_log", [P, NPAIR * BH])
        rest = sb("rest", [P, NPAIR * BH])
        parts = sb("parts", [P, NPAIR, R_TOP], BF16)
        cum_t = sb("cum_t", [P, NPAIR, P], BF16)

        th = sb("th", [P, NBATCH, CONVD])
        thz = sb("thz", [P, NBATCH, P])
        xbc = [sb(f"xbc{u}", [P, NBATCH, CONVD]) for u in range(2)]
        z_all = sb("z_all", [P, NPAIR, NBATCH, P])
        bt = [sb(f"bt{u}", [2 * QUAD, P]) for u in range(2)]
        ct = [sb(f"ct{u}", [2 * QUAD, P]) for u in range(2)]
        gm = [sb(f"gm{u}", [P, NBATCH, P]) for u in range(2)]
        em = [sb(f"em{u}", [P, NBATCH, HEADS, P]) for u in range(2)]
        xdt = [sb(f"xdt{u}", [P, NBATCH, HEADS // 2, 2, 2 * HD]) for u in range(2)]
        xd = [sb(f"xd{u}", [P, NBATCH, DIN]) for u in range(2)]
        yg = [sb(f"yg{u}", [P, NBATCH, P]) for u in range(2)]
        ysq = [sb(f"ysq{u}", [P, NBATCH, P]) for u in range(2)]
        var = [sb(f"var{u}", [P, NBATCH]) for u in range(2)]
        rr = [sb(f"rr{u}", [P, NBATCH]) for u in range(2)]
        oc = [sb(f"oc{u}", [P, P]) for u in range(2)]
        on = [sb(f"on{u}", [P, P]) for u in range(2)]
        xsq = [sb(f"xsq{u}", [P, P]) for u in range(2)]

        x_in = sb("x_in", [P, NPAIR, NBATCH, C])
        stat = sb("stat", [P, NPAIR * NBATCH])
        stat2 = sb("stat2", [P, NPAIR * NBATCH])

        s_ld = sem("x_loaded")
        s_wld = sem("weights_loaded")
        s_const = sem("constants_made")
        s_wd = sem("weights_made")
        s_bld = sem("bias_rows_placed")
        s_ln = sem("norm_step")
        s_tp = sem("norm_transposed")
        s_x0 = sem("x0_ready")

        win_raw = z_all[:].rearrange("p a b c -> p (a b c)")[:, 0:2 * NL * PROJ].rearrange(
            "p (s l n) -> p s l n", s=2, l=NL)
        cw_raw = em[0][:].rearrange("p a b c -> p (a b c)")[:, 0:2 * NL * CONVD].rearrange(
            "p (s l n) -> p s l n", s=2, l=NL)
        cw_raw2 = em[1][:].rearrange("p a b c -> p (a b c)")[:, 0:2 * NL * CONVD].rearrange(
            "p (s l n) -> p s l n", s=2, l=NL)
        wout_raw = sb("wout_raw", [P, 2, NL, C])
        small = sb("small", [P, 2, NL, 2])
        hd_raw = sb("hd_raw", [P, 2, NL, 2, HEADS])
        cb_raw = sb("cb_raw", [2 * NL * CONVD // 16, 16])
        cb_rest = sb("cb_rest", [2 * NL * CONVD // 16, 16])
        cb_part = sb("cb_part", [2 * NL * CONVD // 16, NPART, 16], BF16)
        CBROWS = NL * CONVD // 16

        names = ("t", "b")
        N_WDMA = 28
        WD_CB = 4
        WD_ALL = 34
        N_FIRST = 7
        N_CONST = 51
        LN_STEPS = 8
        MIX_STEPS = 28
        s_ea = sem("exp_a_log")
        s_tm = sem("block_rows_made")

        s_sq, s_ms, s_lnv, s_rstd, s_h = (sem(n) for n in (
            "squares", "mean_squares", "log_var", "rstd_ready", "h_ready"))
        s_ct0 = sem("first_cum_t_ready")
        s_ct2 = sem("cum_t_late_ready")
        s_dtf, s_dtt = sem("dt_copied"), sem("dt_transposed")
        s_xs, s_mx, s_mc = (sem(n) for n in ("x_squared", "x_mean_square", "mean_square_copied"))
        s_dtp, s_v, s_abs, s_e, s_l, s_dt, s_dta, s_cum = (sem(n) for n in (
            "dt_projected", "dt_biased", "dt_abs", "dt_exp", "dt_log1p", "dt_ready", "dta_ready", "cum_ready"))
        s_hi, s_rest, s_mid, s_lo, s_pt, s_ct = (sem(n) for n in (
            "cum_hi", "cum_rest", "cum_mid", "cum_lo", "parts_transposed", "cum_t_ready"))
        s_wcur = sem("current_weights")
        s_st = [sem("slot0_staged"), sem("slot1_staged")]
        s_tg = [sem("target0_staged"), sem("target1_staged")]
        s_proj, s_zp, s_th, s_thz, s_xbc, s_z, s_bt, s_btc, s_g, s_gm = (sem(n) for n in (
            "projected", "z_projected", "tanh_done", "tanh_z_done", "xbc_ready", "z_ready", "bc_transposed",
            "bc_copied", "g_ready", "gm_ready"))
        s_seg, s_exp, s_m, s_xdt, s_xd, s_y, s_yg = (sem(n) for n in (
            "seg_ready", "exp_done", "m_ready", "xdt_ready", "xd_ready", "y_ready", "y_gated"))
        s_ysq, s_o, s_oc, s_ss, s_var, s_rr, s_rb, s_on, s_x = (sem(n) for n in (
            "y_squared", "o_ready", "o_copied", "ss_ready", "var_ready", "r_ready", "r_spread", "o_normed", "x_updated"))

        w1s = em[0][:].rearrange("p a b c -> p (a b c)").rearrange("p (e h) -> p e h", e=E)
        w2s = em[1][:].rearrange("p a b c -> p (a b c)").rearrange("p (e h) -> p e h", e=E)
        w3s = h_pad[0][:].rearrange("p j v -> p (j v)")[:, 0:E * C].rearrange("p (e c) -> p e c", e=E)
        zflat = z_all[:].rearrange("p a b c -> p (a b c)")
        sil, act_h = ([zflat[:, CK * (2 * k + b):CK * (2 * k + b + 1)] for b in range(NBATCH)] for k in range(2))
        hidden = [[zflat[:, CK * (4 + 2 * k + b):CK * (5 + 2 * k + b)] for b in range(NBATCH)] for k in range(2)]
        moe = sq[:, 0:CK]
        gate_w = sb("gate_w", [P, NBATCH, E])
        gate_b = sb("gate_b", [P, E])
        rank = sb("rank", [P, E])
        NT2 = NPAIR * NBATCH
        hb = h_pad[1][:].rearrange("p j v -> p (j v)")
        prob, hot1, hot2, work = (hb[:, NT2 * E * i:NT2 * E * (i + 1)].rearrange("p (t e) -> p t e", e=E)
                                  for i in range(4))
        mix = sb("mix", [P, NPAIR, NBATCH, E])
        top = [sb(f"top{i}", [P, NT2]) for i in range(4)]
        s_out = sem("out_stored")
        s_ew = sem("expert_weights_loaded")
        s_bt2, s_x1, s_gate, s_mix, s_prob = (sem(n) for n in (
            "conv_transposed", "x1_ready", "gate_ready", "mix_step", "prob_exp"))
        xq = rstd[:, 0:CK]
        s_sel, s_gt, s_gc = (sem(n) for n in ("selectors_made", "mix_transposed", "mix_rows_copied"))
        s_xq, s_h1, s_h2, s_gb, s_sil, s_u, s_hid, s_eo, s_oc2, s_ot, s_acc = (sem(n) for n in (
            "xq_ready", "h1_ready", "h2_ready", "mix_spread", "silu_done", "silu_times_h2", "hidden_ready", "expert_out",
            "sum_copied", "sum_transposed", "accumulated"))
        NSTEP = NBATCH * E

        def hcols(s, j):
            return h_pad[s][:].rearrange("p j v -> p (j v)")[:, bass.ds(j * wide[s], wide[s])]

        def part(r):
            return parts[:, :, BH * r:BH * (r + 1)]

        def lhs(s, ap, first):
            return ap[:, QS[s] * first:QS[s] * first + P]

        def x_tokens(s, j, n):
            if s == 0:
                return x_io[0][:].rearrange("p (t v) -> p t v", v=P)[:, bass.ds(j, n), :]
            v = x_io[1][:].rearrange("p (v t q) -> p t v q", v=BANDS, q=QS[1])
            return v[:, bass.ds(j, n), :, :]

        def of_tile(ap):
            return ap.rearrange("p (a q) -> p a q", q=QS[1])

        def x_out(s, j):
            v = x_io[1 - s][:, bass.ds(P * j, P)]
            return of_tile(v) if s == 0 else v.rearrange("p (q v) -> p v q", v=SEQ[1])

        def ms_out(s, j):
            if s == 0:
                return rstd[:].rearrange("p (t w) -> p t w", w=P)[:, :, bass.ds(QS[1] * j, QS[1])]
            return rstd[:, bass.ds(P * j, P)].rearrange("p (q v) -> p v q", v=SEQ[1])

        def group(s, ap, c):
            a, b = GROUPS[c]
            if s == 0:
                return ap[:, P * a:P * b].rearrange("p (t v) -> p t v", v=P)
            return ap.rearrange("p (t w) -> p t w", w=P)[:, :, QS[1] * a:QS[1] * b]

        def x_group(s, c):
            if s == 0:
                return group(0, x_io[0][:], c)
            return x_io[1][:].rearrange("p (v t q) -> p t v q", v=BANDS, q=QS[1])[:, :, slice(*GROUPS[c]), :]

        def h_group(s, c):
            a, b = GROUPS[c]
            if s == 0:
                return h_pad[0][:, a:b, wide[0] - P:]
            pad = wide[1] - P
            return h_pad[1][:, :, pad + QS[1] * a:pad + QS[1] * b].rearrange("p t (v q) -> p t v q", q=QS[1])

        def x_by_r(dve, s, c, count):
            dve.wait_ge(s_rstd, count + c + 1)
            v = group(s, rstd[:], c)
            if s == 1:
                v = v.rearrange("p t (v q) -> p t v q", q=QS[1])
            dve.tensor_tensor(h_group(s, c), x_group(s, c), v, ALU.mult).then_inc(s_h, 1)

        def log_of(act, s, c):
            v = group(s, rstd[:], c)
            act.activation(v, v, ACT.Ln, bias=eps6[:]).then_inc(s_lnv, 1)

        def root_of(act, s, c, count):
            v = group(s, rstd[:], c)
            act.wait_ge(s_lnv, count + c + 1)
            act.activation(v, v, ACT.Exp, scale=-0.5).then_inc(s_rstd, 1)

        def in_tiles(s, ap):
            if s == 0:
                return ap.rearrange("p (t v) -> p t v", v=P)
            return ap.rearrange("p (t v q) -> p t v q", v=BANDS, q=QS[1])

        block = ctx.enter_context(nc.Block())

        @block.sync
        def _(sp):
            for b in range(NBATCH):
                sp.dma_start(x_in[:, :, b, :], a["x"][b].rearrange("t k c -> (t k) c").rearrange(
                    "(j p) c -> p j c", p=P)).then_inc(s_ld, 16)
            for s, nm in enumerate(names):
                for d in range(2):
                    rows = slice(C * d, C * d + C)
                    sp.dma_start(win_raw[rows, s], a[f"{nm}_Win"].rearrange("l c n -> c l n")).then_inc(s_wld, 16)
                    sp.dma_start(small[rows, s, :, 0:1], a[f"{nm}_norm"].rearrange("l (c o) -> c l o", o=1),
                                 allow_slow_non_contiguous=True).then_inc(s_wld, 16)
                    sp.dma_start(cw_raw[rows, s], a[f"{nm}_cw"][:, d, :].partition_broadcast(C)).then_inc(s_wld, 16)
                    sp.dma_start(cw_raw2[rows, s], a[f"{nm}_cw"][:, 2 + d, :].partition_broadcast(C)).then_inc(s_wld, 16)
                sp.dma_start(small[:, s, :, 1:2], a[f"{nm}_gn"].rearrange("l (c o) -> c l o", o=1),
                                 allow_slow_non_contiguous=True).then_inc(s_wld, 16)
                sp.dma_start(wout_raw[:, s], a[f"{nm}_Wout"].rearrange("l c n -> c l n")).then_inc(s_wld, 16)
                sp.dma_start(hd_raw[:, s, :, 0, :], a[f"{nm}_D"].partition_broadcast(P)).then_inc(s_wld, 16)
                sp.dma_start(hd_raw[:, s, :, 1, :], a[f"{nm}_Alog"].partition_broadcast(P)).then_inc(s_wld, 16)
                sp.dma_start(wall[:, 0:NL, s, W_DTB:W_DTB + HEADS], a[f"{nm}_dtb"].partition_broadcast(P)).then_inc(s_wld, 16)
                sp.dma_start(cb_raw[CBROWS * s:CBROWS * (s + 1), :],
                             a[f"{nm}_cb"].rearrange("l n -> (l n)").rearrange("(p f) -> p f", f=16)).then_inc(s_wld, 16)
            sp.wait_ge(s_wd, WD_CB)
            sp.wait_ge(s_const, N_CONST)
            for r in range(NPART):
                for s in range(2):
                    sp.dma_start(ball[r:r + 1, s, 0:NL, :].rearrange("o l n -> o (l n)").rearrange(
                        "o (p f) -> o p f", f=16), cb_part[CBROWS * s:CBROWS * (s + 1), r, :]).then_inc(s_bld, 16)

            def weights_in(s, layer):
                sp.dma_start(wcur[s][:], wall[:, bass.ds(layer, 1), s, :].rearrange("p l n -> p (l n)")
                             ).then_inc(s_wcur, 16)
                sp.dma_start(bcur[s][:], ball[:, s, bass.ds(layer, 1), :].rearrange("p l n -> p (l n)")
                             ).then_inc(s_wcur, 16)

            sp.wait_ge(s_wd, WD_ALL)
            sp.wait_ge(s_bld, 16 * 2 * NPART)
            weights_in(0, 0)

            with sp.Fori(0, n_layers) as layer:
                for s in range(2):
                    g = 2 * layer + s

                    def stage_in(m, u, first):
                        j = 2 * m + u
                        if not first:
                            sp.wait_ge(s_zp, NPAIR * g + j - 1)
                        for b in range(2):
                            src = hcols(s, j)[C * b:C * b + C, :]
                            sp.dma_start(slot[s][u][b][0:C, :], src).then_inc(s_st[u], 16)
                            sp.dma_start(slot[s][u][b][C:P, 0:wide[s] - QS[s]], src[:, QS[s]:wide[s]]).then_inc(s_st[u], 16)

                    def target_in(m, u, first):
                        j = 2 * m + u
                        if first:
                            sp.wait_ge(s_ct, g + 1)
                        if not first:
                            sp.wait_ge(s_seg, 4 * (NPAIR * g + j - 1))
                        for r in range(NPART):
                            sp.dma_start(target[u][R_ONE + r:R_ONE + r + 1, :, :],
                                         cum_t[BH * r:BH * (r + 1), bass.ds(j, 1), :].rearrange("h o t -> h (o t)")
                                         ).then_inc(s_tg[u], 16)

                    sp.wait_ge(s_h, NG * (g + 1))
                    stage_in(0, 0, True)
                    stage_in(0, 1, True)
                    stage_in(1, 0, False)
                    target_in(0, 1, True)
                    target_in(1, 0, False)
                    stage_in(1, 1, False)
                    target_in(1, 1, False)
                    sp.wait_ge(s_ct2, g + 1)
                    sp.wait_ge(s_xd, NPAIR * g + 1)
                    weights_in(1 - s, layer + s)
                    with sp.Fori(2, NPAIR // 2) as m:
                        for u in range(2):
                            stage_in(m, u, False)
                            target_in(m, u, False)

            sp.wait_ge(s_x, NPAIR * 2 * n_layers)
            sp.wait_ge(s_y, NPAIR * 2 * n_layers)
            for b in range(2):
                rows = slice(C * b, C * b + C)
                sp.dma_start(w1s[rows], a["w1"].rearrange("e c h -> c e h")).then_inc(s_ew, 16)
                sp.dma_start(w2s[rows], a["w2"].rearrange("e c h -> c e h")).then_inc(s_ew, 16)
                sp.dma_start(gate_w[rows, b, :], a["gate_w"]).then_inc(s_ew, 16)
            sp.wait_ge(s_h, NG * (2 * n_layers + 1))
            sp.dma_start(w3s, a["w3"].rearrange("e h c -> h e c")).then_inc(s_ew, 16)
            sp.dma_start(gate_b[:], a["gate_b"].partition_broadcast(P)).then_inc(s_ew, 16)

            with sp.Fori(0, NCK) as q:
                for b in range(NBATCH):
                    sp.wait_ge(s_acc, q + 1)
                    sp.dma_start(out[b].rearrange("t k c -> (t k) c").rearrange("(j p) c -> p j c", p=P)[
                        :, bass.ds(4 * q, 4), :], x_in[:, bass.ds(4 * q, 4), b, :]).then_inc(s_out, 16)
            sp.wait_ge(s_out, 16 * NBATCH * NCK)

        @block.gpsimd
        def _(pool):
            made = [0]

            def const(ins):
                made[0] += 1
                ins.then_inc(s_const, 1)
                pool.wait_ge(s_const, made[0])

            const(pool.memset(eps6[:], 1e-6))
            const(pool.memset(eps5[:], 1e-5))
            const(pool.memset(mean64[:], 0.0))
            for b in range(2):
                const(pool.memset(mean64[C * b:C * b + C, C * b:C * b + C], 1.0 / C))
            const(pool.memset(ident[:], 0.0))
            const(pool.affine_select(out=ident[:], in_=ident[:], compare_op=ALU.not_equal, fill=1.0, base=0,
                                     pattern=[[-1, P]], channel_multiplier=1))
            assert made[0] == N_FIRST
            const(pool.tensor_copy(identb[:], ident[:]))
            const(pool.memset(tri[0][:], 1.0))
            const(pool.memset(tri[1][:], 0.0))
            v = tri[1][:].rearrange("p (v q) -> p v q", q=QS[1])
            for k in range(SEQ[1]):
                const(pool.affine_select(out=v, in_=v, compare_op=ALU.not_equal, fill=1.0, base=-QS[1] * k,
                                         pattern=[[0, SEQ[1]], [-1, QS[1]]], channel_multiplier=1))
            for s in range(2):
                const(pool.affine_select(out=tri[s][:], in_=tri[s][:], compare_op=ALU.is_ge, fill=0.0, base=0,
                                         pattern=[[1, P]], channel_multiplier=-1))
            const(pool.memset(ones3[:], 0.0))
            const(pool.memset(ones3[0:NPART, :], 1.0))
            const(pool.memset(target[0][:], 0.0))
            v = target[0][0:R_TOP]
            for r in range(NPART):
                const(pool.affine_select(out=v, in_=v, compare_op=ALU.not_equal, fill=-1.0, base=-BH * r,
                                         pattern=[[-1, BH], [0, P]], channel_multiplier=1))
            const(pool.memset(cum_t[:], 0.0))
            const(pool.memset(far_rows[:], 0.0))
            v = far_rows[R_BLK:P].rearrange("p (k t) -> p k t", k=NBLK)
            const(pool.affine_select(out=v, in_=v, compare_op=ALU.is_ge, fill=FAR, base=0,
                                     pattern=[[1, NBLK], [0, P // NBLK]], channel_multiplier=-1))
            const(pool.memset(one_rows[:], 0.0))
            v = one_rows[R_BLK:P].rearrange("p (k t) -> p k t", k=NBLK)
            const(pool.affine_select(out=v, in_=v, compare_op=ALU.not_equal, fill=1.0, base=0,
                                     pattern=[[-1, NBLK], [0, P // NBLK]], channel_multiplier=1))
            const(pool.memset(mhalf[:], -0.5))
            const(pool.memset(ones1[:], 1.0))
            for u in range(2):
                const(pool.memset(xdt[u][:], 0.0))
            const(pool.memset(ball[:], 0.0))
            const(pool.memset(wall[:, NL, 0, :], 0.0))
            const(pool.memset(parts[:], 0.0))
            const(pool.memset(parts[:, :, R_ONE:R_ONE + NPART], 1.0))
            for s in range(2):
                const(pool.memset(h_pad[s][:], 0.0))
            const(pool.memset(gate_w[:], 0.0))
            const(pool.iota(rank[:], pattern=[[-1, E]], base=E, channel_multiplier=0,
                            allow_small_or_imprecise_dtypes=True))
            assert made[0] == N_CONST

            with pool.Fori(0, n_layers) as layer:
                for s in range(2):
                    g = 2 * layer + s

                    pool.wait_ge(s_wcur, 32 * (g + 1))
                    pool.wait_ge(s_dt, 2 * g + 2)

                    def x_dt(m, u, first):
                        j, n = 2 * m + u, NPAIR * g + 2 * m + u
                        pool.wait_ge(s_xbc, n + 1)
                        if not first:
                            pool.wait_ge(s_y, n - 1)
                        for b in range(NBATCH):
                            for r in range(2):
                                ins = pool.tensor_tensor(
                                    out=xdt[u][:, b, :, r, HD * r:HD * (r + 1)],
                                    in0=xbc[u][:, b, 0:DIN].rearrange("p (k r d) -> p k r d", r=2, d=HD)[:, :, r, :],
                                    in1=dt_half[:, bass.ds(BH * j, BH)].rearrange(
                                        "p (b k r) -> p b k r", b=NBATCH, r=2)[:, b, :, r:r + 1]
                                        .to_broadcast([P, HEADS // 2, HD]),
                                    op=ALU.mult)
                        ins.then_inc(s_xdt, 1)
                        pool.tensor_tensor(
                            out=xd[u][:], in0=xbc[u][:, :, 0:DIN],
                            in1=wcur[s][:, W_D:W_D + DIN].rearrange("p (o d) -> p o d", o=1)
                                .to_broadcast([P, NBATCH, DIN]),
                            op=ALU.mult).then_inc(s_xd, 1)

                    def norm(m, u, first):
                        n, j = NPAIR * g + 2 * m + u, 2 * m + u
                        pool.wait_ge(s_var, n + 1)
                        if not first:
                            pool.wait_ge(s_rb, n - 1)
                        pool.tensor_tensor(out=rr[u][:], in0=var[u][:], in1=mhalf[:], op=ALU.pow).then_inc(s_rr, 1)

                    def add_x(m, u):
                        n, j = NPAIR * g + 2 * m + u, 2 * m + u
                        pool.wait_ge(s_on, n + 1)
                        o = x_io[1 - s][:].rearrange("p (t v) -> p t v", v=P)[:, bass.ds(j, 1), :]
                        if s == 1:
                            o = o.rearrange("p t (q v) -> p t v q", v=SEQ[1])
                        pool.tensor_tensor(out=o, in0=in_tiles(s, on[u][:]), in1=x_tokens(s, j, 1),
                                           op=ALU.add).then_inc(s_x, 1)

                    def step(m, u, j=None):
                        if j is None or j >= 2:
                            norm(m - 1, u, j is not None and j - 2 < 2)
                        if j is None or j + 1 < NPAIR:
                            x_dt(m + (u + 1) // 2, (u + 1) % 2, j is not None and j + 1 < 2)
                        if j is None or j >= 2:
                            add_x(m - 1, u)

                    for j in range(-1, 4):
                        step(j // 2, j % 2, j)
                    with pool.Fori(2, NPAIR // 2 - 1) as m:
                        step(m, 0)
                        step(m, 1)
                    for j in range(NPAIR - 2, NPAIR + 2):
                        step(j // 2, j % 2, j)

            pool.wait_ge(s_seg, 4 * NPAIR * 2 * n_layers)
            made_sel = [0]

            def select(ins):
                made_sel[0] += 1
                ins.then_inc(s_sel, 1)
                pool.wait_ge(s_sel, made_sel[0])

            for b in range(NBATCH):
                select(pool.memset(target[b][:], 0.0))
                for r in range(NPART):
                    v = target[b][QUAD * r:QUAD * (r + 1)]
                    select(pool.affine_select(out=v, in_=v, compare_op=ALU.not_equal, fill=1.0, base=-E * b,
                                              pattern=[[-1, E], [0, P]], channel_multiplier=1))

        @block.tensor
        def _(pe):
            pe.wait_ge(s_const, N_FIRST)

            def to_features(done, tiles, count):
                for j in range(NPAIR):
                    t = pe.transpose(bank[j // 4][:, P * (j % 4):P * (j % 4) + P], tiles(j), ident[:])
                    if j % 4 == 3:
                        t.then_inc(done, 1)

            pe.wait_ge(s_ln, LN_STEPS)
            to_features(s_tp, lambda j: sq[:, P * j:P * j + P], 0)

            for c in range(NCK):
                pe.wait_ge(s_sq, c + 1)
                pe.matmul(bank[c][:], mean64[:], sq[:, CK * c:CK * (c + 1)],
                          start=True, stop=True).then_inc(s_ms, 1)

            pe.wait_ge(s_const, N_CONST)
            with pe.Fori(0, n_layers) as layer:
                for s in range(2):
                    g = 2 * layer + s
                    w = wcur[s]

                    pe.wait_ge(s_wcur, 32 * (g + 1))
                    pe.wait_ge(s_h, NG * (g + 1))
                    for c in range(NCK):
                        mm = pe.matmul(bank[4][QUAD * c:QUAD * (c + 1), :], w[:, W_DT:W_DT + QUAD],
                                       h_pad[s][:, 4 * c:4 * (c + 1), wide[s] - P:], start=True, stop=True)
                    mm.then_inc(s_dtp, 1)
                    pe.wait_ge(s_dtf, g + 1)
                    for t in range(4):
                        tr = pe.transpose(bank[4][:, P * t:P * (t + 1)], dtf[:, P * t:P * (t + 1)], ident[:])
                    tr.then_inc(s_dtt, 1)

                    def project(m, u, first):
                        n = NPAIR * g + 2 * m + u
                        pe.wait_ge(s_st[u], 64 * ((NPAIR // 2) * g + m + 1))
                        if not first:
                            pe.wait_ge(s_gm, n)
                        both = bank[0][:, 0:NBATCH * CONVD].rearrange("p (b n) -> p b n", b=NBATCH)
                        pe.matmul(both, ones3[:], bcur[s][:].rearrange("p (o n) -> p o n", o=1).to_broadcast(
                            [P, NBATCH, CONVD]), start=True, stop=False, skip_group_check=True)
                        for b in range(2):
                            src = slot[s][u][b][:]
                            o = bank[0][:, CONVD * b:CONVD * (b + 1)]
                            pe.matmul(o, lhs(s, src, 0), w[:, W_C0:W_C0 + CONVD], start=False,
                                      stop=False, skip_group_check=True)
                            mm = pe.matmul(o, lhs(s, src, 2), w[:, W_C1:W_C1 + CONVD],
                                           start=False, stop=True, skip_group_check=True)
                        mm.then_inc(s_proj, 1)

                    def project_z(m, u, first):
                        n = NPAIR * g + 2 * m + u
                        if not first:
                            pe.wait_ge(s_z, n)
                        for b in range(2):
                            mm = pe.matmul(bank[1][:, P * b:P * (b + 1)], w[C:P, W_Z:W_Z + DIN],
                                           lhs(s, slot[s][u][b][C:P], 2), start=True, stop=True)
                        mm.then_inc(s_zp, 1)

                    def turn_bc(m, u, first):
                        n = NPAIR * g + 2 * m + u
                        pe.wait_ge(s_xbc, n + 1)
                        if not first:
                            pe.wait_ge(s_gm, n)
                        for k in range(2):
                            for b in range(2):
                                row = QUAD * (2 * k + b)
                                t = pe.matmul(bank[4][row:row + NST, 0:P],
                                              xbc[u][:, b, DIN + NST * k:DIN + NST * (k + 1)], ident[:],
                                              start=True, stop=True)
                        t.then_inc(s_bt, 1)

                    def b_dot_c(m, u):
                        pe.wait_ge(s_btc, 2 * (NPAIR * g + 2 * m + u) + 2)
                        for b in range(2):
                            rows = slice(QUAD * b, QUAD * b + NST)
                            mm = pe.matmul(bank[(4, 0)[b]][:, G_COL:G_COL + P], bt[u][rows, :], ct[u][rows, :],
                                           start=True, stop=True)
                        mm.then_inc(s_g, 1)

                    def decays(m, u, q, first, first_pair=False):
                        n = NPAIR * g + 2 * m + u
                        b, hh = q // 2, q % 2
                        if not first:
                            pe.wait_ge(s_exp, 4 * n + q - 1)
                        o = bank[2 + hh]
                        h0 = HEADS * b + 4 * hh
                        if first_pair:
                            if q == 0:
                                pe.wait_ge(s_ct0, g + 1)
                            tile = cum_t[:, 0, :]
                            pe.matmul(o[:], tile, head_neg[:, h0:h0 + 4, :].rearrange("p h t -> p (h t)"),
                                      start=True, stop=False, skip_group_check=True)
                            for h in range(4):
                                mm = pe.matmul(o[:, P * h:P * (h + 1)], head_row[0:R_TOP, h0 + h, :], tile[0:R_TOP],
                                               start=False, stop=(h == 3), skip_group_check=True)
                            mm.then_inc(s_seg, 1)
                            return
                        if q == 0:
                            pe.wait_ge(s_tg[u], 16 * NPART * ((NPAIR // 2 - 1 + u) * g + m + u))
                        tile = cum_t[:, bass.ds(2 * m + u, 1), :].rearrange("p o t -> p (o t)")
                        pe.matmul(o[:], tile, target[u][:, h0:h0 + 4, :].rearrange("p h t -> p (h t)"),
                                  start=True, stop=True).then_inc(s_seg, 1)

                    def mix_states(m, u, first, second):
                        n = NPAIR * g + 2 * m + u
                        pe.wait_ge(s_xd, n + 1)
                        if not first:
                            pe.wait_ge(s_yg, n)
                        if second:
                            pe.wait_ge(s_mc, NCK + n - 2)
                        for b in range(2):
                            pe.matmul(bank[5][:, P * b:P * (b + 1)], xd[u][:, b, :], ident[:], start=True,
                                      stop=False, skip_group_check=True)
                            pe.wait_ge(s_m, 4 * n + 2 * b + 2)
                            for r in range(2):
                                for k in range(HEADS // 2):
                                    mm = pe.matmul(bank[5][QUAD * k:QUAD * (k + 1), P * b:P * (b + 1)],
                                                   xdt[u][:, b, k, r, :], em[u][:, b, 2 * k + r, :],
                                                   start=False, stop=(r == 1), skip_group_check=True)
                        mm.then_inc(s_y, 1)

                    def project_out(m, u, first):
                        n = NPAIR * g + 2 * m + u
                        pe.wait_ge(s_yg, n + 1)
                        if not first:
                            pe.wait_ge(s_oc, n)
                        for b in range(2):
                            mm = pe.matmul(bank[6][C * b:C * (b + 1), 0:P], w[:, W_OUT:W_OUT + C], yg[u][:, b, :],
                                           start=True, stop=True)
                        mm.then_inc(s_o, 1)
                        pe.wait_ge(s_ysq, n + 1)
                        if not first:
                            pe.wait_ge(s_on, n)
                        for b in range(2):
                            mm = pe.matmul(bank[7][:, b:b + 1], ysq[u][:, b, :], ones1[:], start=True, stop=True)
                        mm.then_inc(s_ss, 1)

                    def spread_r(m, u):
                        pe.wait_ge(s_rr, NPAIR * g + 2 * m + u + 1)
                        for b in range(2):
                            mm = pe.matmul(bank[7][C * b:C * (b + 1), P:2 * P], rr[u][:, b:b + 1].to_broadcast([P, C]),
                                           ident[:], start=True, stop=True)
                        mm.then_inc(s_rb, 1)

                    def mean_x(m, u, y_read):
                        n = NPAIR * g + 2 * m + u
                        pe.wait_ge(s_xs, n + 1)
                        if y_read:
                            pe.wait_ge(s_yg, n + 3)
                        pe.matmul(bank[5][:, 2 * P:3 * P], mean64[:], xsq[u][:], start=True,
                                  stop=True).then_inc(s_mx, 1)

                    def step(m, u, j=None):
                        nxt = (m + (u + 1) // 2, (u + 1) % 2)
                        prv = (m + (u - 1) // 2, (u - 1) % 2)
                        pr2 = (m - 1, u)
                        has_next = j is None or j + 1 < NPAIR
                        here = j is None or 0 <= j < NPAIR
                        pr3 = (m + (u - 3) // 2, (u - 1) % 2)
                        if here:
                            decays(m, u, 0, j == 0, j == 0)
                            decays(m, u, 1, j == 0, j == 0)
                        if j is None or 2 <= j <= NPAIR + 1:
                            project_out(*pr2, j is not None and j - 2 < 1)
                        if has_next:
                            project(*nxt, False)
                        if here:
                            decays(m, u, 2, False, j == 0)
                            decays(m, u, 3, False, j == 0)
                        if j is None or 1 <= j <= NPAIR:
                            mix_states(*prv, j is not None and j - 1 < 1, j is None or j >= 4)
                        if has_next:
                            turn_bc(*nxt, False)
                            project_z(*nxt, False)
                        if j is None or 2 <= j <= NPAIR + 1:
                            spread_r(*pr2)
                        if has_next:
                            b_dot_c(*nxt)
                        if j is None or j >= 3:
                            mean_x(*pr3, j is None or j <= NPAIR)

                    project(0, 0, True)
                    pe.wait_ge(s_dta, g + 1)
                    pe.matmul(bank[5][:, 0:NPAIR * BH], tri[s][:], dta_log[:],
                              start=True, stop=True).then_inc(s_cum, 1)
                    project_z(0, 0, True)
                    turn_bc(0, 0, True)
                    b_dot_c(0, 0)
                    pe.wait_ge(s_lo, g + 1)
                    for i in range(2):
                        ptb = bank[6 + i][:].bitcast(BF16)
                        for k in range(NPAIR // 2):
                            t = pe.transpose(ptb[0:R_TOP, P * k:P * (k + 1)], parts[:, NPAIR // 2 * i + k, :],
                                             identb[:])
                        t.then_inc(s_pt, 1)
                    for j in range(6):
                        step(j // 2, j % 2, j)
                    with pe.Fori(3, NPAIR // 2 - 1) as m:
                        step(m, 0)
                        step(m, 1)
                    for j in range(NPAIR - 2, NPAIR + 3):
                        step(j // 2, j % 2, j)

            pe.wait_ge(s_x, NPAIR * 2 * n_layers)
            to_features(s_bt2, lambda j: x_io[0][:, P * j:P * j + P], 0)
            pe.wait_ge(s_x1, NCK)
            pe.wait_ge(s_ln, 2 * LN_STEPS)
            to_features(s_tp, lambda j: sq[:, P * j:P * j + P], 1)
            pe.wait_ge(s_ew, 16 * 8)
            for j in range(NPAIR):
                if j % 4 == 0:
                    pe.wait_ge(s_x0, NCK + j // 4 + 1)
                mm = pe.matmul(bank[4][:, NBATCH * E * j:NBATCH * E * (j + 1)], x_io[1][:, P * j:P * j + P],
                               gate_w[:].rearrange("p b e -> p (b e)"), start=True, stop=True)
            mm.then_inc(s_gate, 1)

            pe.wait_ge(s_mix, MIX_STEPS)
            for i in range(2):
                ptb = bank[6 + i][:].bitcast(BF16)
                for k in range(NPAIR // 2):
                    t = pe.transpose(ptb[0:NPART * QUAD, P * k:P * (k + 1)], parts[:, NPAIR // 2 * i + k, :], identb[:])
                t.then_inc(s_gt, 1)
            pe.wait_ge(s_gc, 2)
            pe.wait_ge(s_sel, NBATCH * (1 + NPART))
            def chunk(q, first=False):
                def experts_in(e):
                    again = e >= 1 or not first
                    for w, k, used in ((w1s, 0, s_sil), (w2s, 1, s_u)):
                        for b in range(NBATCH):
                            if again:
                                pe.wait_ge(used, NSTEP * q + 2 * e + b - 1)
                            rows = slice(C * b, C * b + C)
                            pe.matmul(bank[2 * b + k][:], w[rows, e, :], xq[rows, :],
                                      start=True, stop=True).then_inc((s_h1, s_h2)[k], 1)
                    for b in range(NBATCH):
                        if again:
                            pe.wait_ge(s_hid, NSTEP * q + 2 * e + b - 1)
                        pe.matmul(bank[4 + b][:], target[b][0:NPART * QUAD, e, :],
                                  cum_t[0:NPART * QUAD, bass.ds(4 * q, 4), :].rearrange("k j t -> k (j t)"),
                                  start=True, stop=True).then_inc(s_gb, 1)

                pe.wait_ge(s_xq, q + 1)
                for e in range(E):
                    experts_in(e)
                    if e >= 1:
                        expert_out(q, e - 1, first)
                    elif not first:
                        expert_out(q - 1, E - 1, False)
                    if e == 1 and not first:
                        sum_to_tokens(q - 1)

            def expert_out(q, e, first):
                pe.wait_ge(s_hid, NSTEP * q + 2 * e + 2)
                if e == 0 and not first:
                    pe.wait_ge(s_oc2, q)
                for b in range(NBATCH):
                    mm = pe.matmul(bank[6][C * b:C * (b + 1), :], w3s[:, e, :], hidden[e % 2][b],
                                   start=(e == 0), stop=(e == E - 1), skip_group_check=True)
                mm.then_inc(s_eo, 1)

            def sum_to_tokens(q):
                pe.wait_ge(s_oc2, q + 1)
                for t in range(4):
                    tr = pe.transpose(bank[7][:, P * t:P * (t + 1)], moe[:, P * t:P * (t + 1)], ident[:])
                tr.then_inc(s_ot, 1)

            chunk(0, first=True)
            with pe.Fori(1, NCK) as q:
                chunk(q)
            expert_out(NCK - 1, E - 1, False)
            sum_to_tokens(NCK - 1)

        @block.scalar
        def _(act):
            def norm_scalar(k, eps):
                act.wait_ge(s_ln, LN_STEPS * k + 3)
                act.activation(x_io[1][:], sq[:], ACT.Square).then_inc(s_ln, 1)
                act.wait_ge(s_ln, LN_STEPS * k + 5)
                act.activation(stat2[:], stat2[:], ACT.Ln, bias=eps[:], scale=1.0 / C).then_inc(s_ln, 1)
                act.wait_ge(s_ln, LN_STEPS * k + 6)
                act.activation(stat2[:], stat2[:], ACT.Exp, scale=-0.5).then_inc(s_ln, 1)

            act.preload_act_table_set("natural_log_exp_and_others")
            act.wait_ge(s_const, N_FIRST)
            norm_scalar(0, eps6)

            act.wait_ge(s_x0, NCK)
            for c in range(NCK):
                act.activation(sq[:, CK * c:CK * (c + 1)], x_io[0][:, CK * c:CK * (c + 1)],
                               ACT.Square).then_inc(s_sq, 1)
            for c in range(NCK):
                act.wait_ge(s_ms, c + 1)
                act.activation(rstd[:, CK * c:CK * (c + 1)], bank[c][:], ACT.Copy).then_inc(s_mc, 1)
            act.wait_ge(s_mc, NCK)
            for c in range(NG):
                log_of(act, 0, c)
                root_of(act, 0, c, 0)

            act.wait_ge(s_wld, 16 * N_WDMA)
            act.activation(hd_raw[:, :, :, 1, :], hd_raw[:, :, :, 1, :], ACT.Exp).then_inc(s_ea, 1)
            act.wait_ge(s_const, N_CONST)

            with act.Fori(0, n_layers) as layer:
                for s in range(2):
                    g = 2 * layer + s
                    act.wait_ge(s_dtp, g + 1)
                    act.activation(dtf[:], bank[4][:], ACT.Copy).then_inc(s_dtf, 1)
                    act.wait_ge(s_v, g + 1)
                    act.activation(dta[:], dtv[:], ACT.Abs).then_inc(s_abs, 1)
                    act.wait_ge(s_abs, g + 1)
                    act.activation(dta[:], dta[:], ACT.Exp, scale=-1.0).then_inc(s_e, 1)
                    act.wait_ge(s_e, g + 1)
                    act.activation(dta[:], dta[:], ACT.Ln, bias=1.0).then_inc(s_l, 1)
                    act.preload_act_table_set("exp_and_others")
                    def tanh(m, u, first):
                        n = NPAIR * g + 2 * m + u
                        act.wait_ge(s_proj, n + 1)
                        if not first:
                            act.wait_ge(s_xbc, n)
                        act.activation(th[:].rearrange("p b c -> p (b c)"), bank[0][:, 0:NBATCH * CONVD], ACT.Tanh,
                                       scale=0.5).then_inc(s_th, 1)

                    def tanh_z(m, u, first):
                        n = NPAIR * g + 2 * m + u
                        act.wait_ge(s_zp, n + 1)
                        if not first:
                            act.wait_ge(s_z, n)
                        act.activation(thz[:].rearrange("p b c -> p (b c)"), bank[1][:, 0:NBATCH * P], ACT.Tanh,
                                       scale=0.5).then_inc(s_thz, 1)

                    def copy_bc(m, u):
                        act.wait_ge(s_bt, NPAIR * g + 2 * m + u + 1)
                        act.activation(bt[u][:], bank[4][0:2 * QUAD, 0:P], ACT.Copy).then_inc(s_btc, 1)
                        act.activation(ct[u][:], bank[4][2 * QUAD:P, 0:P], ACT.Copy).then_inc(s_btc, 1)

                    def exps(m, u, q, first):
                        n = NPAIR * g + 2 * m + u
                        act.wait_ge(s_seg, 4 * n + q + 1)
                        if not first:
                            act.wait_ge(s_y, n - 1)
                        act.activation(em[u][:, q // 2, 4 * (q % 2):4 * (q % 2) + 4, :].rearrange("p h t -> p (h t)"),
                                       bank[2 + q % 2][:], ACT.Exp).then_inc(s_exp, 1)

                    def squares(m, u, first):
                        n = NPAIR * g + 2 * m + u
                        act.wait_ge(s_yg, n + 1)
                        if not first:
                            act.wait_ge(s_ss, n - 1)
                        act.activation(ysq[u][:], yg[u][:], ACT.Square, scale=0.5 * DIN ** -0.5).then_inc(s_ysq, 1)

                    def add_eps(m, u, first):
                        n = NPAIR * g + 2 * m + u
                        act.wait_ge(s_o, n + 1)
                        if not first:
                            act.wait_ge(s_on, n - 1)
                        act.activation(oc[u][:], bank[6][:, 0:P], ACT.Copy).then_inc(s_oc, 1)
                        act.wait_ge(s_ss, n + 1)
                        if not first:
                            act.wait_ge(s_rr, n - 1)
                        act.activation(var[u][:], bank[7][:, 0:NBATCH], ACT.Identity, bias=eps6[:]).then_inc(s_var, 1)

                    def square_x(m, u, first):
                        n, j = NPAIR * g + 2 * m + u, 2 * m + u
                        act.wait_ge(s_x, n + 1)
                        if not first:
                            act.wait_ge(s_mx, n - 1)
                        act.activation(of_tile(xsq[u][:]), x_out(s, j), ACT.Square).then_inc(s_xs, 1)

                    def copy_mean(m, u):
                        n, j = NPAIR * g + 2 * m + u, 2 * m + u
                        act.wait_ge(s_mx, n + 1)
                        act.activation(ms_out(s, j), of_tile(bank[5][:, 2 * P:3 * P]), ACT.Copy).then_inc(s_mc, 1)

                    def log_mean(c):
                        act.wait_ge(s_mc, NCK + NPAIR * g + GROUPS[c][1])
                        log_of(act, 1 - s, c)

                    def inverse_root(c):
                        root_of(act, 1 - s, c, NG * (g + 1))

                    def copy_late_sums():
                        act.wait_ge(s_pt, 2 * g + 2)
                        act.activation(cum_t[0:R_TOP, NPAIR // 2:, :].rearrange("p j t -> p (j t)"),
                                       bank[7][:].bitcast(BF16)[0:R_TOP, :], ACT.Copy).then_inc(s_ct2, 1)

                    def step(m, u, j=None):
                        nxt = (m + (u + 1) // 2, (u + 1) % 2)
                        prv = (m + (u - 1) // 2, (u - 1) % 2)
                        pr2 = (m - 1, u)
                        has_next = j is None or j + 1 < NPAIR
                        here = j is None or 0 <= j < NPAIR
                        pr3 = (m + (u - 3) // 2, (u - 1) % 2)
                        if here:
                            exps(m, u, 0, j is not None and j < 2)
                            exps(m, u, 1, j is not None and j < 2)
                        if j == 0:
                            copy_late_sums()
                        if j is None or j >= 4:
                            copy_mean(m + (u - 4) // 2, u)
                        if j is None or 2 <= j <= NPAIR + 1:
                            add_eps(*pr2, j is not None and j - 2 < 2)
                        if has_next:
                            tanh(*nxt, False)
                        if j is None or 3 <= j <= NPAIR + 2:
                            square_x(*pr3, j is not None and j - 3 < 2)
                        if here:
                            exps(m, u, 2, j is not None and j < 2)
                            exps(m, u, 3, j is not None and j < 2)
                        if j == NPAIR - 1:
                            act.preload_act_table_set("natural_log_exp_and_others")
                        if j == NPAIR:
                            log_mean(0)
                            inverse_root(0)
                            log_mean(1)
                        if has_next:
                            copy_bc(*nxt)
                        if j is None or 1 <= j <= NPAIR:
                            squares(*prv, j is not None and j - 1 < 2)
                        if has_next:
                            tanh_z(*nxt, False)

                    tanh(0, 0, True)
                    act.wait_ge(s_cum, g + 1)
                    act.activation(part(0),
                                   bank[5][:, 0:NPAIR * BH].rearrange("p (j k) -> p j k", k=BH),
                                   ACT.Copy).then_inc(s_hi, 1)
                    copy_bc(0, 0)
                    tanh_z(0, 0, True)
                    for j in range(6):
                        step(j // 2, j % 2, j)
                    with act.Fori(3, NPAIR // 2 - 1) as m:
                        step(m, 0)
                        step(m, 1)
                    for j in range(NPAIR - 2, NPAIR + 4):
                        step(j // 2, j % 2, j)
                        if j == NPAIR + 1:
                            log_mean(2)
                            inverse_root(1)
                            inverse_root(2)
                        if j >= NPAIR + 2:
                            log_mean(j - NPAIR + 1)
                            inverse_root(j - NPAIR + 1)

            norm_scalar(1, eps5)
            act.wait_ge(s_mix, 3)
            act.activation(prob, prob, ACT.Exp).then_inc(s_prob, 1)
            act.preload_act_table_set("silu_and_others")
            act.wait_ge(s_x0, 2 * NCK)
            def copy_x(q):
                act.activation(xq, x_io[1][:, bass.ds(CK * q, CK)], ACT.Copy).then_inc(s_xq, 1)

            copy_x(0)
            act.wait_ge(s_gt, 1)
            act.activation(cum_t[0:NPART * QUAD, 0:NPAIR // 2, :].rearrange("p j t -> p (j t)"),
                           bank[6][:].bitcast(BF16)[0:NPART * QUAD, :], ACT.Copy).then_inc(s_gc, 1)
            act.wait_ge(s_gc, 2)
            def copy_sum(q):
                act.wait_ge(s_eo, E * (q + 1))
                act.activation(moe, bank[6][:], ACT.Copy).then_inc(s_oc2, 1)

            def chunk(q, first=False, last=False):
                for e in range(E):
                    for b in range(NBATCH):
                        k = NSTEP * q + 2 * e + b
                        act.wait_ge(s_h1, k + 1)
                        if e >= 1 or not first:
                            act.wait_ge(s_u, k - 1)
                        act.activation(sil[b], bank[2 * b][:], ACT.Silu).then_inc(s_sil, 1)
                        if e == E - 1 and b == NBATCH - 1 and not last:
                            act.wait_ge(s_h2, k + 1)
                            copy_x(q + 1)
                    if e == 0 and not first:
                        copy_sum(q - 1)

            chunk(0, first=True)
            with act.Fori(1, NCK - 1) as q:
                chunk(q)
            chunk(NCK - 1, last=True)
            copy_sum(NCK - 1)

        @block.vector
        def _(dve):
            tm = sq[:].rearrange("p (t c) -> p t c", c=C)
            xi = x_in[:].rearrange("p j b c -> p (j b) c")
            sq2 = x_io[1][:].rearrange("p (t c) -> p t c", c=C)

            def spread(ap, n):
                return ap.rearrange("p (t o) -> p t o", o=1).to_broadcast([P, NPAIR * NBATCH, n])

            def norm_vector(k):
                dve.tensor_reduce(stat[:], xi, AX.X, ALU.add).then_inc(s_ln, 1)
                dve.wait_ge(s_ln, LN_STEPS * k + 1)
                dve.tensor_scalar(stat[:], stat[:], 1.0 / C, None, ALU.mult).then_inc(s_ln, 1)
                dve.wait_ge(s_ln, LN_STEPS * k + 2)
                dve.tensor_tensor(tm, xi, spread(stat[:], C), ALU.subtract).then_inc(s_ln, 1)
                dve.wait_ge(s_ln, LN_STEPS * k + 4)
                dve.tensor_reduce(stat2[:], sq2, AX.X, ALU.add).then_inc(s_ln, 1)
                dve.wait_ge(s_ln, LN_STEPS * k + 7)
                dve.tensor_tensor(tm, tm, spread(stat2[:], C), ALU.mult).then_inc(s_ln, 1)

            def from_banks(k, dst):
                for c in range(NCK):
                    dve.wait_ge(s_tp, NCK * k + c + 1)
                    dve.tensor_copy(dst[:, CK * c:CK * (c + 1)], bank[c][:]).then_inc(s_x0, 1)

            dve.wait_ge(s_ld, 16 * NBATCH)
            norm_vector(0)
            from_banks(0, x_io[0])

            dve.wait_ge(s_wld, 16 * N_WDMA)

            made = [0]

            def link(ins):
                made[0] += 1
                ins.then_inc(s_wd, 1)
                dve.wait_ge(s_wd, made[0])

            link(dve.tensor_copy(cb_part[:, 0, :], cb_raw[:]))
            link(dve.tensor_tensor(cb_rest[:], cb_raw[:], cb_part[:, 0, :], ALU.subtract))
            link(dve.tensor_copy(cb_part[:, 1, :], cb_rest[:]))
            link(dve.tensor_tensor(cb_part[:, 2, :], cb_rest[:], cb_part[:, 1, :], ALU.subtract))
            for s in range(2):
                wn = win_raw[:, s]
                link(dve.tensor_tensor(wn, wn, small[:, s, :, 0:1].to_broadcast([P, NL, PROJ]), ALU.mult))
                link(dve.tensor_tensor(wall[:, 0:NL, s, W_C0:W_C0 + CONVD], wn[:, :, DIN:DIN + CONVD], cw_raw[:, s],
                                       ALU.mult))
                link(dve.tensor_tensor(wall[:, 0:NL, s, W_C1:W_C1 + CONVD], wn[:, :, DIN:DIN + CONVD], cw_raw2[:, s],
                                       ALU.mult))
                link(dve.memset(wall[:, 0:NL, s, W_Z:W_OUT], 0.0))
                link(dve.tensor_copy(wall[C:P, 0:NL, s, W_C1 + CONVD:W_DT], wn[C:P, :, 0:DIN]))
                for b in range(2):
                    link(dve.tensor_copy(wall[C * b:C * (b + 1), 0:NL, s, W_DT + HEADS * b:W_DT + HEADS * (b + 1)],
                                         wn[C * b:C * (b + 1), :, DIN + CONVD:PROJ]))
                link(dve.scalar_tensor_tensor(out=wall[:, 0:NL, s, W_OUT:W_OUT + C], in0=wout_raw[:, s], scalar=0.5,
                                              in1=small[:, s, :, 1:2].to_broadcast([P, NL, C]),
                                              op0=ALU.mult, op1=ALU.mult))
                for i in range(NL):
                    link(dve.tensor_scalar(
                        wall[:, i, s, W_D:W_D + DIN].rearrange("p (h d) -> p h d", h=HEADS),
                        hd_raw[:, s, i, 0, :].rearrange("p (h o) -> p h o", o=1).to_broadcast([P, HEADS, HD]),
                        0.5, None, ALU.mult))
                dve.wait_ge(s_ea, 1)
                link(dve.tensor_scalar(wall[:, 0:NL, s, W_NA:W_NA + HEADS], hd_raw[:, s, :, 1, :], -1.0, None,
                                       ALU.mult))
            assert made[0] == WD_ALL

            dve.wait_ge(s_const, N_CONST)
            for k, (dst, src) in enumerate(((target[0], far_rows), (cum_t, one_rows))):
                dve.tensor_copy(dst[R_BLK:P], src[R_BLK:P].rearrange("p (o t) -> p o t", o=1).to_broadcast(
                    [NBLK, BH, P])).then_inc(s_tm, 1)
            dve.wait_ge(s_tm, 2)
            dve.tensor_copy(target[1][:], target[0][:]).then_inc(s_tm, 1)

            for c in range(NG):
                x_by_r(dve, 0, c, 0)
            dve.wait_ge(s_tm, 3)
            dve.tensor_copy(head_neg, target[0][:]).then_inc(s_tm, 1)
            dve.tensor_scalar(head_row[0:R_TOP], target[0][0:R_TOP], -1.0, None, ALU.mult).then_inc(s_tm, 1)

            with dve.Fori(0, n_layers) as layer:
                for s in range(2):
                    g = 2 * layer + s
                    w = wcur[s]
                    dve.wait_ge(s_dtt, g + 1)

                    def per_head(col):
                        return w[:, col:col + HEADS].rearrange("p (o q h) -> p o q h", o=1, q=1).to_broadcast(
                            [P, NPAIR, NBATCH, HEADS])

                    def heads(t):
                        return t[:].rearrange("p (t b h) -> p t b h", b=NBATCH, h=HEADS)

                    def block_of(ap, t):
                        return ap[:, NCK * BH * t:NCK * BH * (t + 1)].rearrange("p (c k) -> p c k", k=BH)

                    dve.wait_ge(s_wcur, 32 * (g + 1))
                    cols = bank[4][:].rearrange("p (t k) -> p t k", k=QUAD)[:, :, 0:BH].rearrange(
                        "p t (b h) -> p t b h", h=HEADS)
                    dve.tensor_tensor(heads(dtv), cols, per_head(W_DTB), ALU.add).then_inc(s_v, 1)
                    dve.wait_ge(s_l, g + 1)
                    for t in range(NPAIR // NCK):
                        ins = dve.scalar_tensor_tensor(
                            out=dtl[:].rearrange("p (c t k) -> p c t k", c=NCK, k=BH)[:, :, t, :],
                            in0=block_of(dtv, t), scalar=0.0, in1=block_of(dta, t), op0=ALU.max, op1=ALU.add)
                    ins.then_inc(s_dt, 1)
                    dve.wait_ge(s_dt, 2 * g + 1)
                    dve.tensor_tensor(heads(dta_log), heads(dtl), per_head(W_NA), ALU.mult).then_inc(s_dta, 1)
                    dve.tensor_scalar(dt_half[:], dtl[:], 0.5, None, ALU.mult).then_inc(s_dt, 1)
                    def gates(m, u, first):
                        n, j = NPAIR * g + 2 * m + u, 2 * m + u
                        if not first:
                            dve.wait_ge(s_xd, n - 1)
                        dve.wait_ge(s_th, n + 1)
                        dve.scalar_tensor_tensor(
                            out=xbc[u][:].rearrange("p b c -> p (b c)"), in0=th[:].rearrange("p b c -> p (b c)"),
                            scalar=1.0, in1=bank[0][:, 0:NBATCH * CONVD], op0=ALU.add, op1=ALU.mult
                            ).then_inc(s_xbc, 1)

                    def gate_z(m, u):
                        n, j = NPAIR * g + 2 * m + u, 2 * m + u
                        dve.wait_ge(s_thz, n + 1)
                        dve.scalar_tensor_tensor(
                            out=z_all[:, bass.ds(j, 1), :, :].rearrange("p o b t -> p (o b t)"),
                            in0=thz[:].rearrange("p b t -> p (b t)"), scalar=1.0, in1=bank[1][:, 0:NBATCH * P],
                            op0=ALU.add, op1=ALU.mult).then_inc(s_z, 1)

                    def mask(m, u):
                        dve.wait_ge(s_g, NPAIR * g + 2 * m + u + 1)
                        for b in range(2):
                            ins = dve.scalar_tensor_tensor(out=gm[u][:, b, :], in0=bank[(4, 0)[b]][:, G_COL:G_COL + P],
                                                           scalar=0.25, in1=tri[s][:], op0=ALU.mult, op1=ALU.mult)
                        ins.then_inc(s_gm, 1)

                    def weigh(m, u, q):
                        n, b, hh = NPAIR * g + 2 * m + u, q // 2, q % 2
                        dve.wait_ge(s_exp, 4 * n + q + 1)
                        if q == 0:
                            dve.wait_ge(s_gm, n + 1)
                        e = em[u][:, b, 4 * hh:4 * hh + 4, :]
                        dve.scalar_tensor_tensor(out=e, in0=e, scalar=1.0,
                                                 in1=gm[u][:, b:b + 1, :].to_broadcast([P, 4, P]),
                                                 op0=ALU.min, op1=ALU.mult).then_inc(s_m, 1)

                    def gate_y(m, u, first):
                        n, j = NPAIR * g + 2 * m + u, 2 * m + u
                        dve.wait_ge(s_y, n + 1)
                        dve.wait_ge(s_z, n + 1)
                        if not first:
                            dve.wait_ge(s_ss, n - 1)
                        dve.tensor_tensor(yg[u][:], bank[5][:, 0:2 * P].rearrange("p (b t) -> p b t", b=2),
                                          z_all[:, bass.ds(j, 1), :, :].rearrange("p o b t -> p (o b) t"),
                                          ALU.mult).then_inc(s_yg, 1)

                    def norm_out(m, u, first):
                        n = NPAIR * g + 2 * m + u
                        dve.wait_ge(s_oc, n + 1)
                        dve.wait_ge(s_rb, n + 1)
                        if not first:
                            dve.wait_ge(s_x, n - 1)
                        dve.tensor_tensor(on[u][:], bank[7][:, P:2 * P], oc[u][:], ALU.mult).then_inc(s_on, 1)

                    def step(m, u, j=None):
                        nxt = (m + (u + 1) // 2, (u + 1) % 2)
                        prv = (m + (u - 1) // 2, (u - 1) % 2)
                        has_next = j is None or j + 1 < NPAIR
                        here = j is None or 0 <= j < NPAIR
                        if here:
                            weigh(m, u, 0)
                            weigh(m, u, 1)
                        if has_next:
                            gates(*nxt, j is not None and j + 1 < 2)
                        if here:
                            weigh(m, u, 2)
                            weigh(m, u, 3)
                        if j is None or 1 <= j <= NPAIR:
                            gate_y(*prv, j is not None and j - 1 < 2)
                        if j is None or j >= 2:
                            norm_out(m - 1, u, j is not None and j - 2 < 2)
                        if has_next:
                            mask(*nxt)
                            gate_z(*nxt)

                    gates(0, 0, True)
                    dve.wait_ge(s_hi, g + 1)
                    cum = bank[5][:, 0:NPAIR * BH].rearrange("p (j k) -> p j k", k=BH)
                    r3 = rest[:].rearrange("p (j k) -> p j k", k=BH)
                    dve.tensor_tensor(r3, cum, part(0), ALU.subtract).then_inc(s_rest, 1)
                    dve.wait_ge(s_rest, g + 1)
                    dve.tensor_copy(part(1), r3).then_inc(s_mid, 1)
                    dve.wait_ge(s_mid, g + 1)
                    dve.tensor_tensor(part(2), r3, part(1), ALU.subtract).then_inc(s_lo, 1)
                    mask(0, 0)
                    dve.wait_ge(s_pt, 2 * g + 1)
                    early = bank[6][:].bitcast(BF16)[0:R_TOP, :]
                    dve.tensor_copy(cum_t[0:R_TOP, 0, :], early[:, 0:P]).then_inc(s_ct0, 1)
                    dve.tensor_copy(cum_t[0:R_TOP, 1:NPAIR // 2, :].rearrange("p j t -> p (j t)"),
                                    early[:, P:]).then_inc(s_ct, 1)
                    gate_z(0, 0)
                    for j in range(4):
                        step(j // 2, j % 2, j)
                    with dve.Fori(2, NPAIR // 2 - 1) as m:
                        step(m, 0)
                        step(m, 1)
                    for j in range(NPAIR - 2, NPAIR + 1):
                        step(j // 2, j % 2, j)
                    for c in range(NG):
                        if c == 1:
                            norm_out(NPAIR // 2 - 1, 1, False)
                        x_by_r(dve, 1 - s, c, NG * (g + 1))

            for c in range(NCK):
                dve.wait_ge(s_bt2, c + 1)
                v = x_in[:].rearrange("p j b c -> p (j b c)")[:, CK * c:CK * (c + 1)]
                dve.tensor_tensor(v, bank[c][:], v, ALU.add).then_inc(s_x1, 1)
            dve.wait_ge(s_x1, NCK)
            norm_vector(1)
            from_banks(1, x_io[1])

            made2 = [0]

            def mixed(ins):
                made2[0] += 1
                ins.then_inc(s_mix, 1)
                dve.wait_ge(s_mix, made2[0])

            def over_e(t):
                return t[:].rearrange("p (t o) -> p t o", o=1).to_broadcast([P, NT2, E])

            dve.wait_ge(s_gate, 1)
            mixed(dve.tensor_tensor(prob, bank[4][:].rearrange("p (t e) -> p t e", e=E),
                                    gate_b[:].rearrange("p (o e) -> p o e", o=1).to_broadcast([P, NT2, E]), ALU.add))
            mixed(dve.tensor_reduce(top[0][:], prob, AX.X, ALU.max))
            mixed(dve.tensor_tensor(prob, prob, over_e(top[0]), ALU.subtract))
            dve.wait_ge(s_prob, 1)
            mixed(dve.tensor_reduce(top[0][:], prob, AX.X, ALU.add))
            mixed(dve.reciprocal(top[1][:], top[0][:]))
            mixed(dve.tensor_tensor(prob, prob, over_e(top[1]), ALU.mult))
            rk = rank[:].rearrange("p (o e) -> p o e", o=1).to_broadcast([P, NT2, E])
            for i, (hot, src) in enumerate(((hot1, prob), (hot2, work))):
                if i == 1:
                    mixed(dve.scalar_tensor_tensor(out=work, in0=hot1, scalar=-2.0, in1=prob, op0=ALU.mult,
                                                   op1=ALU.add))
                mixed(dve.tensor_reduce(top[i][:], src, AX.X, ALU.max))
                mixed(dve.tensor_tensor(hot, src, over_e(top[i]), ALU.is_equal))
                mixed(dve.tensor_tensor(hot, hot, rk, ALU.mult))
                mixed(dve.tensor_reduce(top[2][:], hot, AX.X, ALU.max))
                mixed(dve.tensor_tensor(hot, hot, over_e(top[2]), ALU.is_equal))
            mixed(dve.tensor_tensor(top[2][:], top[0][:], top[1][:], ALU.add))
            mixed(dve.reciprocal(top[3][:], top[2][:]))
            for i, hot in enumerate((hot1, hot2)):
                mixed(dve.tensor_tensor(top[i][:], top[i][:], top[3][:], ALU.mult))
                mixed(dve.tensor_tensor(hot, hot, over_e(top[i]), ALU.mult))
            mixed(dve.tensor_tensor(mix[:].rearrange("p j b e -> p (j b) e"), hot1, hot2, ALU.add))
            mixv = mix[:].rearrange("p j b e -> p j (b e)")
            left = work.rearrange("p (j b) e -> p j (b e)", b=NBATCH)

            def mix_part(i):
                return parts[:, :, QUAD * i:QUAD * (i + 1)]

            mixed(dve.tensor_copy(mix_part(0), mixv))
            mixed(dve.tensor_tensor(left, mixv, mix_part(0), ALU.subtract))
            mixed(dve.tensor_copy(mix_part(1), left))
            mixed(dve.tensor_tensor(mix_part(2), left, mix_part(1), ALU.subtract))
            assert made2[0] == MIX_STEPS
            dve.wait_ge(s_gt, 2)
            dve.tensor_copy(cum_t[0:NPART * QUAD, NPAIR // 2:, :].rearrange("p j t -> p (j t)"),
                            bank[7][:].bitcast(BF16)[0:NPART * QUAD, :]).then_inc(s_gc, 1)

            def add_sum(q):
                dve.wait_ge(s_ot, q + 1)
                v = x_in[:, bass.ds(4 * q, 4), :, :].rearrange("p j b c -> p (j b c)")
                dve.tensor_tensor(v, bank[7][:], v, ALU.add).then_inc(s_acc, 1)

            def chunk(q, first=False):
                for e in range(E):
                    for b in range(NBATCH):
                        k = NSTEP * q + 2 * e + b
                        dve.wait_ge(s_sil, k + 1)
                        dve.wait_ge(s_h2, k + 1)
                        dve.tensor_tensor(act_h[b], sil[b], bank[2 * b + 1][:], ALU.mult).then_inc(s_u, 1)
                        dve.wait_ge(s_gb, k + 1)
                        dve.wait_ge(s_u, k + 1)
                        if e >= 2 or not first:
                            dve.wait_ge(s_eo, E * q + e - 1)
                        dve.tensor_tensor(hidden[e % 2][b], act_h[b], bank[4 + b][:], ALU.mult).then_inc(s_hid, 1)
                    if e == 2 and not first:
                        add_sum(q - 1)

            chunk(0, first=True)
            with dve.Fori(1, NCK) as q:
                chunk(q)
            add_sum(NCK - 1)


_INS = ["x"] + [f"L0_conv_{k}_{n}" for k in ("t", "b")
                for n in ("norm", "Win", "cw", "cb", "dtb", "Alog", "D", "gn", "Wout")] + [
    f"L0_ffn_{n}" for n in ("gate_w", "gate_b", "w1", "w2", "w3")]


def kernel(**inputs):
    import numpy as _np
    import concourse.bacc as _bacc
    from concourse import mybir as _mybir
    from concourse.bass_utils import run_bass_kernel_spmd as _run

    nc = _bacc.Bacc("TRN2", target_bir_lowering=False, num_devices=1)
    arrays, args = {}, {}
    for name in _INS:
        v = _np.ascontiguousarray(inputs[name])
        arrays[f"in_{name}"] = v
        args[name.replace("L0_conv_", "").replace("L0_ffn_", "")] = nc.dram_tensor(
            f"in_{name}", v.shape, _mybir.dt.from_np(v.dtype), kind="ExternalInput").ap()
    out = nc.dram_tensor("out", inputs["x"].shape, _mybir.dt.from_np(_np.dtype("float32")),
                         kind="ExternalOutput").ap()
    build(nc, args, out)
    return _run(nc, [arrays], core_ids=[0]).results[0]["out"]
```
